# Optimizing a Trainium2 kernel written in Bass

```python
import numpy as np
import jax
import jax.numpy as jnp

def _softmax(x, axis=-1):
    return jax.nn.softmax(x, axis=axis)

def _gelu(x):
    return jax.nn.gelu(x, approximate=True)

def _silu(x):
    return jax.nn.silu(x)

def _sigmoid(x):
    return jax.nn.sigmoid(x)

def _layernorm(x, axis=-1, eps=1e-05):
    m = jnp.mean(x, axis=axis, keepdims=True)
    v = jnp.var(x, axis=axis, keepdims=True)
    return (x - m) / jnp.sqrt(v + eps)

def _scatter_add(tgt, idx, src, axis=0):
    return tgt.at[idx].add(src)

def _segment_sum(src, seg, n):
    return jax.ops.segment_sum(src, seg, n)
kernel_name = 'mk_gnn_preln_d2_gnn_r8_9c01ce'

def setup_inputs(seed: int=0):
    np.random.seed(seed)
    _w = jnp.asarray

    def _rec_inputs():
        import jax
        import jax.numpy as jnp
        _gk = jax.random.key(seed)
        x = -0.000202 + 1 * jax.random.normal(jax.random.fold_in(_gk, 1), (12500, 128), jnp.float32)
        _s = jax.random.randint(jax.random.fold_in(_gk, 2), (100000,), 0, 12500, jnp.int32)
        _d = jax.random.randint(jax.random.fold_in(_gk, 3), (100000,), 0, 12500, jnp.int32)
        _loop = jnp.arange(12500, dtype=jnp.int32)
        src = jnp.concatenate([_s, _d, _loop])
        dst = jnp.concatenate([_d, _s, _loop])
        _o = jnp.argsort(dst, stable=True)
        src = src[_o]
        dst = dst[_o]
        edge_attr_128 = -4.21973e-05 + 0.999841 * jax.random.normal(jax.random.fold_in(_gk, 11), (212500, 128), jnp.float32)
        edge_type_8 = jax.random.randint(jax.random.fold_in(_gk, 13), (212500,), 0, 8, jnp.int32)
        return (x, src, dst, edge_attr_128, edge_type_8)
    x, src, dst, edge_attr_128, edge_type_8 = _rec_inputs()

    def _L0_gnn_setup():
        import jax, jax.numpy as jnp
        import numpy as np
        N_NODES = 6250
        N_EDGES = 75000
        F = 128
        LOG2 = np.float32(np.log(2.0))

        def shifted_softplus(x):
            return jax.nn.softplus(x) - LOG2
        key = jax.random.key(seed)
        k1, k2, k3, k4, k5 = jax.random.split(key, 5)
        nodes = jax.random.normal(k1, (N_NODES, F), dtype=jnp.float32)
        edges = jax.random.normal(k2, (N_EDGES, F), dtype=jnp.float32)
        edge_index = jax.random.randint(k3, (2, N_EDGES), 0, N_NODES, dtype=jnp.int32)
        W1 = jax.random.normal(k4, (F, F), dtype=jnp.float32) * np.float32(1.0 / np.sqrt(F))
        W2 = jax.random.normal(k5, (F, F), dtype=jnp.float32) * np.float32(1.0 / np.sqrt(F))
        b1 = jnp.zeros((F,), dtype=jnp.float32)
        b2 = jnp.zeros((F,), dtype=jnp.float32)
        return {'nodes': nodes, 'edges': edges, 'edge_index': edge_index, 'W1': W1, 'b1': b1, 'W2': W2, 'b2': b2}
    _L0_gnn_all = _L0_gnn_setup()
    _L0_gnn_in = {k: v for k, v in _L0_gnn_all.items() if k in ('W1', 'b1', 'W2', 'b2')}
    del _L0_gnn_all

    def _L1_gnn_setup():
        import jax, jax.numpy as jnp
        import numpy as np
        N, E, D_IN, D_HID, D_OUT, R, B = (6250, 75000, 128, 128, 128, 8, 4)

        def _rgcn_conv(x, src, dst, etype, basis, comp, root, bias):
            n = x.shape[0]
            r = comp.shape[0]
            W = jnp.einsum('rb,bio->rio', comp, basis)
            seg = dst * r + etype
            agg = jax.ops.segment_sum(x[src], seg, num_segments=n * r)
            cnt = jax.ops.segment_sum(jnp.ones_like(seg, x.dtype), seg, num_segments=n * r)
            mean = (agg / jnp.maximum(cnt, 1.0)[:, None]).reshape(n, r, -1)
            return jnp.einsum('nri,rio->no', mean, W) + x @ root + bias
        key = jax.random.key(seed)
        ks = jax.random.split(key, 12)
        s = 0.05
        return {'x': jax.random.normal(ks[0], (N, D_IN), jnp.float32), 'edge_index': jax.random.randint(ks[1], (2, E), 0, N, jnp.int32), 'edge_type': jax.random.randint(ks[2], (E,), 0, R, jnp.int32), 'basis1': jax.random.normal(ks[3], (B, D_IN, D_HID), jnp.float32) * s, 'comp1': jax.random.normal(ks[4], (R, B), jnp.float32) * s, 'root1': jax.random.normal(ks[5], (D_IN, D_HID), jnp.float32) * s, 'bias1': jnp.zeros((D_HID,), jnp.float32), 'basis2': jax.random.normal(ks[6], (B, D_HID, D_OUT), jnp.float32) * s, 'comp2': jax.random.normal(ks[7], (R, B), jnp.float32) * s, 'root2': jax.random.normal(ks[8], (D_HID, D_OUT), jnp.float32) * s, 'bias2': jnp.zeros((D_OUT,), jnp.float32)}
    _L1_gnn_all = _L1_gnn_setup()
    _L1_gnn_in = {k: v for k, v in _L1_gnn_all.items() if k in ('basis1', 'comp1', 'root1', 'bias1', 'basis2', 'comp2', 'root2', 'bias2')}
    del _L1_gnn_all
    return {'x': x, 'src': src, 'dst': dst, 'edge_attr_128': edge_attr_128, 'edge_type_8': edge_type_8, 'L0_gnn_W1': _L0_gnn_in['W1'], 'L0_gnn_b1': _L0_gnn_in['b1'], 'L0_gnn_W2': _L0_gnn_in['W2'], 'L0_gnn_b2': _L0_gnn_in['b2'], 'L1_gnn_basis1': _L1_gnn_in['basis1'], 'L1_gnn_comp1': _L1_gnn_in['comp1'], 'L1_gnn_root1': _L1_gnn_in['root1'], 'L1_gnn_bias1': _L1_gnn_in['bias1'], 'L1_gnn_basis2': _L1_gnn_in['basis2'], 'L1_gnn_comp2': _L1_gnn_in['comp2'], 'L1_gnn_root2': _L1_gnn_in['root2'], 'L1_gnn_bias2': _L1_gnn_in['bias2']}

def reference(x, src, dst, edge_attr_128, edge_type_8, L0_gnn_W1, L0_gnn_b1, L0_gnn_W2, L0_gnn_b2, L1_gnn_basis1, L1_gnn_comp1, L1_gnn_root1, L1_gnn_bias1, L1_gnn_basis2, L1_gnn_comp2, L1_gnn_root2, L1_gnn_bias2):
    import jax
    import jax.numpy as jnp

    def _L0_gnn_ref(nodes, edges, edge_index, W1, b1, W2, b2):
        import jax, jax.numpy as jnp
        import numpy as np
        N_NODES = 6250
        N_EDGES = 75000
        F = 128
        LOG2 = np.float32(np.log(2.0))

        def shifted_softplus(x):
            return jax.nn.softplus(x) - LOG2
        x = shifted_softplus(edges @ W1 + b1)
        x = x @ W2 + b2
        receiver = edge_index[0]
        sender = edge_index[1]
        msg = nodes[sender] * x
        out = jax.ops.segment_sum(msg, receiver, num_segments=nodes.shape[0])
        return out

    def _L1_gnn_ref(x, edge_index, edge_type, basis1, comp1, root1, bias1, basis2, comp2, root2, bias2):
        import jax, jax.numpy as jnp
        import numpy as np
        N, E, D_IN, D_HID, D_OUT, R, B = (6250, 75000, 128, 128, 128, 8, 4)

        def _rgcn_conv(x, src, dst, etype, basis, comp, root, bias):
            n = x.shape[0]
            r = comp.shape[0]
            W = jnp.einsum('rb,bio->rio', comp, basis)
            seg = dst * r + etype
            agg = jax.ops.segment_sum(x[src], seg, num_segments=n * r)
            cnt = jax.ops.segment_sum(jnp.ones_like(seg, x.dtype), seg, num_segments=n * r)
            mean = (agg / jnp.maximum(cnt, 1.0)[:, None]).reshape(n, r, -1)
            return jnp.einsum('nri,rio->no', mean, W) + x @ root + bias
        src, dst = (edge_index[0], edge_index[1])
        h = _rgcn_conv(x, src, dst, edge_type, basis1, comp1, root1, bias1)
        h = jax.nn.relu(h)
        out = _rgcn_conv(h, src, dst, edge_type, basis2, comp2, root2, bias2)
        return out
    edge_index = jnp.stack([src, dst])
    h = jnp.maximum(_layernorm(x, axis=-1), 0.0)
    x = x + _L0_gnn_ref(h, edge_attr_128, edge_index, L0_gnn_W1, L0_gnn_b1, L0_gnn_W2, L0_gnn_b2)
    h = jnp.maximum(_layernorm(x, axis=-1), 0.0)
    x = x + _L1_gnn_ref(h, edge_index, edge_type_8, L1_gnn_basis1, L1_gnn_comp1, L1_gnn_root1, L1_gnn_bias1, L1_gnn_basis2, L1_gnn_comp2, L1_gnn_root2, L1_gnn_bias2)
    return x

_drawn_inputs = setup_inputs


def setup_inputs(seed=0):
    import zlib

    import numpy as np

    out = dict(_drawn_inputs(seed))
    spreads = {'L0_gnn_b1': (0.0, 0.1),
     'L0_gnn_b2': (0.0, 0.1),
     'L1_gnn_bias1': (0.0, 0.486),
     'L1_gnn_bias2': (0.0, 0.1)}
    factors = {'L1_gnn_basis1': 3.621,
     'L1_gnn_comp1': 3.427,
     'L1_gnn_basis2': 3.104,
     'L1_gnn_comp2': 3.221}
    for name, (base, spread) in spreads.items():
        noise = np.random.default_rng([zlib.crc32(name.encode()), seed]).standard_normal(out[name].shape)
        drawn = base * np.exp(spread * noise) if base else spread * noise
        out[name] = jnp.asarray(drawn.astype(out[name].dtype))
    for name, factor in factors.items():
        out[name] = (out[name] * factor).astype(out[name].dtype)
    return out
```

```python
from contextlib import ExitStack

import numpy as np

import concourse.bass as bass
from concourse import mybir


ALU = mybir.AluOpType
ACT = mybir.ActivationFunctionType
F32 = mybir.dt.float32
BF16 = mybir.dt.bfloat16
I32 = mybir.dt.int32
AX_X = mybir.AxisListType.X

P = 128
F = 128
TG = 4
GE = TG * P
R = 8
NBASIS = 4
UNROLL = 4
LOG2 = float(np.float32(np.log(2.0)))
EPS = 1e-5
EXP_CLAMP = 1e19
PAD_DST = 16383


class Step:

    def __init__(self, i, c):
        self.i, self.c = i, c

    def at(self, lag):
        return self.i * UNROLL + (self.c - lag)

    def use(self, slots, lag):
        return self.i * (UNROLL // slots) + (self.c - lag) // slots

    def slot(self, slots, lag):
        return (self.c - lag) % slots

    def live(self, lag, n):
        return not isinstance(self.i, int) or 0 <= self.c - lag < n


def run_steps(eng, n, tail, body):
    for c in range(UNROLL):
        body(Step(0, c))
    with eng.Fori(0, n // UNROLL - 1) as i:
        for k in range(UNROLL):
            body(Step(i, UNROLL + k))
    for c in range(n, n + tail):
        body(Step(0, c))


def need(eng, sem, value):
    if not isinstance(value, int) or value > 0:
        eng.wait_ge(sem, value)



def apart(eng, s_gate):
    eng.sem_inc(s_gate, 1)


class Chain:

    def __init__(self, eng, sem):
        self.eng, self.sem, self.n = eng, sem, 0

    def __call__(self, instruction):
        instruction.then_inc(self.sem, 1)
        self.n += 1
        self.eng.wait_ge(self.sem, self.n)


class Graph:

    def __init__(self, nc, ctx, N, E):
        self.nc = nc
        self.N, self.E = N, E
        self.NBLK = -(-N // P)
        self.NBX = self.NBLK + 1
        self.NG = -(-(-(-E // GE)) // UNROLL) * UNROLL
        self.NT = self.NG * TG
        self.QP = self.NG // 4
        self.EQ = 4 * GE
        self.ELAST = E - (self.NG - 1) * GE
        self.NROWS = self.NBLK * P
        self.TRASH = self.NROWS
        self.NACC = self.NROWS + 2 * P
        assert 0 < self.ELAST <= GE and self.ELAST % TG == 0 and self.QP <= P
        assert self.NG >= max(2 * UNROLL, self.NBLK) and self.NBLK % 2 == 0 and self.NBX % 3 == 0
        assert self.NROWS + P < PAD_DST

        self.acc_dram = [nc.dram_tensor(f"acc_dram{j}", [self.NACC, F], F32).ap() for j in range(TG)]
        self.split_dram = nc.dram_tensor("split_dram", [self.NBX * P, 3 * F], BF16).ap()
        self.rows_dram = nc.dram_tensor("rows_dram", [self.NG, 2, 2, GE], BF16).ap()
        self.span_dram = nc.dram_tensor("span_dram", [2, self.NG], F32).ap()
        self.nid_dram = nc.dram_tensor("nid_dram", [self.NG, P], F32).ap()
        self.table_dram = nc.dram_tensor("table_dram", [self.NROWS * R, F], F32).ap()

        self.bank = [ctx.enter_context(nc.psum_tensor(f"bank{k}", [P, 512], F32)) for k in range(8)]

        def sb(name, shape, dt=F32):
            return ctx.enter_context(nc.sbuf_tensor(name, shape, dt))

        self.gate = {name: nc.alloc_semaphore(f"gate_{name}") for name in ("pe", "dve", "pool")}
        NBX, NT, NG = self.NBX, self.NT, self.NG
        self.xs = sb("xs", [P, NBX, F])
        self.rstd = sb("rstd", [P, NBX])
        self.shift = sb("shift", [P, NBX])
        self.cnt = sb("cnt", [P, NBX, R])
        self.rcnt3 = sb("rcnt3", [P, NBX, 3 * R], BF16)
        self.dstcol = sb("dstcol", [P, NT])
        self.srccol = sb("srccol", [P, NT])
        self.etcol = sb("etcol", [P, NT])
        self.mask_hi = sb("mask_hi", [P, NG + 1])
        self.mask_lo = sb("mask_lo", [P, NG + 1])
        self.blk = sb("blk", [P, NG + 1], I32)
        self.base = sb("base", [P, NG], I32)
        self.nid_lin = sb("nid_lin", [P, NG])
        self.nid_res = sb("nid_res", [P, NG])
        self.ctl = sb("ctl", [P, 4], I32)
        self.ident = sb("ident", [P, P])
        self.part = sb("part", [P, 1])
        self.iota_r = sb("iota_r", [P, R])
        self.eps = sb("eps", [P, 1])
        self.coef = sb("coef", [2, P], BF16)
        self.zero16 = sb("zero16", [1, 512], BF16)
        self.ones3 = sb("ones3", [P, P], BF16)
        self.bias3 = sb("bias3", [P, 512], BF16)
        self.pow2 = sb("pow2", [P, 1], BF16)
        self.dup_above = sb("dup_above", [P, 1])
        self.trash_row = sb("trash_row", [P, 1])
        self.w1 = sb("w1", [F, F])
        self.w2 = sb("w2", [F, F])
        self.b1c = sb("b1c", [F, 1])
        self.wrel = [sb(f"wrel{k}", [F, R * F]) for k in range(2)]
        self.wroot = [sb(f"wroot{k}", [F, F]) for k in range(2)]
        self.biasb = [sb(f"biasb{k}", [P, F]) for k in range(2)]

    def controls(self, eng):
        return (eng.value_load(self.ctl[0:1, 0:1], min_val=1, max_val=self.NBLK),
                eng.value_load(self.ctl[0:1, 1:2], min_val=0, max_val=1),
                eng.value_load(self.ctl[0:1, 2:3], min_val=0, max_val=self.NBLK))

    def entry(self, eng, value, top=None):
        return value.with_bounds(min_val=0, max_val=self.NG - 1 if top is None else top)


def norm_stats(nc, chain, g, bn, tmp):
    mean_e, sq_e, mean_o, sq_o = (bn[:, :, k] for k in (1, 2, 4, 5))
    chain(nc.vector.tensor_tensor(tmp[:, :], mean_e, mean_o, ALU.subtract))
    chain(nc.vector.tensor_tensor(tmp[:, :], tmp[:, :], tmp[:, :], ALU.mult))
    chain(nc.vector.tensor_scalar(tmp[:, :], tmp[:, :], 0.25, None, ALU.mult))
    chain(nc.vector.tensor_tensor(g.rstd[:, :], sq_e, sq_o, ALU.add))
    chain(nc.vector.scalar_tensor_tensor(g.rstd[:, :], g.rstd[:, :], 1.0 / F, tmp[:, :], ALU.mult, ALU.add))
    chain(nc.vector.tensor_tensor(g.shift[:, :], mean_e, mean_o, ALU.add))


def norm_scale(nc, chain, g):
    chain(nc.vector.reciprocal(g.rstd[:, :], g.rstd[:, :]))
    chain(nc.vector.scalar_tensor_tensor(g.shift[:, :], g.shift[:, :], -0.5, g.rstd[:, :], ALU.mult, ALU.mult))


def prepare(nc, g, x, src, dst, edge_type, W1, b1, W2, b2, basis, comp, root, bias):
    N, E, NG, NBLK, NBX, QP, EQ = g.N, g.E, g.NG, g.NBLK, g.NBX, g.QP, g.EQ
    CB = 3
    NCH = NBX // CB
    ZR = max(d for d in range(1, 11) if (NBLK + 2) % d == 0)
    with ExitStack() as ctx:
        def sb(name, shape, dt=F32):
            return ctx.enter_context(nc.sbuf_tensor(name, shape, dt))

        def sem(name):
            return nc.alloc_semaphore(name)

        ids = [sb(f"ids{k}", [QP, EQ], I32) for k in range(2)]
        idt = sb("idt", [QP, EQ], I32)
        idf = sb("idf", [QP, EQ])
        parts = [sb(f"parts{k}", [QP, 2, EQ], BF16) for k in range(2)]
        span = sb("span", [QP, 2, 4])
        span_b = sb("span_b", [P, 2, NG])
        first = sb("first", [P, NG])
        first_i = sb("first_i", [P, NG], I32)
        base_f = sb("base_f", [P, NG])
        off_f = sb("off_f", [P, NG])
        blk_f = sb("blk_f", [P, NG])
        off_i = sb("off_i", [P, NG], I32)
        widest = sb("widest", [P, 1])
        fits = sb("fits", [P, 1])
        ctl_f = sb("ctl_f", [P, 4])
        part_i = sb("part_i", [P, 1], I32)
        iota_i = sb("iota_i", [P, R], I32)
        pow2_i = sb("pow2_i", [P, 1], I32)
        nid_t = sb("nid_t", [QP, 4, P])
        zeros = sb("zeros", [P, ZR * F])
        neglog = sb("neglog", [P, P])
        b2b = sb("b2b", [P, F])
        bsum = sb("bsum", [P, F])
        bpart = [sb(f"bpart{k}", [P, F], BF16) for k in range(3)]
        basis_sb = [sb(f"basis_sb{k}", [F, NBASIS, F]) for k in range(2)]
        comp_sb = [sb(f"comp_sb{k}", [P, R * NBASIS]) for k in range(2)]
        bn = sb("bn", [P, NBX, 6])
        bn_tmp = sb("bn_tmp", [P, NBX])
        h = [sb(f"h{k}", [P, CB, F]) for k in range(2)]
        rest = [sb(f"rest{k}", [P, CB, F]) for k in range(2)]
        split = [sb(f"split{k}", [P, CB, 3, F], BF16) for k in range(2)]

        s_pads = sem("p_pads")
        s_x = sem("p_x")
        s_ids = [sem(f"p_ids{k}") for k in range(2)]
        s_cols = sem("p_cols")
        s_weights = sem("p_weights")
        s_iota = sem("p_iota")
        s_chain = sem("p_chain")
        s_parts = sem("p_parts")
        s_rows = sem("p_rows")
        s_span = sem("p_span")
        s_span_out = sem("p_span_out")
        s_span_in = sem("p_span_in")
        s_nid = sem("p_nid")
        s_nid_tr = sem("p_nid_tr")
        s_nid_cp = sem("p_nid_cp")
        s_nid_out = sem("p_nid_out")
        s_zero = sem("p_zero")
        s_cleared = sem("p_cleared")
        s_neglog = sem("p_neglog")
        s_bsum = sem("p_bsum")
        s_bn = sem("p_bn")
        s_var = sem("p_var")
        s_std = sem("p_std")
        s_scale = sem("p_scale")
        s_h = sem("p_h")
        s_part1 = sem("p_part1")
        s_rest1 = sem("p_rest1")
        s_part2 = sem("p_part2")
        s_part3 = sem("p_part3")
        s_split_out = [sem(f"p_split_out{k}") for k in range(2)]

        x_main = x[0:(NBLK - 1) * P, :].rearrange("(b p) f -> p b f", p=P)
        x_rest = N - (NBLK - 1) * P

        block = ctx.enter_context(nc.Block())

        @block.sync
        def _(sp):
            sp.wait_ge(s_pads, 6)
            for k, ap in enumerate((dst, src)):
                sp.dma_start(ids[k][0:QP - 1, :], ap[0:(QP - 1) * EQ].rearrange("(q e) -> q e", e=EQ)).then_inc(s_ids[k], 16)
                sp.dma_start(ids[k][QP - 1:QP, 0:E - (QP - 1) * EQ],
                             ap[(QP - 1) * EQ:E].rearrange("(a e) -> a e", a=1)).then_inc(s_ids[k], 16)
            sp.dma_start(g.xs[:, 0:NBLK - 1, :], x_main).then_inc(s_x, 16)
            sp.dma_start(g.xs[0:x_rest, NBLK - 1, :], x[(NBLK - 1) * P:N, :]).then_inc(s_x, 16)
            for k in range(2):
                sp.wait_ge(s_parts, k + 1)
                for half in range(2):
                    for s in range(4):
                        sp.dma_start(g.rows_dram[:, half, k, :].rearrange("(q s) e -> q s e", s=4)[:, s, :],
                                     parts[k][:, half, s * GE:(s + 1) * GE]).then_inc(s_rows, 16)
            sp.wait_ge(s_span, 2)
            for k in range(2):
                sp.dma_start(g.span_dram[k, :].rearrange("(q s) -> q s", s=4), span[:, k, :]).then_inc(s_span_out, 16)
            sp.wait_ge(s_span_out, 32)
            sp.dma_start(span_b[:, :, :], g.span_dram.partition_broadcast(P)).then_inc(s_span_in, 16)
            sp.wait_ge(s_nid_cp, 4)
            sp.dma_start(g.nid_dram.rearrange("(c q) p -> q c p", q=QP), nid_t[:, :, :]).then_inc(s_nid_out, 16)
            sp.wait_ge(s_nid_out, 16)
            sp.wait_ge(s_rows, 16 * 16)

        @block.gpsimd
        def _(pool):
            nc.gpsimd.memset(g.ident[:, :], 0.0).then_inc(s_iota, 1)
            pool.wait_ge(s_iota, 1)
            nc.gpsimd.affine_select(out=g.ident[:, :], in_=g.ident[:, :], compare_op=ALU.not_equal, fill=1.0,
                                    base=0, pattern=[[-1, P]], channel_multiplier=1).then_inc(s_iota, 1)
            nc.gpsimd.iota(part_i[:, :], [[0, 1]], base=0, channel_multiplier=1).then_inc(s_iota, 1)
            nc.gpsimd.iota(iota_i[:, :], [[1, R]], base=0, channel_multiplier=0).then_inc(s_iota, 1)
            nc.gpsimd.iota(first_i[:, :], [[P, NG]], base=0, channel_multiplier=0).then_inc(s_iota, 1)

        @block.scalar
        def _(act):
            act.dma_start(g.w2[:, :], W2).then_inc(s_weights, 16)
            act.dma_start(b2b[:, :], b2.partition_broadcast(P)).then_inc(s_weights, 16)
            act.dma_start(g.w1[:, :], W1).then_inc(s_weights, 16)
            act.dma_start(g.b1c[:, :], b1.rearrange("(f a) -> f a", a=1)).then_inc(s_weights, 16)
            for k in range(2):
                act.dma_start(comp_sb[k][:, :], comp[k].rearrange("r b -> (r b)").partition_broadcast(P)).then_inc(s_weights, 16)
                act.dma_start(basis_sb[k][:, :, :], basis[k].rearrange("b i o -> i b o")).then_inc(s_weights, 16)
                act.dma_start(g.wroot[k][:, :], root[k]).then_inc(s_weights, 16)
                act.dma_start(g.biasb[k][:, :], bias[k].partition_broadcast(P)).then_inc(s_weights, 16)
            act.wait_ge(s_pads, 6)
            for ap, col in ((dst, g.dstcol), (src, g.srccol), (edge_type, g.etcol)):
                col_i = col[:, :].bitcast(I32).rearrange("p (g j) -> p g j", j=TG)
                act.dma_start(col_i[:, 0:NG - 1, :],
                              ap[0:(NG - 1) * GE].rearrange("(g p j) -> p g j", p=P, j=TG)).then_inc(s_cols, 16)
                act.dma_start(col_i[0:g.ELAST // TG, NG - 1, :],
                              ap[(NG - 1) * GE:E].rearrange("(p j) -> p j", j=TG)).then_inc(s_cols, 16)
            act.wait_ge(s_zero, 1)
            for k in range(TG):
                to = g.acc_dram[k].rearrange("(p a r) f -> p a (r f)", p=P, r=ZR)
                act.dma_start(to, zeros[:, :].unsqueeze(1).to_broadcast([P, g.NACC // P // ZR, ZR * F])).then_inc(s_cleared, 16)
            act.wait_ge(s_var, 1)
            nc.scalar.activation(g.rstd[:, :], g.rstd[:, :], ACT.Sqrt, bias=g.eps[:, 0:1]).then_inc(s_std, 1)
            act.wait_ge(s_scale, 1)

            def split_chunk(c, k):
                if not isinstance(c, int) or c >= 2:
                    act.wait_ge(s_part3, c - 1)
                for b in range(CB):
                    i = c * CB + b
                    nc.scalar.activation(h[k][:, b, :], g.xs[:, bass.ds(i, 1), :].rearrange("p a f -> p (a f)"), ACT.Relu,
                                         bias=g.shift[:, bass.ds(i, 1)], scale=g.rstd[:, bass.ds(i, 1)]).then_inc(s_h, 1)
                act.wait_ge(s_h, c * CB + CB)
                if not isinstance(c, int) or c >= 2:
                    act.wait_ge(s_split_out[k], half(c, k) * 16)
                nc.scalar.activation(split[k][:, :, 0, :], h[k][:, :, :], ACT.Copy).then_inc(s_part1, 1)
                act.wait_ge(s_rest1, c + 1)
                nc.scalar.activation(split[k][:, :, 1, :], rest[k][:, :, :], ACT.Copy).then_inc(s_part2, 1)

            def half(c, k):
                return c // 2 if isinstance(c, int) else c_half[0] + k // 2

            c_half = [0]
            for c in range(2):
                split_chunk(c, c)
            with act.Fori(1, NCH // 2) as i:
                for k in range(2):
                    c_half[0] = i
                    split_chunk(i * 2 + k, k)
            if NCH % 2:
                split_chunk(NCH - 1, 0)
            for k in range(4):
                act.wait_ge(s_nid_tr, k + 1)
                nc.scalar.activation(nid_t[:, k, :], g.bank[k][0:QP, 0:P], ACT.Copy).then_inc(s_nid_cp, 1)
            act.wait_ge(s_cleared, 16 * TG)

        @block.tensor
        def _(pe):
            pe.wait_ge(s_neglog, 1)
            pe.wait_ge(s_weights, 16 * 12)
            nc.tensor.matmul(g.bank[4][:, 0:F], neglog[:, :], g.w2[:, :], start=True, stop=True).then_inc(s_bsum, 1)
            pe.wait_ge(s_nid, 1)
            pe.wait_ge(s_iota, 5)
            for k in range(4):
                nc.tensor.transpose(g.bank[k][0:QP, 0:P], g.nid_res[:, k * QP:(k + 1) * QP], g.ident[:, :]).then_inc(s_nid_tr, 1)

        @block.vector
        def _(dve):
            chain = Chain(dve, s_chain)
            v = nc.vector
            v.memset(g.xs[:, NBLK - 1:NBX, :], 0.0).then_inc(s_pads, 1)
            v.memset(ids[0][:, :], PAD_DST).then_inc(s_pads, 1)
            v.memset(ids[1][:, :], g.TRASH).then_inc(s_pads, 1)
            v.memset(g.dstcol[:, :].bitcast(I32)[:, (NG - 1) * TG:], PAD_DST).then_inc(s_pads, 1)
            v.memset(g.srccol[:, :].bitcast(I32)[:, (NG - 1) * TG:], g.TRASH).then_inc(s_pads, 1)
            v.memset(g.etcol[:, :].bitcast(I32)[:, (NG - 1) * TG:], 0).then_inc(s_pads, 1)
            v.memset(zeros[:, :], 0.0).then_inc(s_zero, 1)
            v.memset(neglog[:, :], -LOG2).then_inc(s_neglog, 1)
            v.memset(g.eps[:, :], EPS)
            v.memset(g.cnt[:, :, :], 0.0)
            v.memset(g.zero16[:, :], 0.0)
            v.memset(g.ones3[:, :], 1.0)
            v.memset(g.bias3[:, :], 0.0)
            chain(v.memset(g.coef[0:2, :], 1.0))
            chain(v.memset(g.coef[0:1, :], float(P)))

            for k in range(2):
                dve.wait_ge(s_ids[k], 32)
                chain(v.tensor_scalar(idt[:, :], ids[k][:, :], 7, None, ALU.arith_shift_right))
                chain(v.tensor_copy(parts[k][:, 0, :], idt[:, :]))
                chain(v.tensor_scalar(idt[:, :], ids[k][:, :], P - 1, None, ALU.bitwise_and))
                v.tensor_copy(parts[k][:, 1, :], idt[:, :]).then_inc(s_parts, 1)
                if k == 0:
                    chain(v.tensor_copy(idf[:, :], ids[0][:, :]))
                    v.tensor_reduce(span[:, 0, :], idf[:, :].rearrange("q (s e) -> q s e", s=4), AX_X, ALU.min).then_inc(s_span, 1)
                    dve.wait_ge(s_span, 1)
                    chain(v.scalar_tensor_tensor(idf[:, :], idf[:, :], float(PAD_DST), idf[:, :], ALU.is_lt, ALU.mult))
                    v.tensor_reduce(span[:, 1, :], idf[:, :].rearrange("q (s e) -> q s e", s=4), AX_X, ALU.max).then_inc(s_span, 1)
                    dve.wait_ge(s_parts, 1)

            dve.wait_ge(s_x, 32)
            with dve.Fori(0, NCH) as i:
                for k in range(CB):
                    b = i * CB + k
                    v.bn_stats(bn[:, bass.ds(b, 1), :].rearrange("p a k -> p (a k)"),
                               g.xs[:, bass.ds(b, 1), :].rearrange("p a f -> p (a f)")).then_inc(s_bn, 1)
            dve.wait_ge(s_bn, NBX)
            norm_stats(nc, chain, g, bn, bn_tmp)
            v.engine_nop().then_inc(s_var, 1)
            dve.wait_ge(s_std, 1)
            norm_scale(nc, chain, g)
            v.engine_nop().then_inc(s_scale, 1)

            def split_chunk(c, k):
                dve.wait_ge(s_part1, c + 1)
                v.tensor_tensor(rest[k][:, :, :], h[k][:, :, :], split[k][:, :, 0, :], ALU.subtract).then_inc(s_rest1, 1)
                dve.wait_ge(s_part2, c + 1)
                v.tensor_tensor(split[k][:, :, 2, :], rest[k][:, :, :], split[k][:, :, 1, :], ALU.subtract).then_inc(s_part3, 1)

            with dve.Fori(0, NCH // 2) as i:
                for k in range(2):
                    split_chunk(i * 2 + k, k)
            if NCH % 2:
                split_chunk(NCH - 1, 0)

            dve.wait_ge(s_iota, 5)
            chain(v.tensor_copy(g.part[:, :], part_i[:, :]))
            chain(v.tensor_copy(g.iota_r[:, :], iota_i[:, :]))
            chain(v.tensor_copy(first[:, :], first_i[:, :]))
            chain(v.tensor_scalar(g.trash_row[:, :], g.part[:, :], float(g.TRASH + 1), None, ALU.add))
            chain(v.tensor_scalar(pow2_i[:, :], g.part[:, :], -float(1 << 23), 190.0 * (1 << 23), ALU.mult, ALU.add))
            chain(v.tensor_copy(g.pow2[:, :], pow2_i[:, :].bitcast(F32)))
            chain(v.tensor_scalar(g.dup_above[:, :], pow2_i[:, :].bitcast(F32), 2.5, None, ALU.mult))

            dve.wait_ge(s_span_in, 16)
            chain(v.tensor_tensor(off_f[:, :], span_b[:, 1, :], span_b[:, 0, :], ALU.subtract))
            chain(v.reduce_max(widest[:, :], off_f[:, :], AX_X))
            chain(v.tensor_scalar(fits[:, :], widest[:, :], float(P), None, ALU.is_lt))
            chain(v.tensor_tensor(base_f[:, :], span_b[:, 0, :], first[:, :], ALU.subtract))
            chain(v.scalar_tensor_tensor(base_f[:, :], base_f[:, :], fits[:, 0:1], first[:, :], ALU.mult, ALU.add))
            chain(v.tensor_copy(g.base[:, :], base_f[:, :]))
            chain(v.tensor_scalar(g.blk[:, 1:], g.base[:, :], 7, None, ALU.arith_shift_right))
            chain(v.tensor_scalar(off_i[:, :], g.base[:, :], P - 1, None, ALU.bitwise_and))
            chain(v.tensor_copy(blk_f[:, :], g.blk[:, 1:]))
            chain(v.tensor_copy(off_f[:, :], off_i[:, :]))
            chain(v.tensor_scalar(g.mask_hi[:, 1:], off_f[:, :], g.part[:, 0:1], None, ALU.is_le))
            chain(v.tensor_scalar(g.mask_lo[:, 1:], g.mask_hi[:, 1:], -1.0, 1.0, ALU.mult, ALU.add))
            chain(v.tensor_scalar(g.nid_lin[:, :], base_f[:, :], g.part[:, 0:1], None, ALU.add))
            chain(v.tensor_scalar(blk_f[:, :], blk_f[:, :], float(P), g.part[:, 0:1], ALU.mult, ALU.add))
            v.scalar_tensor_tensor(g.nid_res[:, :], g.mask_lo[:, 1:], float(P), blk_f[:, :], ALU.mult, ALU.add).then_inc(s_nid, 1)
            for t in (g.mask_hi, g.mask_lo, g.blk):
                chain(v.tensor_copy(t[:, 0:1], t[:, NBLK:NBLK + 1]))
            chain(v.tensor_scalar(ctl_f[:, 0:1], fits[:, :], 1.0 - NBLK, float(NBLK), ALU.mult, ALU.add))
            chain(v.tensor_copy(ctl_f[:, 1:2], fits[:, :]))
            chain(v.tensor_scalar(ctl_f[:, 2:3], fits[:, :], -float(NBLK), float(NBLK), ALU.mult, ALU.add))
            chain(v.tensor_copy(g.ctl[:, 0:3], ctl_f[:, 0:3]))

            dve.wait_ge(s_cols, 96)
            for col in (g.dstcol, g.srccol, g.etcol):
                chain(v.tensor_copy(col[:, :], col[:, :].bitcast(I32)))

            dve.wait_ge(s_bsum, 1)
            chain(v.tensor_tensor(bsum[:, :], g.bank[4][:, 0:F], b2b[:, :], ALU.add))
            for k in range(3):
                chain(v.tensor_copy(bpart[k][:, :], bsum[:, :]))
                chain(v.tensor_tensor(bsum[:, :], bsum[:, :], bpart[k][:, :], ALU.subtract))
                for j in range(TG):
                    chain(v.tensor_copy(g.bias3[32 * k:32 * k + 1, j * F:(j + 1) * F], bpart[k][32 * k:32 * k + 1, :]))

            for k in range(2):
                for r in range(R):
                    w = g.wrel[k][:, r * F:(r + 1) * F]
                    chain(v.tensor_scalar(w, basis_sb[k][:, 0, :], comp_sb[k][:, r * NBASIS:r * NBASIS + 1], None, ALU.mult))
                    for b in range(1, NBASIS):
                        c = r * NBASIS + b
                        chain(v.scalar_tensor_tensor(w, basis_sb[k][:, b, :], comp_sb[k][:, c:c + 1], w, ALU.mult, ALU.add))

        @block.gpsimd
        def _(pool):
            to = g.split_dram.rearrange("(c b p) f -> c p b f", b=CB, p=P)
            with pool.Fori(0, NCH // 2) as i:
                for k in range(2):
                    pool.wait_ge(s_part3, i * 2 + k + 1)
                    pool.dma_start(to[bass.ds(i * 2 + k, 1)].rearrange("a p b f -> p (a b) f"),
                                   split[k][:, :, :, :].rearrange("p b k f -> p b (k f)")).then_inc(s_split_out[k], 16)
            if NCH % 2:
                pool.wait_ge(s_part3, NCH)
                pool.dma_start(to[NCH - 1], split[0][:, :, :, :].rearrange("p b k f -> p b (k f)")).then_inc(s_split_out[0], 16)
            pool.wait_ge(s_split_out[0], 16 * (NCH - NCH // 2))
            pool.wait_ge(s_split_out[1], 16 * (NCH // 2))


def filter_layer(nc, g, edge_attr):
    N, E, NG = g.N, g.E, g.NG
    NE = 4
    with ExitStack() as ctx:
        def sb(name, shape, dt=F32):
            return ctx.enter_context(nc.sbuf_tensor(name, shape, dt))

        def sem(name):
            return nc.alloc_semaphore(name)

        edges = [sb(f"edges{k}", [P, TG, F]) for k in range(NE)]
        rows = [sb(f"rows{k}", [2, 2, GE], BF16) for k in range(NE)]
        nid_row = [sb(f"nid_row{k}", [P, P]) for k in range(2)]
        win = [sb(f"win{k}", [P, 3 * F], BF16) for k in range(2)]
        edges_t = [sb(f"edges_t{k}", [F, GE]) for k in range(2)]
        grown = [sb(f"grown{k}", [F, GE]) for k in range(2)]
        soft = [sb(f"soft{k}", [F, GE]) for k in range(2)]
        factor = [sb(f"factor{k}", [P, GE]) for k in range(2)]
        same = [sb(f"same{k}", [P, TG, P]) for k in range(2)]
        msg = [sb(f"msg{k}", [P, TG, F]) for k in range(2)]
        total = [sb(f"total{k}", [P, TG, F]) for k in range(2)]
        to_edge = [sb(f"to_edge{k}", [P, TG, P], BF16) for k in range(2)]
        to_node = [sb(f"to_node{k}", [P, TG, P], BF16) for k in range(2)]
        types = [sb(f"types{k}", [P, TG, R], BF16) for k in range(2)]
        dup = sb("dup", [P, TG])
        idx = [sb(f"idx{k}", [P, TG], I32) for k in range(2)]

        bank_t, bank_z, bank_e, bank_r = g.bank[0], g.bank[1:3], g.bank[3], g.bank[4]
        bank_h, bank_c, bank_s = g.bank[5], g.bank[6], g.bank[7]
        counts = bank_s[:, 0:R]
        leaders = bank_s[:, 256:256 + TG]

        s_edges = [sem(f"f_edges{k}") for k in range(NE)]
        s_rows = [sem(f"f_rows{k}") for k in range(NE)]
        s_nid = [sem(f"f_nid{k}") for k in range(2)]
        s_win = [sem(f"f_win{k}") for k in range(2)]
        s_tr = sem("f_tr")
        s_trc = sem("f_trc")
        s_z = sem("f_z")
        s_exp = sem("f_exp")
        s_clamp = sem("f_clamp")
        s_ln = sem("f_ln")
        s_soft = sem("f_soft")
        s_e = sem("f_e")
        s_ec = sem("f_ec")
        s_src = sem("f_src")
        s_same = sem("f_same")
        s_dst = sem("f_dst")
        s_hot = sem("f_hot")
        s_hot2 = sem("f_hot2")
        s_types = sem("f_types")
        s_pass = sem("f_pass")
        s_cnt = sem("f_cnt")
        s_msg = sem("f_msg")
        s_total = sem("f_total")
        s_totc = sem("f_totc")
        s_dup = sem("f_dup")
        s_idx = sem("f_idx")
        s_sc = [sem(f"f_sc{j}") for j in range(TG)]

        def passes_before(s, w, one, many):
            last = max(s.at(3), 0) if isinstance(s.i, int) else s.at(3)
            return s.at(2) * many + w + last * one + 1

        block = ctx.enter_context(nc.Block())

        @block.sync
        def _(sp):
            passes, one, many = g.controls(sp)

            def step(s):
                if s.live(0, NG):
                    k = s.slot(NE, 0)
                    need(sp, s_tr, s.at(NE - 1))
                    if isinstance(s.i, int) and s.c == NG - 1 and g.ELAST < GE:
                        sp.dma_start(edges[k][0:g.ELAST // TG, :, :],
                                     edge_attr[(NG - 1) * GE:E, :].rearrange("(p j) f -> p j f", j=TG)).then_inc(s_edges[k], 16)
                    else:
                        sp.dma_start(edges[k][:, :, :],
                                     edge_attr[bass.ds(s.at(0) * GE, GE), :].rearrange("(p j) f -> p j f", j=TG)).then_inc(s_edges[k], 16)
                    need(sp, s_dst, s.at(NE - 1))
                    sp.dma_start(rows[k][:, :, :],
                                 g.rows_dram[bass.ds(s.at(0), 1)].rearrange("a h d e -> (a h) d e")).then_inc(s_rows[k], 16)
                if s.live(2, NG):
                    k = s.slot(2, 2)
                    with sp.Fori(0, passes) as w:
                        at = g.entry(sp, s.at(2) * one + w)
                        sp.wait_ge(s_pass, passes_before(s, w, one, many))
                        sp.dma_start(nid_row[k][:, :],
                                     g.nid_dram[bass.ds(at, 1), :].rearrange("a p -> (a p)").partition_broadcast(P)).then_inc(s_nid[k], 16)
                        first = sp.value_load(g.base[0:1, bass.ds(at, 1)], min_val=0, max_val=g.NROWS)
                        sp.dma_start(win[k][:, :], g.split_dram[bass.ds(first, P), :]).then_inc(s_win[k], 16)

            run_steps(sp, NG - UNROLL, UNROLL + 4, step)

        @block.tensor
        def _(pe):
            passes, one, many = g.controls(pe)
            nc.tensor.matmul(counts, g.zero16[0:1, 0:P], g.zero16[0:1, 0:R], start=True, stop=True).then_inc(s_pass, 1)

            def step(s):
                if s.live(0, NG):
                    need(pe, s_edges[s.slot(NE, 0)], s.use(NE, 0) * 16 + 16)
                    need(pe, s_trc, s.at(0))
                    for j in range(TG):
                        ins = nc.tensor.transpose(bank_t[:, j * P:(j + 1) * P], edges[s.slot(NE, 0)][:, j, :], g.ident[:, :])
                    ins.then_inc(s_tr, 1)
                if s.live(2, NG):
                    need(pe, s_rows[s.slot(NE, 2)], s.use(NE, 2) * 16 + 16)
                    if s.c > 2:
                        pe.wait_ge(s_hot, s.at(2) * passes)
                    nc.tensor.matmul(bank_r[:, :], g.coef[0:2, :], rows[s.slot(NE, 2)][0:2, 1, :],
                                     start=True, stop=True).then_inc(s_src, 1)
                if s.live(1, NG):
                    need(pe, s_trc, s.at(1) + 1)
                    need(pe, s_soft, s.at(2))
                    nc.tensor.matmul(bank_z[s.slot(2, 1)][:, :], g.w1[:, :], edges_t[s.slot(2, 1)][:, :],
                                     start=True, stop=True).then_inc(s_z, 1)
                if s.live(3, NG):
                    k = s.slot(2, 3)
                    need(pe, s_same, s.at(3) + 1)
                    need(pe, s_msg, s.at(3) + 1)
                    need(pe, s_totc, s.at(3))
                    need(pe, s_dup, s.at(3))
                    for j in range(TG):
                        nc.tensor.matmul(bank_c[:, j * F:(j + 1) * F], same[k][:, j, :], msg[k][:, j, :], start=True, stop=True)
                        ins = nc.tensor.matmul(leaders[:, j:j + 1], same[k][:, j, :].bitcast(BF16)[:, 1::2], g.pow2[:, :],
                                               start=True, stop=True)
                    ins.then_inc(s_total, 1)
                if s.live(2, NG):
                    k = s.slot(2, 2)
                    pe.wait_ge(s_same, s.at(2) + 1)
                    nc.tensor.matmul(bank_r[:, :], g.coef[0:2, :], rows[s.slot(NE, 2)][0:2, 0, :],
                                     start=True, stop=True).then_inc(s_dst, 1)
                    need(pe, s_soft, s.at(2) + 1)
                    need(pe, s_ec, s.at(2))
                    nc.tensor.matmul(bank_e[:, :], g.ones3[0:96, :], g.bias3[0:96, :], start=True, stop=True)
                    for j in range(TG):
                        ins = nc.tensor.matmul(bank_e[:, j * F:(j + 1) * F], soft[k][:, j * P:(j + 1) * P], g.w2[:, :],
                                               start=False, stop=True, skip_group_check=True)
                    ins.then_inc(s_e, 1)
                    need(pe, s_dup, s.at(3) + 1 if s.live(3, NG) else 0)
                    need(pe, s_msg, s.at(2))
                    nc.tensor.matmul(bank_h[:, :], g.zero16[0:1, 0:P], g.zero16[0:1, :], start=True, stop=True)
                    pe.wait_ge(s_types, s.at(2) + 1)
                    apart(pe, g.gate["pe"])
                    with pe.Fori(0, passes) as w:
                        q = pe.snap(s.at(2) * passes + w)
                        pe.wait_ge(s_hot, q + 1)
                        pe.wait_ge(s_win[k], (s.use(2, 2) * passes + w) * 16 + 16)
                        for j in range(TG):
                            for part in range(3):
                                nc.tensor.matmul(bank_h[:, j * F:(j + 1) * F], to_edge[k][:, j, :], win[k][:, part * F:(part + 1) * F],
                                                 start=False, stop=True, skip_group_check=True)
                        pe.wait_ge(s_hot2, q + 1)
                        pe.wait_ge(s_cnt, q * 2 + 3)
                        for j in range(TG):
                            ins = nc.tensor.matmul(counts, to_node[k][:, j, :], types[k][:, j, :], start=j == 0, stop=j == TG - 1)
                        ins.then_inc(s_pass, 1)

            run_steps(pe, NG, 4, step)

        @block.scalar
        def _(act):
            def step(s):
                if s.live(0, NG):
                    need(act, s_tr, s.at(0) + 1)
                    need(act, s_z, s.at(1))
                    nc.scalar.activation(edges_t[s.slot(2, 0)][:, :], bank_t[:, :], ACT.Copy).then_inc(s_trc, 1)
                if s.live(1, NG):
                    need(act, s_z, s.at(1) + 1)
                    need(act, s_soft, s.at(2))
                    nc.scalar.activation(grown[s.slot(2, 1)][:, :], bank_z[s.slot(2, 1)][:, :], ACT.Exp,
                                         bias=g.b1c[:, 0:1]).then_inc(s_exp, 1)
                if s.live(3, NG):
                    need(act, s_total, s.at(3) + 1)
                    for j in range(TG):
                        need(act, s_sc[j], s.at(4) * 16)
                    nc.scalar.activation(total[s.slot(2, 3)][:, :, :].rearrange("p a b -> p (a b)"), bank_c[:, :],
                                         ACT.Copy).then_inc(s_totc, 1)
                if s.live(1, NG):
                    need(act, s_clamp, s.at(1) + 1)
                    nc.scalar.activation(grown[s.slot(2, 1)][:, :], grown[s.slot(2, 1)][:, :], ACT.Ln, bias=1.0).then_inc(s_ln, 1)
                if s.live(2, NG):
                    need(act, s_e, s.at(2) + 1)
                    need(act, s_msg, s.at(3))
                    nc.scalar.activation(factor[s.slot(2, 2)][:, :], bank_e[:, :], ACT.Copy).then_inc(s_ec, 1)

            nc.scalar.preload_act_table_set("natural_log_exp_and_others")
            run_steps(act, NG, 4, step)

        @block.vector
        def _(dve):
            v = nc.vector
            passes, one, many = g.controls(dve)
            v.engine_nop().then_inc(s_cnt, 1)

            def add_counts(entry, q):
                dve.wait_ge(s_pass, q + 1)
                dve.wait_ge(s_cnt, q * 2 + 1)
                b = dve.value_load(g.blk[0:1, bass.ds(entry, 1)], min_val=0, max_val=g.NBLK - 1)
                for mask, at in ((g.mask_hi, b), (g.mask_lo, b + 1)):
                    to = g.cnt[:, bass.ds(at, 1), :].rearrange("p a r -> p (a r)")
                    v.scalar_tensor_tensor(to, counts, mask[:, bass.ds(entry, 1)], to, ALU.mult, ALU.add).then_inc(s_cnt, 1)

            def step(s):
                if s.live(3, NG):
                    dve.wait_ge(s_pass, s.at(2) * passes + 1)
                    need(dve, s_ec, s.at(3) + 1)
                    need(dve, s_total, s.at(4))
                    v.tensor_tensor(msg[s.slot(2, 3)][:, :, :].rearrange("p a b -> p (a b)"), bank_h[:, :], factor[s.slot(2, 3)][:, :],
                                    ALU.mult).then_inc(s_msg, 1)
                if s.live(2, NG):
                    k = s.slot(2, 2)
                    four = bass.ds(s.at(2) * TG, TG)
                    need(dve, s_src, s.at(2) + 1)
                    need(dve, s_total, s.at(3))
                    v.tensor_tensor(same[k][:, :, :], bank_r[:, :].rearrange("q (p j) -> q j p", j=TG),
                                    g.srccol[:, four].unsqueeze(2).to_broadcast([P, TG, P]), ALU.is_equal).then_inc(s_same, 1)
                if s.live(1, NG):
                    need(dve, s_exp, s.at(1) + 1)
                    t = grown[s.slot(2, 1)]
                    v.tensor_scalar(t[:, :], t[:, :], EXP_CLAMP, None, ALU.min).then_inc(s_clamp, 1)
                if s.live(3, NG):
                    need(dve, s_total, s.at(3) + 1)
                    need(dve, s_idx, s.at(3))
                    v.tensor_scalar(dup[:, :], leaders, g.dup_above[:, 0:1], g.trash_row[:, 0:1], ALU.is_gt, ALU.mult).then_inc(s_dup, 1)
                if s.live(2, NG):
                    dve.wait_ge(s_pass, passes_before(s, 0, one, many))
                    v.tensor_tensor(types[k][:, :, :], g.etcol[:, four].unsqueeze(2).to_broadcast([P, TG, R]),
                                    g.iota_r[:, :].unsqueeze(1).to_broadcast([P, TG, R]), ALU.is_equal).then_inc(s_types, 1)
                    dve.wait_ge(s_dst, s.at(2) + 1)
                    apart(dve, g.gate["dve"])
                    with dve.Fori(0, passes) as w:
                        at = g.entry(dve, s.at(2) * one + w)
                        q = dve.snap(s.at(2) * passes + w)
                        dve.wait_ge(s_pass, passes_before(s, w, one, many))
                        v.tensor_scalar(to_edge[k][:, :, :], bank_r[:, :].rearrange("q (p j) -> q j p", j=TG),
                                        g.nid_lin[:, bass.ds(at, 1)], None, ALU.is_equal).then_inc(s_hot, 1)
                        dve.wait_ge(s_nid[k], (s.use(2, 2) * passes + w) * 16 + 16)
                        v.tensor_tensor(to_node[k][:, :, :], nid_row[k][:, :].unsqueeze(1).to_broadcast([P, TG, P]),
                                        g.dstcol[:, four].unsqueeze(2).to_broadcast([P, TG, P]), ALU.is_equal).then_inc(s_hot2, 1)
                        add_counts(at, q)
                if s.live(3, NG):
                    need(dve, s_totc, s.at(3) + 1)
                    need(dve, s_dup, s.at(3) + 1)
                    v.tensor_tensor(idx[s.slot(2, 3)][:, :], dup[:, :], g.srccol[:, bass.ds(s.at(3) * TG, TG)],
                                    ALU.max).then_inc(s_idx, 1)
                if s.live(1, NG):
                    need(dve, s_ln, s.at(1) + 1)
                    need(dve, s_e, s.at(2))
                    v.scalar_tensor_tensor(soft[s.slot(2, 1)][:, :], bank_z[s.slot(2, 1)][:, :], g.b1c[:, 0:1],
                                           grown[s.slot(2, 1)][:, :], ALU.add, ALU.max).then_inc(s_soft, 1)

            run_steps(dve, NG, 4, step)
            add_counts(g.entry(dve, (NG - 1) * one + passes, NG), passes * NG)

        @block.gpsimd
        def _(pool):

            def step(s):
                k = s.slot(2, 0)
                need(pool, s_idx, s.at(0) + 1)
                need(pool, s_totc, s.at(0) + 1)
                for j in range(TG):
                    need(pool, s_sc[j], s.at(0) * 16)
                    apart(pool, g.gate["pool"])
                    pool.indirect_dma_start(g.acc_dram[j][:, :], bass.IndirectOffsetOnAxis(ap=idx[k][:, j:j + 1], axis=0),
                                            total[k][:, j, :], None, compute_op=ALU.add).then_inc(s_sc[j], 16)

            run_steps(pool, NG, 0, step)
            for j in range(TG):
                pool.wait_ge(s_sc[j], NG * 16)


def sum_layer(nc, g):
    NBLK, NBX = g.NBLK, g.NBX
    with ExitStack() as ctx:
        def sb(name, shape, dt=F32):
            return ctx.enter_context(nc.sbuf_tensor(name, shape, dt))

        def sem(name):
            return nc.alloc_semaphore(name)

        SLOTS = 2
        sums = [sb(f"sums{k}", [P, TG, F]) for k in range(SLOTS)]
        added = [sb(f"added{k}", [P, F]) for k in range(SLOTS)]
        bn = sb("bn2", [P, NBX, 6])
        bn_tmp = sb("bn2_tmp", [P, NBX])
        rest = sb("rest2", [P, NBX, R])
        seg = sb("seg", [P, g.NT])
        s_sums = [sem(f"a_sums{k}") for k in range(SLOTS)]
        s_added = sem("a_added")
        s_x = sem("a_x")
        s_bn = sem("a_bn")
        s_var = sem("a_var")
        s_std = sem("a_std")
        s_chain = sem("a_chain")
        block = ctx.enter_context(nc.Block())

        @block.sync
        def _(sp):
            def load(b, k):
                for j in range(TG):
                    sp.dma_start(sums[k][:, j, :], g.acc_dram[j][bass.ds(b * P, P), :]).then_inc(s_sums[k], 16)

            for k in range(SLOTS):
                load(k, k)
            with sp.Fori(1, NBLK // SLOTS) as i:
                for k in range(SLOTS):
                    sp.wait_ge(s_added, i * SLOTS + k - 1)
                    load(i * SLOTS + k, k)

        @block.scalar
        def _(act):
            act.wait_ge(s_var, 1)
            nc.scalar.activation(g.rstd[:, :], g.rstd[:, :], ACT.Sqrt, bias=g.eps[:, 0:1]).then_inc(s_std, 1)

        @block.vector
        def _(dve):
            v = nc.vector
            chain = Chain(dve, s_chain)

            chain(v.tensor_scalar(seg[:, :], g.srccol[:, :], float(R), None, ALU.mult))
            chain(v.tensor_tensor(seg[:, :], seg[:, :], g.etcol[:, :], ALU.add))
            chain(v.tensor_scalar(g.srccol[:, :].bitcast(I32), seg[:, :], float(g.NROWS * R - 1), None, ALU.min))

            with dve.Fori(0, NBLK // SLOTS) as i:
                for k in range(SLOTS):
                    b = i * SLOTS + k
                    dve.wait_ge(s_sums[k], i * (16 * TG) + 16 * TG)
                    v.tensor_reduce(added[k][:, :], sums[k][:, :, :].rearrange("p j f -> p f j"), AX_X, ALU.add).then_inc(s_added, 1)
                    dve.wait_ge(s_added, b + 1)
                    to = g.xs[:, bass.ds(b, 1), :].rearrange("p a f -> p (a f)")
                    v.tensor_tensor(to, to, added[k][:, :], ALU.add).then_inc(s_x, 1)
                    dve.wait_ge(s_x, b + 1)
                    v.bn_stats(bn[:, bass.ds(b, 1), :].rearrange("p a k -> p (a k)"), to).then_inc(s_bn, 1)
            chain(v.memset(bn[:, NBLK:NBX, :], 0.0))
            dve.wait_ge(s_bn, NBLK)
            norm_stats(nc, chain, g, bn, bn_tmp)
            v.engine_nop().then_inc(s_var, 1)
            dve.wait_ge(s_std, 1)
            norm_scale(nc, chain, g)

            chain(v.tensor_scalar(g.cnt[:, :, :], g.cnt[:, :, :], 1.0, None, ALU.max))
            chain(v.reciprocal(g.cnt[:, :, :], g.cnt[:, :, :]))
            chain(v.tensor_copy(rest[:, :, :], g.cnt[:, :, :]))
            for k in range(3):
                part = g.rcnt3[:, :, k * R:(k + 1) * R]
                chain(v.tensor_copy(part, rest[:, :, :]))
                if k < 2:
                    chain(v.tensor_tensor(rest[:, :, :], rest[:, :, :], part, ALU.subtract))


def make_table(nc, g, hacc, which):
    NBLK = g.NBLK
    with ExitStack() as ctx:
        def sb(name, shape, dt=F32):
            return ctx.enter_context(nc.sbuf_tensor(f"{name}_{which}", shape, dt))

        def sem(name):
            return nc.alloc_semaphore(f"{name}_{which}")

        NST = 4
        h = [sb(f"th{k}", [P, F]) for k in range(2)]
        h_t = [sb(f"th_t{k}", [F, P]) for k in range(2)]
        made = [sb(f"made{k}", [P, R * F]) for k in range(NST)]
        own = [sb(f"own{k}", [P, F]) for k in range(2)]
        s_h = sem("t_h")
        s_tr = sem("t_tr")
        s_trc = sem("t_trc")
        s_mm = sem("t_mm")
        s_left = sem("t_left")
        s_right = sem("t_right")
        s_own = sem("t_own")
        s_sum = sem("t_sum")
        s_out = [sem(f"t_out{k}") for k in range(NST)]
        table = g.table_dram.rearrange("(b p r) f -> b p (r f)", p=P, r=R)
        wrel, wroot, biasb = g.wrel[which], g.wroot[which], g.biasb[which]
        block = ctx.enter_context(nc.Block())
        HALF = R * F // 2

        def blocks(eng, body):
            n = NBLK // UNROLL * UNROLL
            run_steps(eng, n, 0, body)
            for c in range(n, NBLK + 1):
                body(Step(0, c))

        def one(ap, at):
            return ap[:, bass.ds(at, 1), :].rearrange("p a f -> p (a f)")

        @block.scalar
        def _(act):
            def step(s):
                if s.live(0, NBLK):
                    k = s.slot(2, 0)
                    need(act, s_tr, s.at(1))
                    if which == 0:
                        nc.scalar.activation(h[k][:, :], one(g.xs, s.at(0)), ACT.Relu, bias=g.shift[:, bass.ds(s.at(0), 1)],
                                             scale=g.rstd[:, bass.ds(s.at(0), 1)]).then_inc(s_h, 1)
                    else:
                        nc.scalar.activation(h[k][:, :], one(hacc, s.at(0)), ACT.Relu).then_inc(s_h, 1)
                if s.live(1, NBLK):
                    need(act, s_mm, s.at(1) + 1)
                    need(act, s_out[s.slot(NST, 1)], s.use(NST, 1) * 16)
                    nc.scalar.activation(made[s.slot(NST, 1)][:, HALF:], g.bank[4 + s.slot(2, 1)][:, :], ACT.Copy).then_inc(s_right, 1)
                if s.live(0, NBLK):
                    need(act, s_tr, s.at(0) + 1)
                    need(act, s_mm, s.at(1))
                    nc.scalar.activation(h_t[k][:, :], g.bank[k][:, 0:P], ACT.Copy).then_inc(s_trc, 1)

            blocks(act, step)

        @block.tensor
        def _(pe):
            def step(s):
                if s.live(0, NBLK):
                    k = s.slot(2, 0)
                    need(pe, s_h, s.at(0) + 1)
                    need(pe, s_trc, s.at(1))
                    nc.tensor.transpose(g.bank[k][:, 0:P], h[k][:, :], g.ident[:, :]).then_inc(s_tr, 1)
                if s.live(1, NBLK):
                    k = s.slot(2, 1)
                    need(pe, s_trc, s.at(1) + 1)
                    need(pe, s_left, s.at(2))
                    need(pe, s_right, s.at(2))
                    need(pe, s_own, s.at(2))
                    nc.tensor.matmul(g.bank[2 + k][:, :], h_t[k][:, :], wrel[:, 0:HALF], start=True, stop=True)
                    nc.tensor.matmul(g.bank[4 + k][:, :], h_t[k][:, :], wrel[:, HALF:], start=True, stop=True)
                    nc.tensor.matmul(g.bank[6 + k][:, 0:F], h_t[k][:, :], wroot[:, :], start=True, stop=True).then_inc(s_mm, 1)

            blocks(pe, step)

        @block.vector
        def _(dve):
            v = nc.vector
            if which == 0:
                v.memset(hacc[:, NBLK:, :], 0.0)

            def step(s):
                if s.live(1, NBLK):
                    k = s.slot(2, 1)
                    need(dve, s_mm, s.at(1) + 1)
                    need(dve, s_out[s.slot(NST, 1)], s.use(NST, 1) * 16)
                    v.tensor_copy(made[s.slot(NST, 1)][:, 0:HALF], g.bank[2 + k][:, :]).then_inc(s_left, 1)
                    if which == 0:
                        v.tensor_tensor(one(hacc, s.at(1)), g.bank[6 + k][:, 0:F], biasb[:, :], ALU.add).then_inc(s_own, 1)
                    else:
                        need(dve, s_sum, s.at(2))
                        v.tensor_tensor(own[k][:, :], g.bank[6 + k][:, 0:F], biasb[:, :], ALU.add).then_inc(s_own, 1)
                        need(dve, s_own, s.at(1) + 1)
                        v.tensor_tensor(one(g.xs, s.at(1)), one(g.xs, s.at(1)), own[k][:, :], ALU.add).then_inc(s_sum, 1)

            blocks(dve, step)

        @block.sync
        def _(sp):
            def step(s):
                if s.live(1, NBLK):
                    k = s.slot(NST, 1)
                    need(sp, s_left, s.at(1) + 1)
                    need(sp, s_right, s.at(1) + 1)
                    sp.dma_start(table[bass.ds(s.at(1), 1)].rearrange("a p c -> (a p) c"), made[k][:, :]).then_inc(s_out[k], 16)

            blocks(sp, step)
            for k in range(NST):
                sp.wait_ge(s_out[k], 16 * len(range(k, NBLK, NST)))


def convolve(nc, g, hacc, which):
    NG = g.NG
    sums = hacc if which == 0 else g.xs
    weigh = which == 0
    NGA = 4
    with ExitStack() as ctx:
        def sb(name, shape, dt=F32):
            return ctx.enter_context(nc.sbuf_tensor(f"{name}_{which}", shape, dt))

        def sem(name):
            return nc.alloc_semaphore(f"{name}_{which}")

        idx = [sb(f"cidx{k}", [P, TG], I32) for k in range(NGA)]
        got = [sb(f"got{k}", [P, TG, F]) for k in range(NGA)]
        nid_row = [sb(f"cnid{k}", [P, P]) for k in range(2)]
        share = [sb(f"share{k}", [P, TG, P]) for k in range(2)]
        if weigh:
            rows = [sb(f"crows{k}", [2, GE], BF16) for k in range(4)]
            to_edge = [sb(f"cto_edge{k}", [P, TG, P], BF16) for k in range(2)]
            lower = [sb(f"lower{k}", [P, 3 * R], BF16) for k in range(2)]
            win = [sb(f"cwin{k}", [P, 3 * R], BF16) for k in range(2)]
            types = sb("ctypes", [P, TG, R])
            by_type = sb("by_type", [P, TG, R])

        bank_r, bank_w, bank_a = g.bank[0], g.bank[1], g.bank[2]
        window = bank_a[:, 0:F]
        rates = bank_w[:, 0:TG * 3 * R]

        s_idx = sem("c_idx")
        s_got = [sem(f"c_got{k}") for k in range(NGA)]
        s_nid = [sem(f"c_nid{k}") for k in range(2)]
        s_rows = [sem(f"c_rows{k}") for k in range(4)]
        s_share = sem("c_share")
        s_pass = sem("c_pass")
        s_sum = sem("c_sum")
        s_dst = sem("c_dst")
        s_hot = sem("c_hot")
        s_low = sem("c_low")
        s_rate = sem("c_rate")
        s_step = sem("c_step")
        block = ctx.enter_context(nc.Block())

        def passes_before(s, lag, w, one, many):
            last = max(s.at(lag + 1), 0) if isinstance(s.i, int) else s.at(lag + 1)
            return s.at(lag) * many + w + last * one + 1

        @block.sync
        def _(sp):
            passes, one, many = g.controls(sp)

            def step(s):
                if weigh and s.live(0, NG):
                    k = s.slot(4, 0)
                    need(sp, s_dst, s.at(3))
                    sp.dma_start(rows[k][:, :], g.rows_dram[bass.ds(s.at(0), 1), :, 0, :].rearrange("a h e -> (a h) e")).then_inc(s_rows[k], 16)
                if s.live(1, NG):
                    k = s.slot(2, 1)
                    with sp.Fori(0, passes) as w:
                        sp.wait_ge(s_pass, passes_before(s, 1, w, one, many))
                        sp.dma_start(nid_row[k][:, :], g.nid_dram[bass.ds(g.entry(sp, s.at(1) * one + w), 1), :]
                                     .rearrange("a p -> (a p)").partition_broadcast(P)).then_inc(s_nid[k], 16)

            run_steps(sp, NG, 1, step)

        @block.gpsimd
        def _(pool):
            passes = pool.value_load(g.ctl[0:1, 0:1], min_val=1, max_val=g.NBLK)

            def step(s):
                k = s.slot(NGA, 0)
                need(pool, s_idx, s.at(0) + 1)
                if not isinstance(s.i, int):
                    pool.wait_ge(s_pass, s.at(NGA - 1) * passes + 1)
                apart(pool, g.gate["pool"])
                for j in range(TG):
                    pool.indirect_dma_start(got[k][:, j, :], None, g.table_dram[:, :],
                                            bass.IndirectOffsetOnAxis(ap=idx[k][:, j:j + 1], axis=0)).then_inc(s_got[k], 16)

            run_steps(pool, NG, 0, step)

        @block.tensor
        def _(pe):
            passes, one, many = g.controls(pe)
            nc.tensor.matmul(window, g.zero16[0:1, 0:P], g.zero16[0:1, 0:F], start=True, stop=True).then_inc(s_pass, 1)
            if weigh:
                nc.tensor.matmul(rates, g.zero16[0:1, 0:P], g.zero16[0:1, 0:TG * 3 * R], start=True, stop=True).then_inc(s_rate, 1)

            def step(s):
                if weigh and s.live(0, NG):
                    k = s.slot(2, 0)
                    need(pe, s_rows[s.slot(4, 0)], s.use(4, 0) * 16 + 16)
                    if s.c > 0:
                        pe.wait_ge(s_hot, s.at(0) * passes)
                    nc.tensor.matmul(bank_r[:, :], g.coef[0:2, :], rows[s.slot(4, 0)][0:2, :], start=True, stop=True).then_inc(s_dst, 1)
                    need(pe, s_step, s.at(0) * 4)
                    nc.tensor.matmul(rates, g.zero16[0:1, 0:P], g.zero16[0:1, 0:TG * 3 * R], start=True, stop=True)
                    with pe.Fori(0, passes) as w:
                        pe.wait_ge(s_hot, s.at(0) * passes + w + 1)
                        for j in range(TG):
                            ins = nc.tensor.matmul(rates[:, j * 3 * R:(j + 1) * 3 * R], to_edge[k][:, j, :], win[k][:, :],
                                                   start=False, stop=True, skip_group_check=True)
                        ins.then_inc(s_rate, 1)
                if s.live(1, NG):
                    k, ka = s.slot(2, 1), s.slot(NGA, 1)
                    need(pe, s_got[ka], s.use(NGA, 1) * (16 * TG) + 16 * TG)
                    apart(pe, g.gate["pe"])
                    with pe.Fori(0, passes) as w:
                        q = pe.snap(s.at(1) * passes + w)
                        pe.wait_ge(s_share, q + 1)
                        pe.wait_ge(s_sum, q * 2 + 3)
                        for j in range(TG):
                            ins = nc.tensor.matmul(window, share[k][:, j, :], got[ka][:, j, :], start=j == 0, stop=j == TG - 1)
                        ins.then_inc(s_pass, 1)

            run_steps(pe, NG, 1, step)

        @block.vector
        def _(dve):
            v = nc.vector
            passes, one, many = g.controls(dve)
            v.engine_nop().then_inc(s_sum, 1)
            rows_of_edges = g.srccol[:, :].bitcast(I32)

            def add_window(entry, q):
                dve.wait_ge(s_pass, q + 1)
                dve.wait_ge(s_sum, q * 2 + 1)
                b = dve.value_load(g.blk[0:1, bass.ds(entry, 1)], min_val=0, max_val=g.NBLK - 1)
                for mask, at in ((g.mask_hi, b), (g.mask_lo, b + 1)):
                    to = sums[:, bass.ds(at, 1), :].rearrange("p a f -> p (a f)")
                    v.scalar_tensor_tensor(to, window, mask[:, bass.ds(entry, 1)], to, ALU.mult, ALU.add).then_inc(s_sum, 1)

            def step(s):
                if s.live(0, NG):
                    v.tensor_copy(idx[s.slot(NGA, 0)][:, :], rows_of_edges[:, bass.ds(s.at(0) * TG, TG)]).then_inc(s_idx, 1)
                if weigh and s.live(1, NG):
                    k = s.slot(2, 1)
                    need(dve, s_dst, s.at(1) + 1)
                    apart(dve, g.gate["dve"])
                    with dve.Fori(0, passes) as w:
                        entry = g.entry(dve, s.at(1) * one + w)
                        dve.wait_ge(s_rate, passes_before(s, 1, w, one, many))
                        v.tensor_scalar(to_edge[k][:, :, :], bank_r[:, :].rearrange("q (p j) -> q j p", j=TG),
                                        g.nid_res[:, bass.ds(entry, 1)], None, ALU.is_equal)
                        b = dve.value_load(g.blk[0:1, bass.ds(entry + 1, 1)], min_val=0, max_val=g.NBLK - 1)
                        v.tensor_scalar(lower[k][:, :], g.rcnt3[:, bass.ds(b + 1, 1), :].rearrange("p a r -> p (a r)"),
                                        g.mask_lo[:, bass.ds(entry + 1, 1)], None, ALU.mult).then_inc(s_low, 1)
                        dve.wait_ge(s_low, s.at(1) * passes + w + 1)
                        v.scalar_tensor_tensor(win[k][:, :], g.rcnt3[:, bass.ds(b, 1), :].rearrange("p a r -> p (a r)"),
                                               g.mask_hi[:, bass.ds(entry + 1, 1)], lower[k][:, :], ALU.mult, ALU.add).then_inc(s_hot, 1)
                if s.live(2, NG):
                    k = s.slot(2, 2)
                    with dve.Fori(0, passes) as w:
                        entry = g.entry(dve, s.at(2) * one + w)
                        q = dve.snap(s.at(2) * passes + w)
                        dve.wait_ge(s_pass, passes_before(s, 2, w, one, many))
                        dve.wait_ge(s_nid[k], (s.use(2, 2) * passes + w) * 16 + 16)
                        for j in range(TG):
                            t = bass.ds(s.at(2) * TG + j, 1)
                            ins = v.tensor_scalar(share[k][:, j, :], nid_row[k][:, :], g.dstcol[:, t], g.etcol[:, t],
                                                  ALU.is_equal, ALU.mult)
                        ins.then_inc(s_share, 1)
                        add_window(entry, q)
                if weigh and s.live(1, NG):
                    four = bass.ds(s.at(1) * TG, TG)
                    v.tensor_tensor(types[:, :, :], g.etcol[:, four].unsqueeze(2).to_broadcast([P, TG, R]),
                                    g.iota_r[:, :].unsqueeze(1).to_broadcast([P, TG, R]), ALU.is_equal).then_inc(s_step, 1)
                    dve.wait_ge(s_rate, s.at(0) * passes + 1)
                    v.tensor_reduce(by_type[:, :, :], rates.rearrange("p (j t r) -> p j r t", j=TG, t=3), AX_X, ALU.add).then_inc(s_step, 1)
                    need(dve, s_step, s.at(1) * 4 + 2)
                    v.tensor_tensor(types[:, :, :], types[:, :, :], by_type[:, :, :], ALU.mult).then_inc(s_step, 1)
                    need(dve, s_step, s.at(1) * 4 + 3)
                    apart(dve, g.gate["dve"])
                    v.tensor_reduce(g.etcol[:, four], types[:, :, :], AX_X, ALU.add).then_inc(s_step, 1)
                    need(dve, s_step, s.at(1) * 4 + 4)

            run_steps(dve, NG, 2, step)
            add_window(g.entry(dve, (NG - 1) * one + passes, NG), passes * NG)


def store_nodes(nc, g, out):
    N, NBLK = g.N, g.NBLK
    with ExitStack() as ctx:
        s_out = nc.alloc_semaphore("s_out")
        block = ctx.enter_context(nc.Block())

        @block.sync
        def _(sp):
            cut = NBLK // 2
            for a, b in ((0, cut), (cut, NBLK - 1)):
                sp.dma_start(out[a * P:b * P, :].rearrange("(b p) f -> p b f", p=P), g.xs[:, a:b, :]).then_inc(s_out, 16)
            sp.dma_start(out[(NBLK - 1) * P:N, :], g.xs[0:N - (NBLK - 1) * P, NBLK - 1, :]).then_inc(s_out, 16)
            sp.wait_ge(s_out, 48)


def gnn_kernel(nc, x, src, dst, edge_attr, edge_type, W1, b1, W2, b2,
               basis1, comp1, root1, bias1, basis2, comp2, root2, bias2, out):
    with ExitStack() as ctx:
        g = Graph(nc, ctx, x.shape[0], edge_attr.shape[0])
        prepare(nc, g, x, src, dst, edge_type, W1, b1, W2, b2,
                (basis1, basis2), (comp1, comp2), (root1, root2), (bias1, bias2))
        filter_layer(nc, g, edge_attr)
        sum_layer(nc, g)
        hacc = ctx.enter_context(nc.sbuf_tensor("hacc", [P, g.NBX, F], F32))
        for which in range(2):
            make_table(nc, g, hacc, which)
            convolve(nc, g, hacc, which)
        store_nodes(nc, g, out)


_INS = ['x', 'src', 'dst', 'edge_attr_128', 'edge_type_8', 'L0_gnn_W1', 'L0_gnn_b1', 'L0_gnn_W2', 'L0_gnn_b2',
        'L1_gnn_basis1', 'L1_gnn_comp1', 'L1_gnn_root1', 'L1_gnn_bias1', 'L1_gnn_basis2', 'L1_gnn_comp2',
        'L1_gnn_root2', 'L1_gnn_bias2']


def kernel(**inputs):
    import numpy as _np
    import concourse.bacc as _bacc
    from concourse import mybir as _mybir
    from concourse.bass_utils import run_bass_kernel_spmd as _run

    nc = _bacc.Bacc("TRN2", target_bir_lowering=False, num_devices=1)
    arrays, args = {}, []
    for name in _INS:
        a = _np.ascontiguousarray(inputs[name])
        arrays[f"in_{name}"] = a
        args.append(nc.dram_tensor(f"in_{name}", a.shape, _mybir.dt.from_np(a.dtype), kind="ExternalInput").ap())
    out = nc.dram_tensor("out_x", inputs['x'].shape, _mybir.dt.float32, kind="ExternalOutput").ap()
    gnn_kernel(nc, *args, out)
    r = _run(nc, [arrays], core_ids=[0])
    return r.results[0]["out_x"]
```

```python
from contextlib import ExitStack, contextmanager

import numpy as np

import concourse.bass as bass
from concourse import mybir


ALU = mybir.AluOpType
ACT = mybir.ActivationFunctionType
F32 = mybir.dt.float32
BF16 = mybir.dt.bfloat16
I32 = mybir.dt.int32
AX_X = mybir.AxisListType.X

P = 128
F = 128
TG = 4
GE = TG * P
R = 8
NBASIS = 4
UNROLL = 4
PEEL = 8
LOG2 = float(np.float32(np.log(2.0)))
EPS = 1e-5
PAD_DST = 16383


class Step:

    def __init__(self, i, c):
        self.i, self.c = i, c

    def at(self, lag):
        return self.i * UNROLL + (self.c - lag)

    def use(self, slots, lag):
        return self.i * (UNROLL // slots) + (self.c - lag) // slots

    def slot(self, slots, lag):
        return (self.c - lag) % slots

    def live(self, lag, n):
        return not isinstance(self.i, int) or 0 <= self.c - lag < n


def run_steps(eng, n, tail, body):
    for c in range(PEEL):
        body(Step(0, c))
    with eng.Fori(0, (n - PEEL) // UNROLL) as i:
        for k in range(UNROLL):
            body(Step(i, PEEL + k))
    for c in range(n, n + tail):
        body(Step(0, c))


def need(eng, sem, value):
    if not isinstance(value, int) or value > 0:
        eng.wait_ge(sem, value)



def apart(eng, s_gate):
    eng.sem_inc(s_gate, 1)


class Chain:

    def __init__(self, eng, sem):
        self.eng, self.sem, self.n = eng, sem, 0

    def __call__(self, instruction):
        instruction.then_inc(self.sem, 1)
        self.n += 1
        self.eng.wait_ge(self.sem, self.n)


class Graph:

    def __init__(self, nc, ctx, N, E):
        self.nc = nc
        self.N, self.E = N, E
        self.NBLK = -(-N // P)
        self.NBX = self.NBLK + 1
        self.NG = -(-(-(-E // GE)) // UNROLL) * UNROLL
        self.NT = self.NG * TG
        self.QP = self.NG // 4
        self.EQ = 4 * GE
        self.ELAST = E - (self.NG - 1) * GE
        self.NROWS = self.NBLK * P
        self.TRASH = self.NROWS
        self.NACC = self.NROWS + 2 * P
        assert 0 < self.ELAST <= GE and self.ELAST % TG == 0 and self.QP <= P
        assert self.NG >= max(PEEL + 2 * UNROLL, self.NBLK) and self.NBLK % 2 == 0 and self.NBX % 3 == 0
        assert self.NROWS + P < PAD_DST

        self.acc_dram = [nc.dram_tensor(f"acc_dram{j}", [self.NACC, F], F32).ap() for j in range(TG)]
        self.split_dram = nc.dram_tensor("split_dram", [self.NBX * P, 3 * F], BF16).ap()
        self.rows_dram = nc.dram_tensor("rows_dram", [self.NG, 2, 2, GE], BF16).ap()
        self.span_dram = nc.dram_tensor("span_dram", [2, self.NG], F32).ap()
        self.table_dram = nc.dram_tensor("table_dram", [self.NROWS * R, F], F32).ap()

        self.bank = [ctx.enter_context(nc.psum_tensor(f"bank{k}", [P, 512], F32)) for k in range(8)]

        def sb(name, shape, dt=F32):
            return ctx.enter_context(nc.sbuf_tensor(name, shape, dt))

        self.gate = {name: nc.alloc_semaphore(f"gate_{name}") for name in ("pe", "dve", "pool")}
        NBX, NT, NG = self.NBX, self.NT, self.NG
        self.xs = sb("xs", [P, NBX, F])
        self.rstd = sb("rstd", [P, NBX])
        self.shift = sb("shift", [P, NBX])
        self.cnt = sb("cnt", [P, NBX, R])
        self.rcnt3 = sb("rcnt3", [P, NBX, 3 * R], BF16)
        self.dstcol = sb("dstcol", [P, NT])
        self.local16 = sb("local16", [P, NT], BF16)
        self.srccol = sb("srccol", [P, NT])
        self.etcol = sb("etcol", [P, NT])
        self.base = sb("base", [P, NG], I32)
        self.base_f = sb("base_f", [P, NG])
        self.blk = sb("blk", [P, NG], I32)
        self.mask_hi = sb("mask_hi", [P, NG])
        self.mask_lo = sb("mask_lo", [P, NG])
        self.neg_nid = sb("neg_nid", [P, NG])
        self.nid_res = sb("nid_res", [P, NG])
        self.ctl = sb("ctl", [P, 1], I32)
        self.ident = sb("ident", [P, P])
        self.part = sb("part", [P, 1])
        self.iota_r = sb("iota_r", [P, R])
        self.iota_c = sb("iota_c", [P, P, TG], BF16)
        self.eps = sb("eps", [P, 1])
        self.coef = sb("coef", [2, P], BF16)
        self.zero16 = sb("zero16", [1, 512], BF16)
        self.ones3 = sb("ones3", [P, P], BF16)
        self.bias3 = sb("bias3", [P, 512], BF16)
        self.pow2 = sb("pow2", [P, 1])
        self.dup_above = sb("dup_above", [P, 1])
        self.trash_row = sb("trash_row", [P, 1])
        self.w1 = sb("w1", [F, F])
        self.w2 = sb("w2", [F, F])
        self.b1c = sb("b1c", [F, 1])
        self.wrel = [sb(f"wrel{k}", [F, R * F]) for k in range(2)]
        self.wroot = [sb(f"wroot{k}", [F, F]) for k in range(2)]
        self.biasb = [sb(f"biasb{k}", [P, F]) for k in range(2)]


class Windows:

    def __init__(self, g, own):
        self.g, self.own = g, own

    @contextmanager
    def passes(self, eng):
        if self.own:
            yield 0
        else:
            with eng.Fori(0, self.g.NBLK) as w:
                yield w

    def entry(self, group, w):
        return group if self.own else w

    def number(self, group, w=0):
        return group if self.own else group * self.g.NBLK + w


def for_windows(eng, g, program):
    own = eng.value_load(g.ctl[0:1, 0:1], min_val=0, max_val=1)
    with eng.If(own):
        program(Windows(g, True))
    with eng.Else():
        program(Windows(g, False))


def add_window(nc, dve, g, sums, window, s_pass, s_sum, entry, number):
    b = dve.value_load(g.blk[0:1, bass.ds(entry, 1)], min_val=0, max_val=g.NBLK - 1)
    dve.wait_ge(s_pass, number + 1)
    need(dve, s_sum, number * 2)
    for mask, at in ((g.mask_hi, b), (g.mask_lo, b + 1)):
        to = sums[:, bass.ds(at, 1), :].rearrange("p a r -> p (a r)")
        nc.vector.scalar_tensor_tensor(to, window, mask[:, bass.ds(entry, 1)], to, ALU.mult, ALU.add).then_inc(s_sum, 1)


def norm_stats(nc, chain, g, bn, tmp):
    mean_e, sq_e, mean_o, sq_o = (bn[:, :, k] for k in (1, 2, 4, 5))
    chain(nc.vector.tensor_tensor(tmp[:, :], mean_e, mean_o, ALU.subtract))
    chain(nc.vector.tensor_tensor(tmp[:, :], tmp[:, :], tmp[:, :], ALU.mult))
    chain(nc.vector.tensor_scalar(tmp[:, :], tmp[:, :], 0.25, None, ALU.mult))
    chain(nc.vector.tensor_tensor(g.rstd[:, :], sq_e, sq_o, ALU.add))
    chain(nc.vector.scalar_tensor_tensor(g.rstd[:, :], g.rstd[:, :], 1.0 / F, tmp[:, :], ALU.mult, ALU.add))
    chain(nc.vector.tensor_tensor(g.shift[:, :], mean_e, mean_o, ALU.add))


def norm_scale(nc, chain, g):
    chain(nc.vector.reciprocal(g.rstd[:, :], g.rstd[:, :]))
    chain(nc.vector.scalar_tensor_tensor(g.shift[:, :], g.shift[:, :], -0.5, g.rstd[:, :], ALU.mult, ALU.mult))


def prepare(nc, g, x, src, dst, edge_type, W1, b1, W2, b2, basis, comp, root, bias):
    N, E, NG, NBLK, NBX, QP, EQ = g.N, g.E, g.NG, g.NBLK, g.NBX, g.QP, g.EQ
    CB = 3
    NCH = NBX // CB
    ZR = max(d for d in range(1, 11) if (NBLK + 2) % d == 0)
    with ExitStack() as ctx:
        def sb(name, shape, dt=F32):
            return ctx.enter_context(nc.sbuf_tensor(name, shape, dt))

        def sem(name):
            return nc.alloc_semaphore(name)

        ids = [sb(f"ids{k}", [QP, EQ], I32) for k in range(2)]
        idt = sb("idt", [QP, EQ], I32)
        idf = sb("idf", [QP, EQ])
        parts = [sb(f"parts{k}", [QP, 2, EQ], BF16) for k in range(2)]
        span = sb("span", [QP, 2, 4])
        span_b = sb("span_b", [P, 2, NG])
        first = sb("first", [P, NG])
        first_i = sb("first_i", [P, NG], I32)
        off_f = sb("off_f", [P, NG])
        blk_f = sb("blk_f", [P, NG])
        off_i = sb("off_i", [P, NG], I32)
        widest = sb("widest", [P, 1])
        fits = sb("fits", [P, 1])
        part_i = sb("part_i", [P, 1], I32)
        iota_i = sb("iota_i", [P, R], I32)
        pow2_i = sb("pow2_i", [P, 1], I32)
        iota_ci = sb("iota_ci", [P, P, TG], I32)
        dst_hi = sb("dst_hi", [P, g.NT], I32)
        dst_hf = sb("dst_hf", [P, g.NT])
        zeros = sb("zeros", [P, ZR * F])
        neglog = sb("neglog", [P, P])
        b2b = sb("b2b", [P, F])
        bsum = sb("bsum", [P, F])
        bpart = [sb(f"bpart{k}", [P, F], BF16) for k in range(3)]
        basis_sb = [sb(f"basis_sb{k}", [F, NBASIS, F]) for k in range(2)]
        comp_sb = [sb(f"comp_sb{k}", [P, R * NBASIS]) for k in range(2)]
        bn = sb("bn", [P, NBX, 6])
        bn_tmp = sb("bn_tmp", [P, NBX])
        h = [sb(f"h{k}", [P, CB, F]) for k in range(2)]
        rest = [sb(f"rest{k}", [P, CB, F]) for k in range(2)]
        split = [sb(f"split{k}", [P, CB, 3, F], BF16) for k in range(2)]

        s_pads = sem("p_pads")
        s_x = sem("p_x")
        s_ids = [sem(f"p_ids{k}") for k in range(2)]
        s_cols = sem("p_cols")
        s_weights = sem("p_weights")
        s_iota = sem("p_iota")
        s_chain = sem("p_chain")
        s_parts = sem("p_parts")
        s_rows = sem("p_rows")
        s_span = sem("p_span")
        s_span_out = sem("p_span_out")
        s_span_in = sem("p_span_in")
        s_zero = sem("p_zero")
        s_cleared = sem("p_cleared")
        s_neglog = sem("p_neglog")
        s_bsum = sem("p_bsum")
        s_bn = sem("p_bn")
        s_var = sem("p_var")
        s_std = sem("p_std")
        s_scale = sem("p_scale")
        s_h = sem("p_h")
        s_part1 = sem("p_part1")
        s_rest1 = sem("p_rest1")
        s_part2 = sem("p_part2")
        s_part3 = sem("p_part3")
        s_split_out = [sem(f"p_split_out{k}") for k in range(2)]

        x_main = x[0:(NBLK - 1) * P, :].rearrange("(b p) f -> p b f", p=P)
        x_rest = N - (NBLK - 1) * P

        block = ctx.enter_context(nc.Block())

        @block.sync
        def _(sp):
            sp.wait_ge(s_pads, 6)
            for k, ap in enumerate((dst, src)):
                sp.dma_start(ids[k][0:QP - 1, :], ap[0:(QP - 1) * EQ].rearrange("(q e) -> q e", e=EQ)).then_inc(s_ids[k], 16)
                sp.dma_start(ids[k][QP - 1:QP, 0:E - (QP - 1) * EQ],
                             ap[(QP - 1) * EQ:E].rearrange("(a e) -> a e", a=1)).then_inc(s_ids[k], 16)
            sp.dma_start(g.xs[:, 0:NBLK - 1, :], x_main).then_inc(s_x, 16)
            sp.dma_start(g.xs[0:x_rest, NBLK - 1, :], x[(NBLK - 1) * P:N, :]).then_inc(s_x, 16)
            for k in range(2):
                sp.wait_ge(s_parts, k + 1)
                for half in range(2):
                    for s in range(4):
                        sp.dma_start(g.rows_dram[:, half, k, :].rearrange("(q s) e -> q s e", s=4)[:, s, :],
                                     parts[k][:, half, s * GE:(s + 1) * GE]).then_inc(s_rows, 16)
            sp.wait_ge(s_span, 2)
            for k in range(2):
                sp.dma_start(g.span_dram[k, :].rearrange("(q s) -> q s", s=4), span[:, k, :]).then_inc(s_span_out, 16)
            sp.wait_ge(s_span_out, 32)
            sp.dma_start(span_b[:, :, :], g.span_dram.partition_broadcast(P)).then_inc(s_span_in, 16)
            sp.wait_ge(s_rows, 16 * 16)

        @block.gpsimd
        def _(pool):
            nc.gpsimd.memset(g.ident[:, :], 0.0).then_inc(s_iota, 1)
            pool.wait_ge(s_iota, 1)
            nc.gpsimd.affine_select(out=g.ident[:, :], in_=g.ident[:, :], compare_op=ALU.not_equal, fill=1.0,
                                    base=0, pattern=[[-1, P]], channel_multiplier=1).then_inc(s_iota, 1)
            nc.gpsimd.iota(part_i[:, :], [[0, 1]], base=0, channel_multiplier=1).then_inc(s_iota, 1)
            nc.gpsimd.iota(iota_i[:, :], [[1, R]], base=0, channel_multiplier=0).then_inc(s_iota, 1)
            nc.gpsimd.iota(first_i[:, :], [[P, NG]], base=0, channel_multiplier=0).then_inc(s_iota, 1)
            nc.gpsimd.iota(iota_ci[:, :, :], [[1, P], [0, TG]], base=0, channel_multiplier=0).then_inc(s_iota, 1)

        @block.scalar
        def _(act):
            act.dma_start(g.w2[:, :], W2).then_inc(s_weights, 16)
            act.dma_start(b2b[:, :], b2.partition_broadcast(P)).then_inc(s_weights, 16)
            act.dma_start(g.w1[:, :], W1).then_inc(s_weights, 16)
            act.dma_start(g.b1c[:, :], b1.rearrange("(f a) -> f a", a=1)).then_inc(s_weights, 16)
            for k in range(2):
                act.dma_start(comp_sb[k][:, :], comp[k].rearrange("r b -> (r b)").partition_broadcast(P)).then_inc(s_weights, 16)
                act.dma_start(basis_sb[k][:, :, :], basis[k].rearrange("b i o -> i b o")).then_inc(s_weights, 16)
                act.dma_start(g.wroot[k][:, :], root[k]).then_inc(s_weights, 16)
                act.dma_start(g.biasb[k][:, :], bias[k].partition_broadcast(P)).then_inc(s_weights, 16)
            act.wait_ge(s_pads, 6)
            for ap, col in ((dst, g.dstcol), (src, g.srccol), (edge_type, g.etcol)):
                col_i = col[:, :].bitcast(I32).rearrange("p (g j) -> p g j", j=TG)
                act.dma_start(col_i[:, 0:NG - 1, :],
                              ap[0:(NG - 1) * GE].rearrange("(g p j) -> p g j", p=P, j=TG)).then_inc(s_cols, 16)
                act.dma_start(col_i[0:g.ELAST // TG, NG - 1, :],
                              ap[(NG - 1) * GE:E].rearrange("(p j) -> p j", j=TG)).then_inc(s_cols, 16)
            act.wait_ge(s_zero, 1)
            for k in range(TG):
                to = g.acc_dram[k].rearrange("(p a r) f -> p a (r f)", p=P, r=ZR)
                act.dma_start(to, zeros[:, :].unsqueeze(1).to_broadcast([P, g.NACC // P // ZR, ZR * F])).then_inc(s_cleared, 16)
            act.wait_ge(s_var, 1)
            nc.scalar.activation(g.rstd[:, :], g.rstd[:, :], ACT.Sqrt, bias=g.eps[:, 0:1]).then_inc(s_std, 1)
            act.wait_ge(s_scale, 1)

            def split_chunk(c, k):
                if not isinstance(c, int) or c >= 2:
                    act.wait_ge(s_part3, c - 1)
                for b in range(CB):
                    i = c * CB + b
                    nc.scalar.activation(h[k][:, b, :], g.xs[:, bass.ds(i, 1), :].rearrange("p a f -> p (a f)"), ACT.Relu,
                                         bias=g.shift[:, bass.ds(i, 1)], scale=g.rstd[:, bass.ds(i, 1)]).then_inc(s_h, 1)
                act.wait_ge(s_h, c * CB + CB)
                if not isinstance(c, int) or c >= 2:
                    act.wait_ge(s_split_out[k], half(c, k) * 16)
                nc.scalar.activation(split[k][:, :, 0, :], h[k][:, :, :], ACT.Copy).then_inc(s_part1, 1)
                act.wait_ge(s_rest1, c + 1)
                nc.scalar.activation(split[k][:, :, 1, :], rest[k][:, :, :], ACT.Copy).then_inc(s_part2, 1)

            def half(c, k):
                return c // 2 if isinstance(c, int) else c_half[0] + k // 2

            c_half = [0]
            for c in range(2):
                split_chunk(c, c)
            with act.Fori(1, NCH // 2) as i:
                for k in range(2):
                    c_half[0] = i
                    split_chunk(i * 2 + k, k)
            if NCH % 2:
                split_chunk(NCH - 1, 0)
            act.wait_ge(s_cleared, 16 * TG)

        @block.tensor
        def _(pe):
            pe.wait_ge(s_neglog, 1)
            pe.wait_ge(s_weights, 16 * 12)
            nc.tensor.matmul(g.bank[4][:, 0:F], neglog[:, :], g.w2[:, :], start=True, stop=True).then_inc(s_bsum, 1)

        @block.vector
        def _(dve):
            chain = Chain(dve, s_chain)
            v = nc.vector
            v.memset(g.xs[:, NBLK - 1:NBX, :], 0.0).then_inc(s_pads, 1)
            v.memset(ids[0][:, :], PAD_DST).then_inc(s_pads, 1)
            v.memset(ids[1][:, :], g.TRASH).then_inc(s_pads, 1)
            v.memset(g.dstcol[:, :].bitcast(I32)[:, (NG - 1) * TG:], PAD_DST).then_inc(s_pads, 1)
            v.memset(g.srccol[:, :].bitcast(I32)[:, (NG - 1) * TG:], g.TRASH).then_inc(s_pads, 1)
            v.memset(g.etcol[:, :].bitcast(I32)[:, (NG - 1) * TG:], R).then_inc(s_pads, 1)
            v.memset(zeros[:, :], 0.0).then_inc(s_zero, 1)
            v.memset(neglog[:, :], -LOG2).then_inc(s_neglog, 1)
            v.memset(g.eps[:, :], EPS)
            v.memset(g.cnt[:, :, :], 0.0)
            v.memset(g.zero16[:, :], 0.0)
            v.memset(g.ones3[:, :], 1.0)
            v.memset(g.bias3[:, :], 0.0)
            chain(v.memset(g.coef[0:2, :], 1.0))
            chain(v.memset(g.coef[0:1, :], float(P)))

            for k in range(2):
                dve.wait_ge(s_ids[k], 32)
                chain(v.tensor_scalar(idt[:, :], ids[k][:, :], 7, None, ALU.arith_shift_right))
                chain(v.tensor_copy(parts[k][:, 0, :], idt[:, :]))
                chain(v.tensor_scalar(idt[:, :], ids[k][:, :], P - 1, None, ALU.bitwise_and))
                v.tensor_copy(parts[k][:, 1, :], idt[:, :]).then_inc(s_parts, 1)
                if k == 0:
                    chain(v.tensor_copy(idf[:, :], ids[0][:, :]))
                    v.tensor_reduce(span[:, 0, :], idf[:, :].rearrange("q (s e) -> q s e", s=4), AX_X, ALU.min).then_inc(s_span, 1)
                    dve.wait_ge(s_span, 1)
                    chain(v.scalar_tensor_tensor(idf[:, :], idf[:, :], float(PAD_DST), idf[:, :], ALU.is_lt, ALU.mult))
                    v.tensor_reduce(span[:, 1, :], idf[:, :].rearrange("q (s e) -> q s e", s=4), AX_X, ALU.max).then_inc(s_span, 1)
                    dve.wait_ge(s_parts, 1)

            dve.wait_ge(s_x, 32)
            with dve.Fori(0, NCH) as i:
                for k in range(CB):
                    b = i * CB + k
                    v.bn_stats(bn[:, bass.ds(b, 1), :].rearrange("p a k -> p (a k)"),
                               g.xs[:, bass.ds(b, 1), :].rearrange("p a f -> p (a f)")).then_inc(s_bn, 1)
            dve.wait_ge(s_bn, NBX)
            norm_stats(nc, chain, g, bn, bn_tmp)
            v.engine_nop().then_inc(s_var, 1)
            dve.wait_ge(s_std, 1)
            norm_scale(nc, chain, g)
            v.engine_nop().then_inc(s_scale, 1)

            def split_chunk(c, k):
                dve.wait_ge(s_part1, c + 1)
                v.tensor_tensor(rest[k][:, :, :], h[k][:, :, :], split[k][:, :, 0, :], ALU.subtract).then_inc(s_rest1, 1)
                dve.wait_ge(s_part2, c + 1)
                v.tensor_tensor(split[k][:, :, 2, :], rest[k][:, :, :], split[k][:, :, 1, :], ALU.subtract).then_inc(s_part3, 1)

            with dve.Fori(0, NCH // 2) as i:
                for k in range(2):
                    split_chunk(i * 2 + k, k)
            if NCH % 2:
                split_chunk(NCH - 1, 0)

            dve.wait_ge(s_iota, 6)
            chain(v.tensor_copy(g.part[:, :], part_i[:, :]))
            chain(v.tensor_copy(g.iota_c[:, :, :], iota_ci[:, :, :]))
            chain(v.tensor_copy(g.iota_r[:, :], iota_i[:, :]))
            chain(v.tensor_copy(first[:, :], first_i[:, :]))
            chain(v.tensor_scalar(g.trash_row[:, :], g.part[:, :], float(g.TRASH + 1), None, ALU.add))
            chain(v.tensor_scalar(pow2_i[:, :], g.part[:, :], -float(1 << 23), 190.0 * (1 << 23), ALU.mult, ALU.add))
            chain(v.tensor_copy(g.pow2[:, :].bitcast(I32), pow2_i[:, :]))
            chain(v.tensor_scalar(g.dup_above[:, :], pow2_i[:, :].bitcast(F32), 2.5, None, ALU.mult))

            dve.wait_ge(s_span_in, 16)
            chain(v.tensor_tensor(off_f[:, :], span_b[:, 1, :], span_b[:, 0, :], ALU.subtract))
            chain(v.reduce_max(widest[:, :], off_f[:, :], AX_X))
            chain(v.tensor_scalar(fits[:, :], widest[:, :], float(P), None, ALU.is_lt))
            chain(v.tensor_tensor(g.base_f[:, :], span_b[:, 0, :], first[:, :], ALU.subtract))
            chain(v.scalar_tensor_tensor(g.base_f[:, :], g.base_f[:, :], fits[:, 0:1], first[:, :], ALU.mult, ALU.add))
            chain(v.tensor_copy(g.base[:, :], g.base_f[:, :]))
            chain(v.tensor_scalar(g.blk[:, :], g.base[:, :], 7, None, ALU.arith_shift_right))
            chain(v.tensor_scalar(off_i[:, :], g.base[:, :], P - 1, None, ALU.bitwise_and))
            chain(v.tensor_copy(blk_f[:, :], g.blk[:, :]))
            chain(v.tensor_copy(off_f[:, :], off_i[:, :]))
            chain(v.tensor_scalar(g.mask_hi[:, :], off_f[:, :], g.part[:, 0:1], None, ALU.is_le))
            chain(v.tensor_scalar(g.mask_lo[:, :], g.mask_hi[:, :], -1.0, 1.0, ALU.mult, ALU.add))
            chain(v.tensor_scalar(g.neg_nid[:, :], g.base_f[:, :], g.part[:, 0:1], -1.0, ALU.add, ALU.mult))
            chain(v.tensor_scalar(blk_f[:, :], blk_f[:, :], float(P), g.part[:, 0:1], ALU.mult, ALU.add))
            chain(v.scalar_tensor_tensor(g.nid_res[:, :], g.mask_lo[:, :], float(P), blk_f[:, :], ALU.mult, ALU.add))
            chain(v.tensor_copy(g.ctl[:, :], fits[:, :]))

            dve.wait_ge(s_cols, 96)
            chain(v.tensor_scalar(dst_hi[:, :], g.dstcol[:, :].bitcast(I32), 7, None, ALU.arith_shift_right))
            for col in (g.dstcol, g.srccol, g.etcol):
                chain(v.tensor_copy(col[:, :], col[:, :].bitcast(I32)))
            chain(v.tensor_copy(dst_hf[:, :], dst_hi[:, :]))
            chain(v.scalar_tensor_tensor(g.local16[:, :], dst_hf[:, :], -float(P), g.dstcol[:, :], ALU.mult, ALU.add))

            dve.wait_ge(s_bsum, 1)
            chain(v.tensor_tensor(bsum[:, :], g.bank[4][:, 0:F], b2b[:, :], ALU.add))
            for k in range(3):
                chain(v.tensor_copy(bpart[k][:, :], bsum[:, :]))
                chain(v.tensor_tensor(bsum[:, :], bsum[:, :], bpart[k][:, :], ALU.subtract))
                for j in range(TG):
                    chain(v.tensor_copy(g.bias3[32 * k:32 * k + 1, j * F:(j + 1) * F], bpart[k][32 * k:32 * k + 1, :]))

            for k in range(2):
                for r in range(R):
                    w = g.wrel[k][:, r * F:(r + 1) * F]
                    chain(v.tensor_scalar(w, basis_sb[k][:, 0, :], comp_sb[k][:, r * NBASIS:r * NBASIS + 1], None, ALU.mult))
                    for b in range(1, NBASIS):
                        c = r * NBASIS + b
                        chain(v.scalar_tensor_tensor(w, basis_sb[k][:, b, :], comp_sb[k][:, c:c + 1], w, ALU.mult, ALU.add))

        @block.gpsimd
        def _(pool):
            to = g.split_dram.rearrange("(c b p) f -> c p b f", b=CB, p=P)
            with pool.Fori(0, NCH // 2) as i:
                for k in range(2):
                    pool.wait_ge(s_part3, i * 2 + k + 1)
                    pool.dma_start(to[bass.ds(i * 2 + k, 1)].rearrange("a p b f -> p (a b) f"),
                                   split[k][:, :, :, :].rearrange("p b k f -> p b (k f)")).then_inc(s_split_out[k], 16)
            if NCH % 2:
                pool.wait_ge(s_part3, NCH)
                pool.dma_start(to[NCH - 1], split[0][:, :, :, :].rearrange("p b k f -> p b (k f)")).then_inc(s_split_out[0], 16)
            pool.wait_ge(s_split_out[0], 16 * (NCH - NCH // 2))
            pool.wait_ge(s_split_out[1], 16 * (NCH // 2))


def filter_layer(nc, g, edge_attr):
    N, E, NG = g.N, g.E, g.NG
    NE = 4
    HALF = TG // 2
    with ExitStack() as ctx:
        def sb(name, shape, dt=F32):
            return ctx.enter_context(nc.sbuf_tensor(name, shape, dt))

        def sem(name):
            return nc.alloc_semaphore(name)

        edges = [sb(f"edges{k}", [P, TG, F]) for k in range(NE)]
        rows = [sb(f"rows{k}", [2, 2, GE], BF16) for k in range(NE)]
        win = [sb(f"win{k}", [P, 3 * F], BF16) for k in range(NE)]
        edges_t = [sb(f"edges_t{k}", [F, GE]) for k in range(2)]
        log1p = [sb(f"log1p{k}", [F, GE]) for k in range(2)]
        soft = [sb(f"soft{k}", [F, GE]) for k in range(2)]
        factor = [sb(f"factor{k}", [P, GE]) for k in range(2)]
        same = [sb(f"same{k}", [P, TG, P]) for k in range(2)]
        msg = [sb(f"msg{k}", [P, TG, F + 1]) for k in range(2)]
        total = [sb(f"total{k}", [P, TG, F + 1]) for k in range(2)]
        apart_by = [sb(f"apart_by{k}", [P, GE], BF16) for k in range(2)]
        to_edge = [sb(f"to_edge{k}", [P, P, TG], BF16) for k in range(2)]
        to_node = [sb(f"to_node{k}", [P, P, TG], BF16) for k in range(2)]
        types = [sb(f"types{k}", [P, TG, R], BF16) for k in range(2)]
        local = sb("local", [P, TG], BF16)
        dup = sb("dup", [P, TG])
        idx = [sb(f"idx{k}", [P, TG], I32) for k in range(2)]

        bank_t, bank_z, bank_e, bank_r, bank_h = g.bank[0:5]
        bank_c, bank_s = g.bank[5:7], g.bank[7]
        counts = bank_s[:, 0:R]

        s_edges = [sem(f"f_edges{k}") for k in range(NE)]
        s_rows = [sem(f"f_rows{k}") for k in range(NE)]
        s_win = [sem(f"f_win{k}") for k in range(NE)]
        s_const = sem("f_const")
        s_tr = sem("f_tr")
        s_trc = sem("f_trc")
        s_z = sem("f_z")
        s_abs = sem("f_abs")
        s_line = sem("f_line")
        s_exp = sem("f_exp")
        s_ln = sem("f_ln")
        s_soft = sem("f_soft")
        s_e = sem("f_e")
        s_ec = sem("f_ec")
        s_src = sem("f_src")
        s_same = sem("f_same")
        s_dst = sem("f_dst")
        s_apart = sem("f_apart")
        s_hot = sem("f_hot")
        s_local = sem("f_local")
        s_node = sem("f_node")
        s_h = sem("f_h")
        s_pass = sem("f_pass")
        s_cnt = sem("f_cnt")
        s_msg = sem("f_msg")
        s_total = sem("f_total")
        s_totc = sem("f_totc")
        s_dup = sem("f_dup")
        s_idx = sem("f_idx")
        s_sc = [sem(f"f_sc{j}") for j in range(TG)]

        block = ctx.enter_context(nc.Block())

        @block.sync
        def _(sp):
            def program(windows):
                def step(s):
                    if s.live(0, NG):
                        k = s.slot(NE, 0)
                        need(sp, s_tr, s.at(NE - 1))
                        if isinstance(s.i, int) and s.c == NG - 1 and g.ELAST < GE:
                            sp.dma_start(edges[k][0:g.ELAST // TG, :, :],
                                         edge_attr[(NG - 1) * GE:E, :].rearrange("(p j) f -> p j f", j=TG)).then_inc(s_edges[k], 16)
                        else:
                            sp.dma_start(edges[k][:, :, :],
                                         edge_attr[bass.ds(s.at(0) * GE, GE), :].rearrange("(p j) f -> p j f", j=TG)).then_inc(s_edges[k], 16)
                        need(sp, s_dst, s.at(NE - 1))
                        sp.dma_start(rows[k][:, :, :],
                                     g.rows_dram[bass.ds(s.at(0), 1)].rearrange("a h d e -> (a h) d e")).then_inc(s_rows[k], 16)
                    if s.live(2, NG):
                        k = s.slot(NE, 2)
                        with windows.passes(sp) as w:
                            if windows.own:
                                need(sp, s_pass, s.at(NE + 1))
                            else:
                                sp.wait_ge(s_hot, windows.number(s.at(2), w) + 1)
                            first = sp.value_load(g.base[0:1, bass.ds(windows.entry(s.at(2), w), 1)], min_val=0, max_val=g.NROWS)
                            sp.dma_start(win[k][:, :], g.split_dram[bass.ds(first, P), :]).then_inc(s_win[k], 16)

                run_steps(sp, NG - UNROLL, UNROLL + 4, step)

            for_windows(sp, g, program)

        @block.tensor
        def _(pe):
            def program(windows):
                def step(s):
                    if s.live(0, NG):
                        need(pe, s_edges[s.slot(NE, 0)], s.use(NE, 0) * 16 + 16)
                        need(pe, s_trc, s.at(0))
                        for j in range(TG):
                            ins = nc.tensor.transpose(bank_t[:, j * P:(j + 1) * P], edges[s.slot(NE, 0)][:, j, :], g.ident[:, :])
                        ins.then_inc(s_tr, 1)
                    if s.live(2, NG):
                        need(pe, s_rows[s.slot(NE, 2)], s.use(NE, 2) * 16 + 16)
                        if windows.own:
                            need(pe, s_apart, s.at(2))
                        elif s.c > 2:
                            pe.wait_ge(s_hot, windows.number(s.at(2)))
                        nc.tensor.matmul(bank_r[:, :], g.coef[0:2, :], rows[s.slot(NE, 2)][0:2, 1, :],
                                         start=True, stop=True).then_inc(s_src, 1)
                    if s.live(1, NG):
                        need(pe, s_trc, s.at(1) + 1)
                        need(pe, s_line, s.at(1))
                        nc.tensor.matmul(bank_z[:, :], g.w1[:, :], edges_t[s.slot(2, 1)][:, :],
                                         start=True, stop=True).then_inc(s_z, 1)
                    if s.live(3, NG):
                        k = s.slot(2, 3)
                        need(pe, s_same, s.at(3) + 1)
                        need(pe, s_msg, s.at(3) + 1)
                        need(pe, s_totc, s.at(3))
                        for j in range(TG):
                            ins = nc.tensor.matmul(bank_c[j // HALF][:, j % HALF * (F + 1):(j % HALF + 1) * (F + 1)],
                                                   same[k][:, j, :], msg[k][:, j, :], start=True, stop=True)
                        ins.then_inc(s_total, 1)
                    if s.live(2, NG):
                        k = s.slot(2, 2)
                        pe.wait_ge(s_same, s.at(2) + 1)
                        nc.tensor.matmul(bank_r[:, :], g.coef[0:2, :], rows[s.slot(NE, 2)][0:2, 0, :],
                                         start=True, stop=True).then_inc(s_dst, 1)
                        need(pe, s_soft, s.at(2) + 1)
                        need(pe, s_ec, s.at(2))
                        nc.tensor.matmul(bank_e[:, :], g.ones3[0:96, :], g.bias3[0:96, :], start=True, stop=True)
                        for j in range(TG):
                            ins = nc.tensor.matmul(bank_e[:, j * F:(j + 1) * F], soft[k][:, j * P:(j + 1) * P], g.w2[:, :],
                                                   start=False, stop=True, skip_group_check=True)
                        ins.then_inc(s_e, 1)
                        need(pe, s_msg, s.at(2))
                        if not windows.own:
                            nc.tensor.matmul(bank_h[:, :], g.zero16[0:1, 0:P], g.zero16[0:1, :], start=True, stop=True)
                        with windows.passes(pe) as w:
                            q = windows.number(s.at(2), w)
                            pe.wait_ge(s_hot, q + 1)
                            pe.wait_ge(s_win[s.slot(NE, 2)], windows.number(s.use(NE, 2), w) * 16 + 16)
                            for j in range(TG):
                                for part in range(3):
                                    ins = nc.tensor.matmul(bank_h[:, j * F:(j + 1) * F], to_edge[k][:, :, j],
                                                           win[s.slot(NE, 2)][:, part * F:(part + 1) * F],
                                                           start=windows.own and part == 0, stop=part == 2 or not windows.own,
                                                           skip_group_check=not windows.own)
                            ins.then_inc(s_h, 1)
                            pe.wait_ge(s_node, q + 1)
                            if windows.own:
                                need(pe, s_cnt, q * 2)
                            for j in range(TG):
                                ins = nc.tensor.matmul(counts, to_node[k][:, :, j], types[k][:, j, :], start=j == 0, stop=j == TG - 1)
                            ins.then_inc(s_pass, 1)

                run_steps(pe, NG, 4, step)

            pe.wait_ge(s_const, 1)
            for_windows(pe, g, program)

        @block.scalar
        def _(act):
            def program(windows):
                def step(s):
                    if s.live(0, NG):
                        need(act, s_tr, s.at(0) + 1)
                        need(act, s_z, s.at(1))
                        nc.scalar.activation(edges_t[s.slot(2, 0)][:, :], bank_t[:, :], ACT.Copy).then_inc(s_trc, 1)
                    if s.live(1, NG):
                        t = log1p[s.slot(2, 1)]
                        need(act, s_z, s.at(1) + 1)
                        need(act, s_soft, s.at(2))
                        nc.scalar.activation(t[:, :], bank_z[:, :], ACT.Abs, bias=g.b1c[:, 0:1]).then_inc(s_abs, 1)
                        need(act, s_abs, s.at(1) + 1)
                        nc.scalar.activation(t[:, :], t[:, :], ACT.Exp, scale=-1.0).then_inc(s_exp, 1)
                    if s.live(2, NG) and windows.own:
                        need(act, s_dst, s.at(2) + 1)
                        need(act, s_hot, s.at(3))
                        nc.scalar.activation(apart_by[s.slot(2, 2)][:, :], bank_r[:, :], ACT.Identity,
                                             bias=g.neg_nid[:, bass.ds(s.at(2), 1)]).then_inc(s_apart, 1)
                    if s.live(1, NG):
                        need(act, s_exp, s.at(1) + 1)
                        nc.scalar.activation(t[:, :], t[:, :], ACT.Ln, bias=1.0).then_inc(s_ln, 1)
                    if s.live(3, NG):
                        need(act, s_total, s.at(3) + 1)
                        need(act, s_dup, s.at(4))
                        for j in range(TG):
                            need(act, s_sc[j], s.at(4) * 16)
                        for h in range(2):
                            ins = nc.scalar.activation(total[s.slot(2, 3)][:, h * HALF:(h + 1) * HALF, :].rearrange("p a b -> p (a b)"),
                                                       bank_c[h][:, 0:HALF * (F + 1)], ACT.Copy)
                        ins.then_inc(s_totc, 1)
                    if s.live(2, NG):
                        need(act, s_e, s.at(2) + 1)
                        need(act, s_msg, s.at(3))
                        nc.scalar.activation(factor[s.slot(2, 2)][:, :], bank_e[:, :], ACT.Copy).then_inc(s_ec, 1)

                run_steps(act, NG, 4, step)

            nc.scalar.preload_act_table_set("natural_log_exp_and_others")
            for_windows(act, g, program)

        @block.vector
        def _(dve):
            v = nc.vector
            for k in range(2):
                ins = v.tensor_copy(msg[k][:, :, F:F + 1], g.pow2[:, 0:1].unsqueeze(1).to_broadcast([P, TG, 1]))
            ins.then_inc(s_const, 1)

            def program(windows):
                def step(s):
                    if s.live(3, NG):
                        k = s.slot(2, 3)
                        need(dve, s_h, windows.number(s.at(2)))
                        need(dve, s_ec, s.at(3) + 1)
                        need(dve, s_total, s.at(4))
                        v.tensor_tensor(msg[k][:, :, 0:F], bank_h[:, :].rearrange("p (j f) -> p j f", j=TG),
                                        factor[k][:, :].rearrange("p (j f) -> p j f", j=TG), ALU.mult).then_inc(s_msg, 1)
                        if windows.own:
                            add_window(nc, dve, g, g.cnt, counts, s_pass, s_cnt, s.at(3), s.at(3))
                    if s.live(2, NG):
                        k = s.slot(2, 2)
                        four = bass.ds(s.at(2) * TG, TG)
                        need(dve, s_src, s.at(2) + 1)
                        need(dve, s_total, s.at(3))
                        v.tensor_tensor(same[k][:, :, :], bank_r[:, :].rearrange("q (p j) -> q j p", j=TG),
                                        g.srccol[:, four].unsqueeze(2).to_broadcast([P, TG, P]), ALU.is_equal).then_inc(s_same, 1)
                        if windows.own:
                            need(dve, s_pass, s.at(3))
                        v.tensor_tensor(types[k][:, :, :], g.etcol[:, four].unsqueeze(2).to_broadcast([P, TG, R]),
                                        g.iota_r[:, :].unsqueeze(1).to_broadcast([P, TG, R]), ALU.is_equal)
                        if windows.own:
                            v.tensor_tensor(to_node[k][:, :, :], g.iota_c[:, :, :],
                                            g.local16[:, four].unsqueeze(1).to_broadcast([P, P, TG]), ALU.is_equal).then_inc(s_node, 1)
                    if s.live(1, NG):
                        need(dve, s_abs, s.at(1) + 1)
                        need(dve, s_e, s.at(2))
                        v.tensor_scalar(soft[s.slot(2, 1)][:, :], bank_z[:, :], g.b1c[:, 0:1], 0.0, ALU.add, ALU.max).then_inc(s_line, 1)
                    if s.live(2, NG) and windows.own:
                        need(dve, s_apart, s.at(2) + 1)
                        v.tensor_scalar(to_edge[k][:, :, :].rearrange("p a b -> p (a b)"), apart_by[k][:, :], 0.0, None,
                                        ALU.is_equal).then_inc(s_hot, 1)
                    if s.live(3, NG):
                        need(dve, s_totc, s.at(3) + 1)
                        need(dve, s_idx, s.at(3))
                        v.tensor_scalar(dup[:, :].unsqueeze(2), total[s.slot(2, 3)][:, :, F:F + 1], g.dup_above[:, 0:1],
                                        g.trash_row[:, 0:1], ALU.is_gt, ALU.mult).then_inc(s_dup, 1)
                        need(dve, s_dup, s.at(3) + 1)
                        v.tensor_tensor(idx[s.slot(2, 3)][:, :], dup[:, :], g.srccol[:, bass.ds(s.at(3) * TG, TG)],
                                        ALU.max).then_inc(s_idx, 1)
                    if s.live(2, NG) and not windows.own:
                        dve.wait_ge(s_dst, s.at(2) + 1)
                        apart(dve, g.gate["dve"])
                        with windows.passes(dve) as w:
                            q = dve.snap(windows.number(s.at(2), w))
                            v.tensor_scalar(to_edge[k][:, :, :].rearrange("p a b -> p (a b)"), bank_r[:, :],
                                            g.neg_nid[:, bass.ds(w, 1)], 0.0, ALU.add, ALU.is_equal).then_inc(s_hot, 1)
                            v.tensor_scalar(local[:, :], g.dstcol[:, four], g.base_f[:, bass.ds(w, 1)], None,
                                            ALU.subtract).then_inc(s_local, 1)
                            dve.wait_ge(s_local, q + 1)
                            v.tensor_tensor(to_node[k][:, :, :], g.iota_c[:, :, :],
                                            local[:, :].unsqueeze(1).to_broadcast([P, P, TG]), ALU.is_equal).then_inc(s_node, 1)
                            add_window(nc, dve, g, g.cnt, counts, s_pass, s_cnt, w, q)
                    if s.live(1, NG):
                        need(dve, s_ln, s.at(1) + 1)
                        need(dve, s_line, s.at(1) + 1)
                        v.tensor_tensor(soft[s.slot(2, 1)][:, :], soft[s.slot(2, 1)][:, :], log1p[s.slot(2, 1)][:, :],
                                        ALU.add).then_inc(s_soft, 1)

                run_steps(dve, NG, 4, step)
                if windows.own:
                    dve.wait_ge(s_cnt, 2 * NG)

            for_windows(dve, g, program)

        @block.gpsimd
        def _(pool):

            def step(s):
                k = s.slot(2, 0)
                need(pool, s_idx, s.at(0) + 1)
                need(pool, s_totc, s.at(0) + 1)
                for j in range(TG):
                    need(pool, s_sc[j], s.at(0) * 16)
                    apart(pool, g.gate["pool"])
                    pool.indirect_dma_start(g.acc_dram[j][:, :], bass.IndirectOffsetOnAxis(ap=idx[k][:, j:j + 1], axis=0),
                                            total[k][:, j, 0:F], None, compute_op=ALU.add).then_inc(s_sc[j], 16)

            run_steps(pool, NG, 0, step)
            for j in range(TG):
                pool.wait_ge(s_sc[j], NG * 16)


def sum_layer(nc, g):
    NBLK, NBX = g.NBLK, g.NBX
    with ExitStack() as ctx:
        def sb(name, shape, dt=F32):
            return ctx.enter_context(nc.sbuf_tensor(name, shape, dt))

        def sem(name):
            return nc.alloc_semaphore(name)

        SLOTS = 2
        sums = [sb(f"sums{k}", [P, TG, F]) for k in range(SLOTS)]
        added = [sb(f"added{k}", [P, F]) for k in range(SLOTS)]
        bn = sb("bn2", [P, NBX, 6])
        bn_tmp = sb("bn2_tmp", [P, NBX])
        rest = sb("rest2", [P, NBX, R])
        seg = sb("seg", [P, g.NT])
        s_sums = [sem(f"a_sums{k}") for k in range(SLOTS)]
        s_added = sem("a_added")
        s_x = sem("a_x")
        s_bn = sem("a_bn")
        s_var = sem("a_var")
        s_std = sem("a_std")
        s_chain = sem("a_chain")
        block = ctx.enter_context(nc.Block())

        @block.sync
        def _(sp):
            def load(b, k):
                for j in range(TG):
                    sp.dma_start(sums[k][:, j, :], g.acc_dram[j][bass.ds(b * P, P), :]).then_inc(s_sums[k], 16)

            for k in range(SLOTS):
                load(k, k)
            with sp.Fori(1, NBLK // SLOTS) as i:
                for k in range(SLOTS):
                    sp.wait_ge(s_added, i * SLOTS + k - 1)
                    load(i * SLOTS + k, k)

        @block.scalar
        def _(act):
            act.wait_ge(s_var, 1)
            nc.scalar.activation(g.rstd[:, :], g.rstd[:, :], ACT.Sqrt, bias=g.eps[:, 0:1]).then_inc(s_std, 1)

        @block.vector
        def _(dve):
            v = nc.vector
            chain = Chain(dve, s_chain)

            chain(v.tensor_scalar(seg[:, :], g.srccol[:, :], float(R), None, ALU.mult))
            chain(v.tensor_tensor(seg[:, :], seg[:, :], g.etcol[:, :], ALU.add))
            chain(v.tensor_scalar(g.srccol[:, :], seg[:, :], float(g.NROWS * R - 1), None, ALU.min))

            with dve.Fori(0, NBLK // SLOTS) as i:
                for k in range(SLOTS):
                    b = i * SLOTS + k
                    dve.wait_ge(s_sums[k], i * (16 * TG) + 16 * TG)
                    v.tensor_reduce(added[k][:, :], sums[k][:, :, :].rearrange("p j f -> p f j"), AX_X, ALU.add).then_inc(s_added, 1)
                    dve.wait_ge(s_added, b + 1)
                    to = g.xs[:, bass.ds(b, 1), :].rearrange("p a f -> p (a f)")
                    v.tensor_tensor(to, to, added[k][:, :], ALU.add).then_inc(s_x, 1)
                    dve.wait_ge(s_x, b + 1)
                    v.bn_stats(bn[:, bass.ds(b, 1), :].rearrange("p a k -> p (a k)"), to).then_inc(s_bn, 1)
            chain(v.memset(bn[:, NBLK:NBX, :], 0.0))
            dve.wait_ge(s_bn, NBLK)
            norm_stats(nc, chain, g, bn, bn_tmp)
            v.engine_nop().then_inc(s_var, 1)
            dve.wait_ge(s_std, 1)
            norm_scale(nc, chain, g)

            chain(v.tensor_scalar(g.cnt[:, :, :], g.cnt[:, :, :], 1.0, None, ALU.max))
            chain(v.reciprocal(g.cnt[:, :, :], g.cnt[:, :, :]))
            chain(v.tensor_copy(rest[:, :, :], g.cnt[:, :, :]))
            for k in range(3):
                part = g.rcnt3[:, :, k * R:(k + 1) * R]
                chain(v.tensor_copy(part, rest[:, :, :]))
                if k < 2:
                    chain(v.tensor_tensor(rest[:, :, :], rest[:, :, :], part, ALU.subtract))


def make_table(nc, g, hacc, which):
    NBLK = g.NBLK
    with ExitStack() as ctx:
        def sb(name, shape, dt=F32):
            return ctx.enter_context(nc.sbuf_tensor(f"{name}_{which}", shape, dt))

        def sem(name):
            return nc.alloc_semaphore(f"{name}_{which}")

        NST = 4
        h = [sb(f"th{k}", [P, F]) for k in range(2)]
        h_t = [sb(f"th_t{k}", [F, P]) for k in range(2)]
        made = [sb(f"made{k}", [P, R * F]) for k in range(NST)]
        own = [sb(f"own{k}", [P, F]) for k in range(2)]
        s_h = sem("t_h")
        s_tr = sem("t_tr")
        s_trc = sem("t_trc")
        s_mm = sem("t_mm")
        s_left = sem("t_left")
        s_right = sem("t_right")
        s_own = sem("t_own")
        s_sum = sem("t_sum")
        s_out = [sem(f"t_out{k}") for k in range(NST)]
        table = g.table_dram.rearrange("(b p r) f -> b p (r f)", p=P, r=R)
        wrel, wroot, biasb = g.wrel[which], g.wroot[which], g.biasb[which]
        block = ctx.enter_context(nc.Block())
        HALF = R * F // 2

        def blocks(eng, body):
            n = NBLK // UNROLL * UNROLL
            run_steps(eng, n, 0, body)
            for c in range(n, NBLK + 1):
                body(Step(0, c))

        def one(ap, at):
            return ap[:, bass.ds(at, 1), :].rearrange("p a f -> p (a f)")

        @block.scalar
        def _(act):
            def step(s):
                if s.live(0, NBLK):
                    k = s.slot(2, 0)
                    need(act, s_tr, s.at(1))
                    if which == 0:
                        nc.scalar.activation(h[k][:, :], one(g.xs, s.at(0)), ACT.Relu, bias=g.shift[:, bass.ds(s.at(0), 1)],
                                             scale=g.rstd[:, bass.ds(s.at(0), 1)]).then_inc(s_h, 1)
                    else:
                        nc.scalar.activation(h[k][:, :], one(hacc, s.at(0)), ACT.Relu).then_inc(s_h, 1)
                if s.live(1, NBLK):
                    need(act, s_mm, s.at(1) + 1)
                    need(act, s_out[s.slot(NST, 1)], s.use(NST, 1) * 16)
                    nc.scalar.activation(made[s.slot(NST, 1)][:, HALF:], g.bank[4 + s.slot(2, 1)][:, :], ACT.Copy).then_inc(s_right, 1)
                if s.live(0, NBLK):
                    need(act, s_tr, s.at(0) + 1)
                    need(act, s_mm, s.at(1))
                    nc.scalar.activation(h_t[k][:, :], g.bank[k][:, 0:P], ACT.Copy).then_inc(s_trc, 1)

            blocks(act, step)

        @block.tensor
        def _(pe):
            def step(s):
                if s.live(0, NBLK):
                    k = s.slot(2, 0)
                    need(pe, s_h, s.at(0) + 1)
                    need(pe, s_trc, s.at(1))
                    nc.tensor.transpose(g.bank[k][:, 0:P], h[k][:, :], g.ident[:, :]).then_inc(s_tr, 1)
                if s.live(1, NBLK):
                    k = s.slot(2, 1)
                    need(pe, s_trc, s.at(1) + 1)
                    need(pe, s_left, s.at(2))
                    need(pe, s_right, s.at(2))
                    need(pe, s_own, s.at(2))
                    nc.tensor.matmul(g.bank[2 + k][:, :], h_t[k][:, :], wrel[:, 0:HALF], start=True, stop=True)
                    nc.tensor.matmul(g.bank[4 + k][:, :], h_t[k][:, :], wrel[:, HALF:], start=True, stop=True)
                    nc.tensor.matmul(g.bank[6 + k][:, 0:F], h_t[k][:, :], wroot[:, :], start=True, stop=True).then_inc(s_mm, 1)

            blocks(pe, step)

        @block.vector
        def _(dve):
            v = nc.vector
            if which == 0:
                v.memset(hacc[:, NBLK:, :], 0.0)

            def step(s):
                if s.live(1, NBLK):
                    k = s.slot(2, 1)
                    need(dve, s_mm, s.at(1) + 1)
                    need(dve, s_out[s.slot(NST, 1)], s.use(NST, 1) * 16)
                    v.tensor_copy(made[s.slot(NST, 1)][:, 0:HALF], g.bank[2 + k][:, :]).then_inc(s_left, 1)
                    if which == 0:
                        v.tensor_tensor(one(hacc, s.at(1)), g.bank[6 + k][:, 0:F], biasb[:, :], ALU.add).then_inc(s_own, 1)
                    else:
                        need(dve, s_sum, s.at(2))
                        v.tensor_tensor(own[k][:, :], g.bank[6 + k][:, 0:F], biasb[:, :], ALU.add).then_inc(s_own, 1)
                        need(dve, s_own, s.at(1) + 1)
                        v.tensor_tensor(one(g.xs, s.at(1)), one(g.xs, s.at(1)), own[k][:, :], ALU.add).then_inc(s_sum, 1)

            blocks(dve, step)

        @block.sync
        def _(sp):
            def step(s):
                if s.live(1, NBLK):
                    k = s.slot(NST, 1)
                    need(sp, s_left, s.at(1) + 1)
                    need(sp, s_right, s.at(1) + 1)
                    sp.dma_start(table[bass.ds(s.at(1), 1)].rearrange("a p c -> (a p) c"), made[k][:, :]).then_inc(s_out[k], 16)

            blocks(sp, step)
            for k in range(NST):
                sp.wait_ge(s_out[k], 16 * len(range(k, NBLK, NST)))


def convolve(nc, g, hacc, which):
    NG = g.NG
    sums = hacc if which == 0 else g.xs
    weigh = which == 0
    NGA = 4
    with ExitStack() as ctx:
        def sb(name, shape, dt=F32):
            return ctx.enter_context(nc.sbuf_tensor(f"{name}_{which}", shape, dt))

        def sem(name):
            return nc.alloc_semaphore(f"{name}_{which}")

        idx = [sb(f"cidx{k}", [P, TG], I32) for k in range(NGA)]
        got = [sb(f"got{k}", [P, TG, F]) for k in range(NGA)]
        local = sb("clocal", [P, TG], BF16)
        to_node = [sb(f"cto_node{k}", [P, P, TG], BF16) for k in range(2)]
        share = [sb(f"share{k}", [P, TG, P]) for k in range(2)]
        if weigh:
            rows = [sb(f"crows{k}", [2, GE], BF16) for k in range(4)]
            to_edge = [sb(f"cto_edge{k}", [P, P, TG], BF16) for k in range(2)]
            lower = [sb(f"lower{k}", [P, 3 * R], BF16) for k in range(2)]
            win = [sb(f"cwin{k}", [P, 3 * R], BF16) for k in range(2)]
            types = sb("ctypes", [P, TG, R])
            by_type = sb("by_type", [P, TG, 3 * R])

        bank_r, bank_w = g.bank[0], g.bank[1]
        window = [g.bank[2 + k][:, 0:F] for k in range(2)]
        rates = bank_w[:, 0:TG * 3 * R]

        s_idx = sem("c_idx")
        s_got = [sem(f"c_got{k}") for k in range(NGA)]
        s_local = sem("c_local")
        s_node = sem("c_node")
        s_share = sem("c_share")
        s_pass = sem("c_pass")
        s_sum = sem("c_sum")
        s_rows = [sem(f"c_rows{k}") for k in range(4)]
        s_dst = sem("c_dst")
        s_low = sem("c_low")
        s_hot = sem("c_hot")
        s_rate = sem("c_rate")
        s_types = sem("c_types")
        s_by_type = sem("c_by_type")
        s_weight = sem("c_weight")
        block = ctx.enter_context(nc.Block())

        if weigh:
            @block.sync
            def _(sp):
                def step(s):
                    k = s.slot(4, 0)
                    need(sp, s_dst, s.at(3))
                    sp.dma_start(rows[k][:, :], g.rows_dram[bass.ds(s.at(0), 1), :, 0, :].rearrange("a h e -> (a h) e")).then_inc(s_rows[k], 16)

                run_steps(sp, NG, 0, step)

        @block.gpsimd
        def _(pool):
            def step(s):
                k = s.slot(NGA, 0)
                need(pool, s_idx, s.at(0) + 1)
                apart(pool, g.gate["pool"])
                for j in range(TG):
                    pool.indirect_dma_start(got[k][:, j, :], None, g.table_dram[:, :],
                                            bass.IndirectOffsetOnAxis(ap=idx[k][:, j:j + 1], axis=0)).then_inc(s_got[k], 16)

            run_steps(pool, NG, 0, step)

        @block.tensor
        def _(pe):
            def program(windows):
                def step(s):
                    if weigh and s.live(1, NG):
                        k = s.slot(2, 1)
                        need(pe, s_by_type, s.at(1))
                        if not windows.own:
                            nc.tensor.matmul(rates, g.zero16[0:1, 0:P], g.zero16[0:1, 0:TG * 3 * R], start=True, stop=True)
                        with windows.passes(pe) as w:
                            pe.wait_ge(s_hot, windows.number(s.at(1), w) + 1)
                            for j in range(TG):
                                ins = nc.tensor.matmul(rates[:, j * 3 * R:(j + 1) * 3 * R], to_edge[k][:, :, j], win[k][:, :],
                                                       start=windows.own, stop=True, skip_group_check=not windows.own)
                            ins.then_inc(s_rate, 1)
                    if weigh and s.live(0, NG):
                        need(pe, s_rows[s.slot(4, 0)], s.use(4, 0) * 16 + 16)
                        need(pe, s_hot, windows.number(s.at(0)))
                        nc.tensor.matmul(bank_r[:, :], g.coef[0:2, :], rows[s.slot(4, 0)][0:2, :], start=True, stop=True).then_inc(s_dst, 1)
                    if s.live(3, NG):
                        k, ka = s.slot(2, 3), s.slot(NGA, 3)
                        need(pe, s_got[ka], s.use(NGA, 3) * (16 * TG) + 16 * TG)
                        if windows.own:
                            need(pe, s_sum, s.at(4) * 2)
                        apart(pe, g.gate["pe"])
                        with windows.passes(pe) as w:
                            pe.wait_ge(s_share, windows.number(s.at(3), w) + 1)
                            for j in range(TG):
                                ins = nc.tensor.matmul(window[k], share[k][:, j, :], got[ka][:, j, :], start=j == 0, stop=j == TG - 1)
                            ins.then_inc(s_pass, 1)

                run_steps(pe, NG, 3, step)

            for_windows(pe, g, program)

        @block.scalar
        def _(act):
            def program(windows):
                share_lag = 2 if windows.own else 3

                def step(s):
                    if s.live(0, NG):
                        need(act, s_pass, windows.number(s.at(NGA - 1)))
                        nc.scalar.activation(idx[s.slot(NGA, 0)][:, :], g.srccol[:, bass.ds(s.at(0) * TG, TG)], ACT.Copy).then_inc(s_idx, 1)
                    if s.live(share_lag, NG):
                        k = s.slot(2, share_lag)
                        if weigh:
                            need(act, s_weight, s.at(share_lag) + 1)
                        if windows.own:
                            need(act, s_pass, s.at(share_lag + 1))
                        with windows.passes(act) as w:
                            act.wait_ge(s_node, windows.number(s.at(share_lag), w) + 1)
                            for j in range(TG):
                                ins = nc.scalar.activation(share[k][:, j, :], to_node[k][:, :, j], ACT.Copy,
                                                           scale=g.etcol[:, bass.ds(s.at(share_lag) * TG + j, 1)])
                            ins.then_inc(s_share, 1)

                run_steps(act, NG, 3, step)

            for_windows(act, g, program)

        @block.vector
        def _(dve):
            v = nc.vector

            def rate_window(windows, s, w):
                k = s.slot(2, 1)
                entry = windows.entry(s.at(1), w)
                b = dve.value_load(g.blk[0:1, bass.ds(entry, 1)], min_val=0, max_val=g.NBLK - 1)
                v.tensor_scalar(lower[k][:, :], g.rcnt3[:, bass.ds(b + 1, 1), :].rearrange("p a r -> p (a r)"),
                                g.mask_lo[:, bass.ds(entry, 1)], None, ALU.mult).then_inc(s_low, 1)
                v.tensor_scalar(to_edge[k][:, :, :].rearrange("p a b -> p (a b)"), bank_r[:, :],
                                g.nid_res[:, bass.ds(entry, 1)], None, ALU.is_equal)
                dve.wait_ge(s_low, windows.number(s.at(1), w) + 1)
                v.scalar_tensor_tensor(win[k][:, :], g.rcnt3[:, bass.ds(b, 1), :].rearrange("p a r -> p (a r)"),
                                       g.mask_hi[:, bass.ds(entry, 1)], lower[k][:, :], ALU.mult, ALU.add).then_inc(s_hot, 1)

            def program(windows):
                def step(s):
                    if weigh and s.live(2, NG):
                        four = bass.ds(s.at(2) * TG, TG)
                        v.tensor_tensor(types[:, :, :], g.etcol[:, four].unsqueeze(2).to_broadcast([P, TG, R]),
                                        g.iota_r[:, :].unsqueeze(1).to_broadcast([P, TG, R]), ALU.is_equal).then_inc(s_types, 1)
                        dve.wait_ge(s_rate, windows.number(s.at(1)))
                        need(dve, s_types, s.at(2) + 1)
                        for j in range(TG):
                            ins = v.tensor_tensor(by_type[:, j, :].rearrange("p (t r) -> p t r", t=3),
                                                  rates[:, j * 3 * R:(j + 1) * 3 * R].rearrange("p (t r) -> p t r", t=3),
                                                  types[:, j:j + 1, :].to_broadcast([P, 3, R]), ALU.mult)
                        ins.then_inc(s_by_type, 1)
                        need(dve, s_by_type, s.at(2) + 1)
                        apart(dve, g.gate["dve"])
                        v.tensor_reduce(g.etcol[:, four], by_type[:, :, :], AX_X, ALU.add).then_inc(s_weight, 1)
                    if weigh and s.live(1, NG):
                        need(dve, s_dst, s.at(1) + 1)
                        if windows.own:
                            need(dve, s_rate, s.at(2))
                            rate_window(windows, s, 0)
                        else:
                            apart(dve, g.gate["dve"])
                            with windows.passes(dve) as w:
                                rate_window(windows, s, w)
                                dve.wait_ge(s_rate, windows.number(s.at(1), w) + 1)
                    if s.live(2, NG) and windows.own:
                        need(dve, s_share, s.at(3))
                        v.tensor_tensor(to_node[s.slot(2, 2)][:, :, :], g.iota_c[:, :, :],
                                        g.local16[:, bass.ds(s.at(2) * TG, TG)].unsqueeze(1).to_broadcast([P, P, TG]),
                                        ALU.is_equal).then_inc(s_node, 1)
                    if s.live(4, NG) and windows.own:
                        add_window(nc, dve, g, sums, window[s.slot(2, 4)], s_pass, s_sum, s.at(4), s.at(4))
                    if s.live(3, NG) and not windows.own:
                        k = s.slot(2, 3)
                        with windows.passes(dve) as w:
                            q = dve.snap(windows.number(s.at(3), w))
                            v.tensor_scalar(local[:, :], g.dstcol[:, bass.ds(s.at(3) * TG, TG)], g.base_f[:, bass.ds(w, 1)], None,
                                            ALU.subtract).then_inc(s_local, 1)
                            dve.wait_ge(s_local, q + 1)
                            v.tensor_tensor(to_node[k][:, :, :], g.iota_c[:, :, :],
                                            local[:, :].unsqueeze(1).to_broadcast([P, P, TG]), ALU.is_equal).then_inc(s_node, 1)
                            add_window(nc, dve, g, sums, window[k], s_pass, s_sum, w, q)

                run_steps(dve, NG, 4, step)

            for_windows(dve, g, program)


def store_nodes(nc, g, out):
    N, NBLK = g.N, g.NBLK
    with ExitStack() as ctx:
        s_out = nc.alloc_semaphore("s_out")
        block = ctx.enter_context(nc.Block())

        @block.sync
        def _(sp):
            cut = NBLK // 2
            for a, b in ((0, cut), (cut, NBLK - 1)):
                sp.dma_start(out[a * P:b * P, :].rearrange("(b p) f -> p b f", p=P), g.xs[:, a:b, :]).then_inc(s_out, 16)
            sp.dma_start(out[(NBLK - 1) * P:N, :], g.xs[0:N - (NBLK - 1) * P, NBLK - 1, :]).then_inc(s_out, 16)
            sp.wait_ge(s_out, 48)


def gnn_kernel(nc, x, src, dst, edge_attr, edge_type, W1, b1, W2, b2,
               basis1, comp1, root1, bias1, basis2, comp2, root2, bias2, out):
    with ExitStack() as ctx:
        g = Graph(nc, ctx, x.shape[0], edge_attr.shape[0])
        prepare(nc, g, x, src, dst, edge_type, W1, b1, W2, b2,
                (basis1, basis2), (comp1, comp2), (root1, root2), (bias1, bias2))
        filter_layer(nc, g, edge_attr)
        sum_layer(nc, g)
        hacc = ctx.enter_context(nc.sbuf_tensor("hacc", [P, g.NBX, F], F32))
        for which in range(2):
            make_table(nc, g, hacc, which)
            convolve(nc, g, hacc, which)
        store_nodes(nc, g, out)


_INS = ['x', 'src', 'dst', 'edge_attr_128', 'edge_type_8', 'L0_gnn_W1', 'L0_gnn_b1', 'L0_gnn_W2', 'L0_gnn_b2',
        'L1_gnn_basis1', 'L1_gnn_comp1', 'L1_gnn_root1', 'L1_gnn_bias1', 'L1_gnn_basis2', 'L1_gnn_comp2',
        'L1_gnn_root2', 'L1_gnn_bias2']


def kernel(**inputs):
    import numpy as _np
    import concourse.bacc as _bacc
    from concourse import mybir as _mybir
    from concourse.bass_utils import run_bass_kernel_spmd as _run

    nc = _bacc.Bacc("TRN2", target_bir_lowering=False, num_devices=1)
    arrays, args = {}, []
    for name in _INS:
        a = _np.ascontiguousarray(inputs[name])
        arrays[f"in_{name}"] = a
        args.append(nc.dram_tensor(f"in_{name}", a.shape, _mybir.dt.from_np(a.dtype), kind="ExternalInput").ap())
    out = nc.dram_tensor("out_x", inputs['x'].shape, _mybir.dt.float32, kind="ExternalOutput").ap()
    gnn_kernel(nc, *args, out)
    r = _run(nc, [arrays], core_ids=[0])
    return r.results[0]["out_x"]
```

```python
from contextlib import ExitStack, contextmanager

import numpy as np

import concourse.bass as bass
from concourse import mybir


ALU = mybir.AluOpType
ACT = mybir.ActivationFunctionType
F32 = mybir.dt.float32
BF16 = mybir.dt.bfloat16
I32 = mybir.dt.int32
AX_X = mybir.AxisListType.X

P = 128
F = 128
TG = 4
GE = TG * P
R = 8
NBASIS = 4
UNROLL = 4
PEEL = 8
LOG2 = float(np.float32(np.log(2.0)))
EPS = 1e-5
PAD_DST = 16383


class Step:

    def __init__(self, i, c):
        self.i, self.c = i, c

    def at(self, lag):
        return self.i * UNROLL + (self.c - lag)

    def use(self, slots, lag):
        return self.i * (UNROLL // slots) + (self.c - lag) // slots

    def slot(self, slots, lag):
        return (self.c - lag) % slots

    def live(self, lag, n):
        return not isinstance(self.i, int) or 0 <= self.c - lag < n


def run_steps(eng, n, tail, body):
    for c in range(PEEL):
        body(Step(0, c))
    with eng.Fori(0, (n - PEEL) // UNROLL) as i:
        for k in range(UNROLL):
            body(Step(i, PEEL + k))
    for c in range(n, n + tail):
        body(Step(0, c))


def need(eng, sem, value):
    if not isinstance(value, int) or value > 0:
        eng.wait_ge(sem, value)


def apart(eng, s_gate):
    eng.sem_inc(s_gate, 1)


class Chain:

    def __init__(self, eng, sem):
        self.eng, self.sem, self.n = eng, sem, 0

    def __call__(self, instruction):
        instruction.then_inc(self.sem, 1)
        self.n += 1
        self.eng.wait_ge(self.sem, self.n)


class Graph:

    def __init__(self, nc, ctx, N, E):
        self.N, self.E = N, E
        self.NBLK = -(-N // P)
        self.NBX = self.NBLK + 1
        self.NG = -(-(-(-E // GE)) // UNROLL) * UNROLL
        self.NT = self.NG * TG
        self.QP = self.NG // 4
        self.EQ = 4 * GE
        self.ELAST = E - (self.NG - 1) * GE
        self.NROWS = self.NBLK * P
        self.TRASH = self.NROWS
        self.NACC = self.NROWS + 2 * P
        assert 0 < self.ELAST <= GE and self.ELAST % TG == 0 and self.QP <= P
        assert self.NG >= max(PEEL + 2 * UNROLL, self.NBLK) and self.NBLK % 2 == 0 and self.NBX % 3 == 0
        assert self.NROWS + P < PAD_DST

        self.acc_dram = [nc.dram_tensor(f"acc_dram{j}", [self.NACC, F], F32).ap() for j in range(TG)]
        self.split_dram = nc.dram_tensor("split_dram", [self.NBX * P, 3 * F], BF16).ap()
        self.rows_dram = nc.dram_tensor("rows_dram", [self.NG, 2, 2, GE], BF16).ap()
        self.span_dram = nc.dram_tensor("span_dram", [2, self.NG], F32).ap()
        self.table_dram = nc.dram_tensor("table_dram", [self.NROWS * R, F], F32).ap()

        self.bank = [ctx.enter_context(nc.psum_tensor(f"bank{k}", [P, 512], F32)) for k in range(8)]

        def sb(name, shape, dt=F32):
            return ctx.enter_context(nc.sbuf_tensor(name, shape, dt))

        self.gate = {name: nc.alloc_semaphore(f"gate_{name}") for name in ("pe", "dve", "pool")}
        NBX, NT, NG = self.NBX, self.NT, self.NG
        self.xs = sb("xs", [P, NBX, F])
        self.rstd = sb("rstd", [P, NBX])
        self.shift = sb("shift", [P, NBX])
        self.cnt = sb("cnt", [P, NBX, R])
        self.rcnt3 = sb("rcnt3", [P, NBX, 3 * R], BF16)
        self.dstcol = sb("dstcol", [P, NT])
        self.local16 = sb("local16", [P, NT], BF16)
        self.srccol = sb("srccol", [P, NT])
        self.etcol = sb("etcol", [P, NT])
        self.base = sb("base", [P, NG], I32)
        self.base_f = sb("base_f", [P, NG])
        self.blk = sb("blk", [P, NG], I32)
        self.mask_hi = sb("mask_hi", [P, NG])
        self.mask_lo = sb("mask_lo", [P, NG])
        self.neg_nid = sb("neg_nid", [P, NG])
        self.nid_res = sb("nid_res", [P, NG])
        self.ctl = sb("ctl", [P, 1], I32)
        self.ident = sb("ident", [P, P])
        self.part = sb("part", [P, 1])
        self.iota_r = sb("iota_r", [P, R])
        self.iota_c = sb("iota_c", [P, P, TG], BF16)
        self.eps = sb("eps", [P, 1])
        self.coef = sb("coef", [2, P], BF16)
        self.zero16 = sb("zero16", [1, 512], BF16)
        self.ones3 = sb("ones3", [P, P], BF16)
        self.bias3 = sb("bias3", [P, 512], BF16)
        self.pow2 = sb("pow2", [P, 1])
        self.dup_above = sb("dup_above", [P, 1])
        self.trash_row = sb("trash_row", [P, 1])
        self.w1 = sb("w1", [F, F])
        self.w2 = sb("w2", [F, F])
        self.b1c = sb("b1c", [F, 1])
        self.wrel = [sb(f"wrel{k}", [F, R * F]) for k in range(2)]
        self.wroot = [sb(f"wroot{k}", [F, F]) for k in range(2)]
        self.biasb = [sb(f"biasb{k}", [P, F]) for k in range(2)]


class Windows:

    def __init__(self, g, own):
        self.g, self.own = g, own

    @contextmanager
    def passes(self, eng):
        if self.own:
            yield 0
        else:
            with eng.Fori(0, self.g.NBLK) as w:
                yield w

    def entry(self, group, w):
        return group if self.own else w

    def number(self, group, w=0):
        return group if self.own else group * self.g.NBLK + w


def for_windows(eng, g, program):
    own = eng.value_load(g.ctl[0:1, 0:1], min_val=0, max_val=1)
    with eng.If(own):
        program(Windows(g, True))
    with eng.Else():
        program(Windows(g, False))


def add_window(nc, dve, g, sums, window, s_pass, s_sum, entry, number, start=0):
    b = dve.value_load(g.blk[0:1, bass.ds(entry, 1)], min_val=0, max_val=g.NBLK - 1)
    dve.wait_ge(s_pass, number + 1)
    need(dve, s_sum, number * 2 + start)
    for mask, at in ((g.mask_hi, b), (g.mask_lo, b + 1)):
        to = sums[:, bass.ds(at, 1), :].rearrange("p a r -> p (a r)")
        nc.vector.scalar_tensor_tensor(to, window, mask[:, bass.ds(entry, 1)], to, ALU.mult, ALU.add).then_inc(s_sum, 1)


def norm_stats(nc, chain, g, bn, tmp):
    mean_e, sq_e, mean_o, sq_o = (bn[:, :, k] for k in (1, 2, 4, 5))
    chain(nc.vector.tensor_tensor(tmp[:, :], mean_e, mean_o, ALU.subtract))
    chain(nc.vector.tensor_tensor(tmp[:, :], tmp[:, :], tmp[:, :], ALU.mult))
    chain(nc.vector.tensor_scalar(tmp[:, :], tmp[:, :], 0.25, None, ALU.mult))
    chain(nc.vector.tensor_tensor(g.rstd[:, :], sq_e, sq_o, ALU.add))
    chain(nc.vector.scalar_tensor_tensor(g.rstd[:, :], g.rstd[:, :], 1.0 / F, tmp[:, :], ALU.mult, ALU.add))
    chain(nc.vector.tensor_tensor(g.shift[:, :], mean_e, mean_o, ALU.add))


def norm_scale(nc, chain, g):
    chain(nc.vector.reciprocal(g.rstd[:, :], g.rstd[:, :]))
    chain(nc.vector.scalar_tensor_tensor(g.shift[:, :], g.shift[:, :], -0.5, g.rstd[:, :], ALU.mult, ALU.mult))


def prepare(nc, g, x, src, dst, edge_type, W1, b1, W2, b2, basis, comp, root, bias):
    N, E, NG, NBLK, NBX, QP, EQ = g.N, g.E, g.NG, g.NBLK, g.NBX, g.QP, g.EQ
    CB = 3
    NCH = NBX // CB
    NSP = 4
    AHEAD = NCH // 2
    with ExitStack() as ctx:
        def sb(name, shape, dt=F32):
            return ctx.enter_context(nc.sbuf_tensor(name, shape, dt))

        def sem(name):
            return nc.alloc_semaphore(name)

        ids = [sb(f"ids{k}", [QP, EQ], I32) for k in range(3)]
        idt = sb("idt", [QP, EQ], I32)
        parts = [sb(f"parts{k}", [QP, 2, EQ], BF16) for k in range(2)]
        span = sb("span", [QP, 2, 4])
        span_b = sb("span_b", [P, 2, NG])
        first = sb("first", [P, NG])
        first_i = sb("first_i", [P, NG], I32)
        off_f = sb("off_f", [P, NG])
        blk_f = sb("blk_f", [P, NG])
        off_i = sb("off_i", [P, NG], I32)
        widest = sb("widest", [P, 1])
        fits = sb("fits", [P, 1])
        part_i = sb("part_i", [P, 1], I32)
        iota_i = sb("iota_i", [P, R], I32)
        pow2_i = sb("pow2_i", [P, 1], I32)
        iota_ci = sb("iota_ci", [P, P, TG], I32)
        dst_i = sb("dst_i", [P, g.NT], I32)
        scaled = sb("scaled", [F, F])
        zeros = sb("zeros", [P, CB * F])
        neglog = sb("neglog", [P, P])
        b2b = sb("b2b", [P, F])
        bsum = sb("bsum", [P, F])
        bpart = [sb(f"bpart{k}", [P, F], BF16) for k in range(3)]
        basis_sb = [sb(f"basis_sb{k}", [F, NBASIS, F]) for k in range(2)]
        comp_sb = [sb(f"comp_sb{k}", [P, R * NBASIS]) for k in range(2)]
        bn = sb("bn", [P, NBX, 6])
        bn_tmp = sb("bn_tmp", [P, NBX])
        h = [sb(f"h{k}", [P, CB, F]) for k in range(2)]
        rest = [sb(f"rest{k}", [P, CB, F]) for k in range(2)]
        split = [sb(f"split{k}", [P, CB, 3, F], BF16) for k in range(NSP)]

        s_pads = sem("p_pads")
        s_x = sem("p_x")
        s_ids = [sem(f"p_ids{k}") for k in range(3)]
        s_idf = sem("p_idf")
        s_col_tr = sem("p_col_tr")
        s_col = sem("p_col")
        s_wrel = sem("p_wrel")
        s_weights = sem("p_weights")
        s_iota = sem("p_iota")
        s_chain = sem("p_chain")
        s_parts = sem("p_parts")
        s_rows = sem("p_rows")
        s_span = sem("p_span")
        s_span_out = sem("p_span_out")
        s_span_in = sem("p_span_in")
        s_zero = sem("p_zero")
        s_cleared = sem("p_cleared")
        s_neglog = sem("p_neglog")
        s_bsum = sem("p_bsum")
        s_bn = sem("p_bn")
        s_var = sem("p_var")
        s_std = sem("p_std")
        s_scale = sem("p_scale")
        s_h = sem("p_h")
        s_part1 = sem("p_part1")
        s_rest1 = sem("p_rest1")
        s_part2 = sem("p_part2")
        s_part3 = sem("p_part3")
        s_split_out = [sem(f"p_split_out{k}") for k in range(NSP)]

        x_main = x[0:(NBLK - 1) * P, :].rearrange("(b p) f -> p b f", p=P)
        x_rest = N - (NBLK - 1) * P

        def for_chunks(eng, body):
            for c in range(NSP):
                body(c, c, 0)
            if NCH >= 2 * NSP:
                with eng.Fori(1, NCH // NSP) as i:
                    for k in range(NSP):
                        body(i * NSP + k, k, i)
            for c in range(NCH // NSP * NSP, NCH):
                body(c, c % NSP, c // NSP)

        block = ctx.enter_context(nc.Block())

        @block.sync
        def _(sp):
            sp.wait_ge(s_pads, 4)
            for k, ap in enumerate((dst, src, edge_type)):
                sp.dma_start(ids[k][0:QP - 1, :], ap[0:(QP - 1) * EQ].rearrange("(q e) -> q e", e=EQ)).then_inc(s_ids[k], 16)
                sp.dma_start(ids[k][QP - 1:QP, 0:E - (QP - 1) * EQ],
                             ap[(QP - 1) * EQ:E].rearrange("(a e) -> a e", a=1)).then_inc(s_ids[k], 16)
            sp.dma_start(g.xs[:, 0:NBLK - 1, :], x_main).then_inc(s_x, 16)
            sp.dma_start(g.xs[0:x_rest, NBLK - 1, :], x[(NBLK - 1) * P:N, :]).then_inc(s_x, 16)
            for k in range(2):
                sp.wait_ge(s_parts, k + 1)
                for half in range(2):
                    for s in range(4):
                        sp.dma_start(g.rows_dram[:, half, k, :].rearrange("(q s) e -> q s e", s=4)[:, s, :],
                                     parts[k][:, half, s * GE:(s + 1) * GE]).then_inc(s_rows, 16)
            sp.wait_ge(s_span, 2)
            for k in range(2):
                sp.dma_start(g.span_dram[k, :].rearrange("(q s) -> q s", s=4), span[:, k, :]).then_inc(s_span_out, 16)
            sp.wait_ge(s_span_out, 32)
            sp.dma_start(span_b[:, :, :], g.span_dram.partition_broadcast(P)).then_inc(s_span_in, 16)

            sp.wait_ge(s_zero, 1)

            def clear(first_row, rows):
                for k in range(TG):
                    sp.dma_start(g.acc_dram[k][bass.ds(first_row, rows), :].rearrange("(p r) f -> p (r f)", p=P),
                                 zeros[:, 0:rows // P * F]).then_inc(s_cleared, 16)

            for c in range(NCH * CB * P, g.NACC, P):
                clear(c, P)
            with sp.Fori(0, AHEAD) as i:
                clear(i * (CB * P), CB * P)
            with sp.Fori(0, NCH - AHEAD) as i:
                sp.wait_ge(s_h, i * (2 * CB) + 1)
                clear(i * (CB * P) + AHEAD * CB * P, CB * P)
            sp.wait_ge(s_cleared, 16 * TG * (NCH + (g.NACC - NCH * CB * P) // P))
            sp.wait_ge(s_rows, 16 * 16)

        @block.gpsimd
        def _(pool):
            nc.gpsimd.memset(g.ident[:, :], 0.0).then_inc(s_iota, 1)
            pool.wait_ge(s_iota, 1)
            nc.gpsimd.affine_select(out=g.ident[:, :], in_=g.ident[:, :], compare_op=ALU.not_equal, fill=1.0,
                                    base=0, pattern=[[-1, P]], channel_multiplier=1).then_inc(s_iota, 1)
            nc.gpsimd.iota(part_i[:, :], [[0, 1]], base=0, channel_multiplier=1).then_inc(s_iota, 1)
            nc.gpsimd.iota(iota_i[:, :], [[1, R]], base=0, channel_multiplier=0).then_inc(s_iota, 1)
            nc.gpsimd.iota(first_i[:, :], [[P, NG]], base=0, channel_multiplier=0).then_inc(s_iota, 1)
            nc.gpsimd.iota(iota_ci[:, :, :], [[1, P], [0, TG]], base=0, channel_multiplier=0).then_inc(s_iota, 1)

            pool.wait_ge(s_weights, 16 * 12)
            chain = Chain(pool, s_wrel)
            for k in range(2):
                for r in range(R):
                    w = g.wrel[k][:, r * F:(r + 1) * F]
                    for b in range(NBASIS):
                        c = r * NBASIS + b
                        chain(nc.gpsimd.tensor_scalar(scaled[:, :] if b else w, basis_sb[k][:, b, :], comp_sb[k][:, c:c + 1], None, ALU.mult))
                        if b:
                            chain(nc.gpsimd.tensor_tensor(w, w, scaled[:, :], ALU.add))

        @block.scalar
        def _(act):
            act.dma_start(g.w2[:, :], W2).then_inc(s_weights, 16)
            act.dma_start(b2b[:, :], b2.partition_broadcast(P)).then_inc(s_weights, 16)
            act.dma_start(g.w1[:, :], W1).then_inc(s_weights, 16)
            act.dma_start(g.b1c[:, :], b1.rearrange("(f a) -> f a", a=1)).then_inc(s_weights, 16)
            for k in range(2):
                act.dma_start(comp_sb[k][:, :], comp[k].rearrange("r b -> (r b)").partition_broadcast(P)).then_inc(s_weights, 16)
                act.dma_start(basis_sb[k][:, :, :], basis[k].rearrange("b i o -> i b o")).then_inc(s_weights, 16)
                act.dma_start(g.wroot[k][:, :], root[k]).then_inc(s_weights, 16)
                act.dma_start(g.biasb[k][:, :], bias[k].partition_broadcast(P)).then_inc(s_weights, 16)
            for n in range(12):
                act.wait_ge(s_col_tr, n + 1)
                col = (g.dstcol, g.srccol, g.etcol)[n // 4]
                nc.scalar.activation(col[:, :].rearrange("p (q s j) -> p s j q", s=4, j=TG)[:, n % 4],
                                     g.bank[n % 4][:, 0:TG * QP].rearrange("p (j q) -> p j q", j=TG), ACT.Copy).then_inc(s_col, 1)
            act.wait_ge(s_var, 1)
            nc.scalar.activation(g.rstd[:, :], g.rstd[:, :], ACT.Sqrt, bias=g.eps[:, 0:1]).then_inc(s_std, 1)
            act.wait_ge(s_scale, 1)

            def first_parts(c, k, used):
                need(act, s_rest1, c - 1)
                for b in range(CB):
                    i = c * CB + b
                    nc.scalar.activation(h[k % 2][:, b, :], g.xs[:, bass.ds(i, 1), :].rearrange("p a f -> p (a f)"), ACT.Relu,
                                         bias=g.shift[:, bass.ds(i, 1)], scale=g.rstd[:, bass.ds(i, 1)]).then_inc(s_h, 1)
                act.wait_ge(s_h, c * CB + CB)
                need(act, s_split_out[k], used * 16)
                nc.scalar.activation(split[k][:, :, 0, :], h[k % 2][:, :, :], ACT.Copy).then_inc(s_part1, 1)

            def second_part(c, k):
                act.wait_ge(s_rest1, c + 1)
                nc.scalar.activation(split[k][:, :, 1, :], rest[k % 2][:, :, :], ACT.Copy).then_inc(s_part2, 1)

            def split_chunk(c, k, used):
                first_parts(c, k, used)
                if not isinstance(c, int) or c > 0:
                    second_part(c - 1, (k - 1) % NSP)

            for_chunks(act, split_chunk)
            second_part(NCH - 1, (NCH - 1) % NSP)

        @block.tensor
        def _(pe):
            pe.wait_ge(s_iota, 6)
            for n in range(12):
                k, s = n // 4, n % 4
                pe.wait_ge(s_idf, k + 1)
                need(pe, s_col, n - 3)
                for j in range(TG):
                    ins = nc.tensor.transpose(g.bank[s][:, j * QP:(j + 1) * QP],
                                              ids[k][:, s * GE + j:(s + 1) * GE:TG].bitcast(F32), g.ident[0:QP, 0:QP])
                ins.then_inc(s_col_tr, 1)
            pe.wait_ge(s_neglog, 1)
            pe.wait_ge(s_weights, 16 * 12)
            nc.tensor.matmul(g.bank[4][:, 0:F], neglog[:, :], g.w2[:, :], start=True, stop=True).then_inc(s_bsum, 1)

        @block.vector
        def _(dve):
            chain = Chain(dve, s_chain)
            v = nc.vector
            v.memset(g.xs[:, NBLK - 1:NBX, :], 0.0).then_inc(s_pads, 1)
            v.memset(ids[0][:, :], PAD_DST).then_inc(s_pads, 1)
            v.memset(ids[1][:, :], g.TRASH).then_inc(s_pads, 1)
            v.memset(ids[2][:, :], R).then_inc(s_pads, 1)
            v.memset(zeros[:, :], 0.0).then_inc(s_zero, 1)
            v.memset(neglog[:, :], -LOG2).then_inc(s_neglog, 1)
            v.memset(g.eps[:, :], EPS)
            v.memset(g.cnt[:, :, :], 0.0)
            v.memset(g.zero16[:, :], 0.0)
            v.memset(g.ones3[:, :], 1.0)
            v.memset(g.bias3[:, :], 0.0)
            chain(v.memset(g.coef[0:2, :], 1.0))
            chain(v.memset(g.coef[0:1, :], float(P)))

            for k in range(2):
                dve.wait_ge(s_ids[k], 32)
                chain(v.tensor_scalar(idt[:, :], ids[k][:, :], 7, None, ALU.arith_shift_right))
                chain(v.tensor_copy(parts[k][:, 0, :], idt[:, :]))
                chain(v.tensor_scalar(idt[:, :], ids[k][:, :], P - 1, None, ALU.bitwise_and))
                v.tensor_copy(parts[k][:, 1, :], idt[:, :]).then_inc(s_parts, 1)
                dve.wait_ge(s_parts, k + 1)
                v.tensor_copy(ids[k][:, :].bitcast(F32), ids[k][:, :]).then_inc(s_idf, 1)
            dve.wait_ge(s_idf, 1)
            by_group = [ap[:, :].bitcast(F32).rearrange("q (s e) -> q s e", s=4) for ap in (ids[0], idt)]
            v.tensor_reduce(span[:, 0, :], by_group[0], AX_X, ALU.min).then_inc(s_span, 1)
            chain(v.scalar_tensor_tensor(by_group[1], by_group[0], float(PAD_DST), by_group[0], ALU.is_lt, ALU.mult))
            v.tensor_reduce(span[:, 1, :], by_group[1], AX_X, ALU.max).then_inc(s_span, 1)
            dve.wait_ge(s_ids[2], 32)
            v.tensor_copy(ids[2][:, :].bitcast(F32), ids[2][:, :]).then_inc(s_idf, 1)

            dve.wait_ge(s_x, 32)
            BODY = max(d for d in range(1, 12) if NBX % d == 0)
            with dve.Fori(0, NBX // BODY) as i:
                for k in range(BODY):
                    b = i * BODY + k
                    v.bn_stats(bn[:, bass.ds(b, 1), :].rearrange("p a k -> p (a k)"),
                               g.xs[:, bass.ds(b, 1), :].rearrange("p a f -> p (a f)")).then_inc(s_bn, 1)
            dve.wait_ge(s_bn, NBX)
            norm_stats(nc, chain, g, bn, bn_tmp)
            v.engine_nop().then_inc(s_var, 1)
            dve.wait_ge(s_std, 1)
            norm_scale(nc, chain, g)
            v.engine_nop().then_inc(s_scale, 1)

            dve.wait_ge(s_iota, 6)
            chain(v.tensor_copy(g.part[:, :], part_i[:, :]))
            chain(v.tensor_copy(g.iota_c[:, :, :], iota_ci[:, :, :]))
            chain(v.tensor_copy(g.iota_r[:, :], iota_i[:, :]))
            chain(v.tensor_copy(first[:, :], first_i[:, :]))
            chain(v.tensor_scalar(g.trash_row[:, :], g.part[:, :], float(g.TRASH + 1), None, ALU.add))
            chain(v.tensor_scalar(pow2_i[:, :], g.part[:, :], -float(1 << 23), 190.0 * (1 << 23), ALU.mult, ALU.add))
            chain(v.tensor_copy(g.pow2[:, :].bitcast(I32), pow2_i[:, :]))
            chain(v.tensor_scalar(g.dup_above[:, :], pow2_i[:, :].bitcast(F32), 2.5, None, ALU.mult))

            dve.wait_ge(s_span_in, 16)
            chain(v.tensor_tensor(off_f[:, :], span_b[:, 1, :], span_b[:, 0, :], ALU.subtract))
            chain(v.reduce_max(widest[:, :], off_f[:, :], AX_X))
            chain(v.tensor_scalar(fits[:, :], widest[:, :], float(P), None, ALU.is_lt))
            chain(v.tensor_tensor(g.base_f[:, :], span_b[:, 0, :], first[:, :], ALU.subtract))
            chain(v.scalar_tensor_tensor(g.base_f[:, :], g.base_f[:, :], fits[:, 0:1], first[:, :], ALU.mult, ALU.add))
            chain(v.tensor_copy(g.base[:, :], g.base_f[:, :]))
            chain(v.tensor_scalar(g.blk[:, :], g.base[:, :], 7, None, ALU.arith_shift_right))
            chain(v.tensor_scalar(off_i[:, :], g.base[:, :], P - 1, None, ALU.bitwise_and))
            chain(v.tensor_copy(blk_f[:, :], g.blk[:, :]))
            chain(v.tensor_copy(off_f[:, :], off_i[:, :]))
            chain(v.tensor_scalar(g.mask_hi[:, :], off_f[:, :], g.part[:, 0:1], None, ALU.is_le))
            chain(v.tensor_scalar(g.mask_lo[:, :], g.mask_hi[:, :], -1.0, 1.0, ALU.mult, ALU.add))
            chain(v.tensor_scalar(g.neg_nid[:, :], g.base_f[:, :], g.part[:, 0:1], -1.0, ALU.add, ALU.mult))
            chain(v.tensor_scalar(blk_f[:, :], blk_f[:, :], float(P), g.part[:, 0:1], ALU.mult, ALU.add))
            chain(v.scalar_tensor_tensor(g.nid_res[:, :], g.mask_lo[:, :], float(P), blk_f[:, :], ALU.mult, ALU.add))
            chain(v.tensor_copy(g.ctl[:, :], fits[:, :]))

            dve.wait_ge(s_col, 12)
            chain(v.tensor_copy(dst_i[:, :], g.dstcol[:, :]))
            chain(v.tensor_scalar(dst_i[:, :], dst_i[:, :], P - 1, None, ALU.bitwise_and))
            chain(v.tensor_copy(g.local16[:, :], dst_i[:, :]))

            dve.wait_ge(s_bsum, 1)
            chain(v.tensor_tensor(bsum[:, :], g.bank[4][:, 0:F], b2b[:, :], ALU.add))
            for k in range(3):
                chain(v.tensor_copy(bpart[k][:, :], bsum[:, :]))
                chain(v.tensor_tensor(bsum[:, :], bsum[:, :], bpart[k][:, :], ALU.subtract))
                for j in range(TG):
                    chain(v.tensor_copy(g.bias3[32 * k:32 * k + 1, j * F:(j + 1) * F], bpart[k][32 * k:32 * k + 1, :]))

            def third_part(c, k):
                dve.wait_ge(s_part2, c + 1)
                v.tensor_tensor(split[k][:, :, 2, :], rest[k % 2][:, :, :], split[k][:, :, 1, :], ALU.subtract).then_inc(s_part3, 1)

            def split_chunk(c, k, used):
                need(dve, s_part3, c - 1)
                dve.wait_ge(s_part1, c + 1)
                v.tensor_tensor(rest[k % 2][:, :, :], h[k % 2][:, :, :], split[k][:, :, 0, :], ALU.subtract).then_inc(s_rest1, 1)
                if not isinstance(c, int) or c > 0:
                    third_part(c - 1, (k - 1) % NSP)

            for_chunks(dve, split_chunk)
            third_part(NCH - 1, (NCH - 1) % NSP)

        @block.gpsimd
        def _(pool):
            to = g.split_dram.rearrange("(c b p) f -> c p b f", b=CB, p=P)

            def store(c, k, used):
                pool.wait_ge(s_part3, c + 1)
                chunk = to[c] if isinstance(c, int) else to[bass.ds(c, 1)].rearrange("a p b f -> p (a b) f")
                pool.dma_start(chunk, split[k][:, :, :, :].rearrange("p b k f -> p b (k f)")).then_inc(s_split_out[k], 16)

            for_chunks(pool, store)
            for k in range(NSP):
                pool.wait_ge(s_split_out[k], 16 * len(range(k, NCH, NSP)))


def filter_layer(nc, g, edge_attr):
    N, E, NG = g.N, g.E, g.NG
    NE = 4
    NTO = 4
    HALF = TG // 2
    with ExitStack() as ctx:
        def sb(name, shape, dt=F32):
            return ctx.enter_context(nc.sbuf_tensor(name, shape, dt))

        def sem(name):
            return nc.alloc_semaphore(name)

        edges = [sb(f"edges{k}", [P, TG, F]) for k in range(NE)]
        rows = [sb(f"rows{k}", [2, 2, GE], BF16) for k in range(NE)]
        win = [sb(f"win{k}", [P, 3 * F], BF16) for k in range(NE)]
        edges_t = [sb(f"edges_t{k}", [F, GE]) for k in range(2)]
        log1p = [sb(f"log1p{k}", [F, GE]) for k in range(2)]
        soft = [sb(f"soft{k}", [F, GE]) for k in range(2)]
        factor = [sb(f"factor{k}", [P, GE]) for k in range(2)]
        same = [sb(f"same{k}", [P, TG, P]) for k in range(2)]
        msg = [sb(f"msg{k}", [P, TG, F + 1]) for k in range(2)]
        total = [sb(f"total{k}", [P, TG, F + 1]) for k in range(NTO)]
        apart_by = [sb(f"apart_by{k}", [P, GE], BF16) for k in range(2)]
        to_edge = [sb(f"to_edge{k}", [P, P, TG], BF16) for k in range(2)]
        to_node = [sb(f"to_node{k}", [P, P, TG], BF16) for k in range(2)]
        types = [sb(f"types{k}", [P, TG, R], BF16) for k in range(2)]
        local = sb("local", [P, TG], BF16)
        dup = sb("dup", [P, TG])
        idx = [sb(f"idx{k}", [P, TG], I32) for k in range(NTO)]

        bank_t, bank_z, bank_e, bank_r, bank_h = g.bank[0:5]
        bank_c, bank_s = g.bank[5:7], g.bank[7]
        counts = bank_s[:, 0:R]

        s_edges = [sem(f"f_edges{k}") for k in range(NE)]
        s_rows = [sem(f"f_rows{k}") for k in range(NE)]
        s_win = [sem(f"f_win{k}") for k in range(NE)]
        s_const = sem("f_const")
        s_tr = sem("f_tr")
        s_trc = sem("f_trc")
        s_z = sem("f_z")
        s_abs = sem("f_abs")
        s_line = sem("f_line")
        s_exp = sem("f_exp")
        s_ln = sem("f_ln")
        s_soft = sem("f_soft")
        s_e = sem("f_e")
        s_ec = sem("f_ec")
        s_src = sem("f_src")
        s_same = sem("f_same")
        s_dst = sem("f_dst")
        s_apart = sem("f_apart")
        s_hot = sem("f_hot")
        s_local = sem("f_local")
        s_node = sem("f_node")
        s_h = sem("f_h")
        s_pass = sem("f_pass")
        s_cnt = sem("f_cnt")
        s_msg = sem("f_msg")
        s_total = sem("f_total")
        s_totc = sem("f_totc")
        s_dup = sem("f_dup")
        s_idx = sem("f_idx")
        s_sc = [sem(f"f_sc{j}") for j in range(TG)]

        block = ctx.enter_context(nc.Block())

        @block.sync
        def _(sp):
            def program(windows):
                def step(s):
                    if s.live(0, NG):
                        k = s.slot(NE, 0)
                        need(sp, s_tr, s.at(NE - 1))
                        if isinstance(s.i, int) and s.c == NG - 1 and g.ELAST < GE:
                            sp.dma_start(edges[k][0:g.ELAST // TG, :, :],
                                         edge_attr[(NG - 1) * GE:E, :].rearrange("(p j) f -> p j f", j=TG)).then_inc(s_edges[k], 16)
                        else:
                            sp.dma_start(edges[k][:, :, :],
                                         edge_attr[bass.ds(s.at(0) * GE, GE), :].rearrange("(p j) f -> p j f", j=TG)).then_inc(s_edges[k], 16)
                        need(sp, s_dst, s.at(NE - 1))
                        sp.dma_start(rows[k][:, :, :],
                                     g.rows_dram[bass.ds(s.at(0), 1)].rearrange("a h d e -> (a h) d e")).then_inc(s_rows[k], 16)
                    if s.live(2, NG):
                        k = s.slot(NE, 2)
                        with windows.passes(sp) as w:
                            if windows.own:
                                need(sp, s_pass, s.at(NE + 1))
                            else:
                                sp.wait_ge(s_hot, windows.number(s.at(2), w) + 1)
                            first = sp.value_load(g.base[0:1, bass.ds(windows.entry(s.at(2), w), 1)], min_val=0, max_val=g.NROWS)
                            sp.dma_start(win[k][:, :], g.split_dram[bass.ds(first, P), :]).then_inc(s_win[k], 16)

                run_steps(sp, NG - UNROLL, UNROLL + 4, step)

            for_windows(sp, g, program)

        @block.tensor
        def _(pe):
            def program(windows):
                def step(s):
                    if s.live(2, NG):
                        need(pe, s_rows[s.slot(NE, 2)], s.use(NE, 2) * 16 + 16)
                        if windows.own:
                            need(pe, s_apart, s.at(2))
                        elif s.c > 2:
                            pe.wait_ge(s_hot, windows.number(s.at(2)))
                        nc.tensor.matmul(bank_r[:, :], g.coef[0:2, :], rows[s.slot(NE, 2)][0:2, 1, :],
                                         start=True, stop=True).then_inc(s_src, 1)
                    if s.live(0, NG):
                        need(pe, s_edges[s.slot(NE, 0)], s.use(NE, 0) * 16 + 16)
                        need(pe, s_trc, s.at(0))
                        for j in range(TG):
                            ins = nc.tensor.transpose(bank_t[:, j * P:(j + 1) * P], edges[s.slot(NE, 0)][:, j, :], g.ident[:, :])
                        ins.then_inc(s_tr, 1)
                    if s.live(1, NG):
                        need(pe, s_trc, s.at(1) + 1)
                        need(pe, s_line, s.at(1))
                        nc.tensor.matmul(bank_z[:, :], g.w1[:, :], edges_t[s.slot(2, 1)][:, :],
                                         start=True, stop=True).then_inc(s_z, 1)
                    if s.live(2, NG):
                        k = s.slot(2, 2)
                        pe.wait_ge(s_same, s.at(2) + 1)
                        nc.tensor.matmul(bank_r[:, :], g.coef[0:2, :], rows[s.slot(NE, 2)][0:2, 0, :],
                                         start=True, stop=True).then_inc(s_dst, 1)
                    if s.live(3, NG):
                        k = s.slot(2, 3)
                        need(pe, s_same, s.at(3) + 1)
                        need(pe, s_msg, s.at(3) + 1)
                        need(pe, s_totc, s.at(3))
                        for j in range(TG):
                            ins = nc.tensor.matmul(bank_c[j // HALF][:, j % HALF * (F + 1):(j % HALF + 1) * (F + 1)],
                                                   same[k][:, j, :], msg[k][:, j, :], start=True, stop=True)
                        ins.then_inc(s_total, 1)
                    if s.live(2, NG):
                        k = s.slot(2, 2)
                        need(pe, s_soft, s.at(2) + 1)
                        need(pe, s_ec, s.at(2))
                        nc.tensor.matmul(bank_e[:, :], g.ones3[0:96, :], g.bias3[0:96, :], start=True, stop=True)
                        for j in range(TG):
                            ins = nc.tensor.matmul(bank_e[:, j * F:(j + 1) * F], soft[k][:, j * P:(j + 1) * P], g.w2[:, :],
                                                   start=False, stop=True, skip_group_check=True)
                        ins.then_inc(s_e, 1)
                        need(pe, s_msg, s.at(2))
                        if not windows.own:
                            nc.tensor.matmul(bank_h[:, :], g.zero16[0:1, 0:P], g.zero16[0:1, :], start=True, stop=True)
                        with windows.passes(pe) as w:
                            q = windows.number(s.at(2), w)
                            pe.wait_ge(s_hot, q + 1)
                            pe.wait_ge(s_win[s.slot(NE, 2)], windows.number(s.use(NE, 2), w) * 16 + 16)
                            for j in range(TG):
                                for part in range(3):
                                    ins = nc.tensor.matmul(bank_h[:, j * F:(j + 1) * F], to_edge[k][:, :, j],
                                                           win[s.slot(NE, 2)][:, part * F:(part + 1) * F],
                                                           start=windows.own and part == 0, stop=part == 2 or not windows.own,
                                                           skip_group_check=not windows.own)
                            ins.then_inc(s_h, 1)
                            pe.wait_ge(s_node, q + 1)
                            if windows.own:
                                need(pe, s_cnt, q * 2)
                            for j in range(TG):
                                ins = nc.tensor.matmul(counts, to_node[k][:, :, j], types[k][:, j, :], start=j == 0, stop=j == TG - 1)
                            ins.then_inc(s_pass, 1)

                run_steps(pe, NG, 4, step)

            pe.wait_ge(s_const, 1)
            for_windows(pe, g, program)

        @block.scalar
        def _(act):
            def program(windows):
                def step(s):
                    if s.live(0, NG):
                        need(act, s_tr, s.at(0) + 1)
                        need(act, s_z, s.at(1))
                        nc.scalar.activation(edges_t[s.slot(2, 0)][:, :], bank_t[:, :], ACT.Copy).then_inc(s_trc, 1)
                    if s.live(1, NG):
                        t = log1p[s.slot(2, 1)]
                        need(act, s_z, s.at(1) + 1)
                        need(act, s_soft, s.at(2))
                        nc.scalar.activation(t[:, :], bank_z[:, :], ACT.Abs, bias=g.b1c[:, 0:1]).then_inc(s_abs, 1)
                    if s.live(2, NG) and windows.own:
                        need(act, s_dst, s.at(2) + 1)
                        need(act, s_hot, s.at(3))
                        nc.scalar.activation(apart_by[s.slot(2, 2)][:, :], bank_r[:, :], ACT.Identity,
                                             bias=g.neg_nid[:, bass.ds(s.at(2), 1)]).then_inc(s_apart, 1)
                    if s.live(1, NG):
                        need(act, s_abs, s.at(1) + 1)
                        nc.scalar.activation(t[:, :], t[:, :], ACT.Exp, scale=-1.0).then_inc(s_exp, 1)
                    if s.live(3, NG):
                        need(act, s_total, s.at(3) + 1)
                        need(act, s_dup, s.at(3 + NTO - 1))
                        for j in range(TG):
                            need(act, s_sc[j], s.at(3 + NTO - 1) * 16)
                        for h in range(2):
                            ins = nc.scalar.activation(total[s.slot(NTO, 3)][:, h * HALF:(h + 1) * HALF, :].rearrange("p a b -> p (a b)"),
                                                       bank_c[h][:, 0:HALF * (F + 1)], ACT.Copy)
                        ins.then_inc(s_totc, 1)
                    if s.live(2, NG):
                        need(act, s_e, s.at(2) + 1)
                        need(act, s_msg, s.at(3))
                        nc.scalar.activation(factor[s.slot(2, 2)][:, :], bank_e[:, :], ACT.Copy).then_inc(s_ec, 1)
                    if s.live(1, NG):
                        need(act, s_exp, s.at(1) + 1)
                        nc.scalar.activation(t[:, :], t[:, :], ACT.Ln, bias=1.0).then_inc(s_ln, 1)

                run_steps(act, NG, 4, step)

            nc.scalar.preload_act_table_set("natural_log_exp_and_others")
            for_windows(act, g, program)

        @block.vector
        def _(dve):
            v = nc.vector
            for k in range(2):
                ins = v.tensor_copy(msg[k][:, :, F:F + 1], g.pow2[:, 0:1].unsqueeze(1).to_broadcast([P, TG, 1]))
            ins.then_inc(s_const, 1)

            def program(windows):
                def step(s):
                    if s.live(2, NG) and windows.own:
                        k = s.slot(2, 2)
                        need(dve, s_apart, s.at(2) + 1)
                        need(dve, s_pass, s.at(3))
                        v.tensor_scalar(to_edge[k][:, :, :].rearrange("p a b -> p (a b)"), apart_by[k][:, :], 0.0, None,
                                        ALU.is_equal).then_inc(s_hot, 1)
                    if s.live(2, NG):
                        k = s.slot(2, 2)
                        four = bass.ds(s.at(2) * TG, TG)
                        v.tensor_tensor(types[k][:, :, :], g.etcol[:, four].unsqueeze(2).to_broadcast([P, TG, R]),
                                        g.iota_r[:, :].unsqueeze(1).to_broadcast([P, TG, R]), ALU.is_equal)
                        if windows.own:
                            v.tensor_tensor(to_node[k][:, :, :], g.iota_c[:, :, :],
                                            g.local16[:, four].unsqueeze(1).to_broadcast([P, P, TG]), ALU.is_equal).then_inc(s_node, 1)
                    if s.live(4, NG):
                        k = s.slot(NTO, 4)
                        need(dve, s_totc, s.at(4) + 1)
                        need(dve, s_idx, s.at(4))
                        v.tensor_scalar(dup[:, :].unsqueeze(2), total[k][:, :, F:F + 1], g.dup_above[:, 0:1],
                                        g.trash_row[:, 0:1], ALU.is_gt, ALU.mult).then_inc(s_dup, 1)
                    if s.live(1, NG):
                        need(dve, s_abs, s.at(1) + 1)
                        need(dve, s_e, s.at(2))
                        v.tensor_scalar(soft[s.slot(2, 1)][:, :], bank_z[:, :], g.b1c[:, 0:1], 0.0, ALU.add, ALU.max).then_inc(s_line, 1)
                    if s.live(4, NG):
                        k = s.slot(NTO, 4)
                        need(dve, s_dup, s.at(4) + 1)
                        v.tensor_tensor(idx[k][:, :], dup[:, :], g.srccol[:, bass.ds(s.at(4) * TG, TG)],
                                        ALU.max).then_inc(s_idx, 1)
                    if s.live(2, NG) and not windows.own:
                        k = s.slot(2, 2)
                        dve.wait_ge(s_dst, s.at(2) + 1)
                        apart(dve, g.gate["dve"])
                        with windows.passes(dve) as w:
                            q = dve.snap(windows.number(s.at(2), w))
                            v.tensor_scalar(to_edge[k][:, :, :].rearrange("p a b -> p (a b)"), bank_r[:, :],
                                            g.neg_nid[:, bass.ds(w, 1)], 0.0, ALU.add, ALU.is_equal).then_inc(s_hot, 1)
                            v.tensor_scalar(local[:, :], g.dstcol[:, four], g.base_f[:, bass.ds(w, 1)], None,
                                            ALU.subtract).then_inc(s_local, 1)
                            dve.wait_ge(s_local, q + 1)
                            v.tensor_tensor(to_node[k][:, :, :], g.iota_c[:, :, :],
                                            local[:, :].unsqueeze(1).to_broadcast([P, P, TG]), ALU.is_equal).then_inc(s_node, 1)
                            add_window(nc, dve, g, g.cnt, counts, s_pass, s_cnt, w, q, start=1)
                    if s.live(2, NG):
                        k = s.slot(2, 2)
                        need(dve, s_h, windows.number(s.at(1)))
                        need(dve, s_ec, s.at(2) + 1)
                        need(dve, s_total, s.at(3))
                        v.tensor_tensor(msg[k][:, :, 0:F], bank_h[:, :].rearrange("p (j f) -> p j f", j=TG),
                                        factor[k][:, :].rearrange("p (j f) -> p j f", j=TG), ALU.mult).then_inc(s_msg, 1)
                    if s.live(1, NG):
                        k = s.slot(2, 1)
                        four = bass.ds(s.at(1) * TG, TG)
                        need(dve, s_src, s.at(1) + 1)
                        need(dve, s_total, s.at(2))
                        v.tensor_tensor(same[k][:, :, :], bank_r[:, :].rearrange("q (p j) -> q j p", j=TG),
                                        g.srccol[:, four].unsqueeze(2).to_broadcast([P, TG, P]), ALU.is_equal).then_inc(s_same, 1)
                    if s.live(1, NG):
                        k = s.slot(2, 1)
                        need(dve, s_ln, s.at(1) + 1)
                        need(dve, s_line, s.at(1) + 1)
                        v.tensor_tensor(soft[k][:, :], soft[k][:, :], log1p[k][:, :], ALU.add).then_inc(s_soft, 1)
                    if s.live(2, NG) and windows.own:
                        add_window(nc, dve, g, g.cnt, counts, s_pass, s_cnt, s.at(2), s.at(2))

                if not windows.own:
                    v.engine_nop().then_inc(s_cnt, 1)
                run_steps(dve, NG, 4, step)
                if windows.own:
                    dve.wait_ge(s_cnt, 2 * NG)

            for_windows(dve, g, program)

        @block.gpsimd
        def _(pool):

            def step(s):
                k = s.slot(NTO, 0)
                need(pool, s_idx, s.at(0) + 1)
                for j in range(TG):
                    need(pool, s_sc[j], s.at(0) * 16)
                    apart(pool, g.gate["pool"])
                    pool.indirect_dma_start(g.acc_dram[j][:, :], bass.IndirectOffsetOnAxis(ap=idx[k][:, j:j + 1], axis=0),
                                            total[k][:, j, 0:F], None, compute_op=ALU.add).then_inc(s_sc[j], 16)

            run_steps(pool, NG, 0, step)
            for j in range(TG):
                pool.wait_ge(s_sc[j], NG * 16)


def make_table(nc, g, hacc, which):
    NBLK = g.NBLK
    first = which == 0
    HL = 2 if first else 0
    ML = HL + 2
    with ExitStack() as ctx:
        def sb(name, shape, dt=F32):
            return ctx.enter_context(nc.sbuf_tensor(f"{name}_{which}", shape, dt))

        def sem(name):
            return nc.alloc_semaphore(f"{name}_{which}")

        NST = 4
        h = [sb(f"th{k}", [P, F]) for k in range(2)]
        h_t = [sb(f"th_t{k}", [F, P]) for k in range(2)]
        made = [sb(f"made{k}", [P, R * F]) for k in range(NST)]
        own = [sb(f"own{k}", [P, F]) for k in range(2)]
        s_h = sem("t_h")
        s_tr = sem("t_tr")
        s_trc = sem("t_trc")
        s_mm = sem("t_mm")
        s_left = sem("t_left")
        s_right = sem("t_right")
        s_own = sem("t_own")
        s_sum = sem("t_sum")
        s_out = [sem(f"t_out{k}") for k in range(NST)]
        if first:
            sums = [sb(f"sums{k}", [P, TG, F]) for k in range(4)]
            added = [sb(f"added{k}", [P, F]) for k in range(2)]
            bn = [sb(f"tbn{k}", [P, 6]) for k in range(2)]
            norm = [sb(f"norm{k}", [P, 2]) for k in range(2)]
            rstd = [sb(f"trstd{k}", [P, 1]) for k in range(2)]
            shift = [sb(f"tshift{k}", [P, 1]) for k in range(2)]
            seg = sb("seg", [P, g.NT])
            s_sums = [sem(f"t_sums{k}") for k in range(4)]
            s_sums2 = [sem(f"t_sums2_{k}") for k in range(4)]
            s_added = sem("t_added")
            s_x = sem("t_x")
            s_bn = sem("t_bn")
            s_var = sem("t_var")
            s_std = sem("t_std")
            s_rstd = sem("t_rstd")
            s_shift = sem("t_shift")
            s_chain = sem("t_chain")
        table = g.table_dram.rearrange("(b p r) f -> b p (r f)", p=P, r=R)
        wrel, wroot, biasb = g.wrel[which], g.wroot[which], g.biasb[which]
        block = ctx.enter_context(nc.Block())
        HALF = R * F // 2

        def blocks(eng, body, last=ML):
            n = NBLK // UNROLL * UNROLL
            run_steps(eng, n, 0, body)
            for c in range(n, NBLK + last):
                body(Step(0, c))

        def one(ap, at):
            return ap[:, bass.ds(at, 1), :].rearrange("p a f -> p (a f)")

        @block.scalar
        def _(act):
            def step(s):
                if s.live(HL, NBLK):
                    k = s.slot(2, HL)
                    need(act, s_tr, s.at(HL + 1))
                    if first:
                        need(act, s_shift, s.at(HL) + 1)
                        nc.scalar.activation(h[k][:, :], one(g.xs, s.at(HL)), ACT.Relu, bias=shift[k][:, 0:1],
                                             scale=rstd[k][:, 0:1]).then_inc(s_h, 1)
                    else:
                        nc.scalar.activation(h[k][:, :], one(hacc, s.at(HL)), ACT.Relu).then_inc(s_h, 1)
                if first and s.live(1, NBLK):
                    need(act, s_var, s.at(1) + 1)
                    nc.scalar.activation(rstd[s.slot(2, 1)][:, :], norm[s.slot(2, 1)][:, 1:2], ACT.Sqrt,
                                         bias=g.eps[:, 0:1]).then_inc(s_std, 1)
                if s.live(ML, NBLK):
                    need(act, s_mm, s.at(ML) + 1)
                    need(act, s_out[s.slot(NST, ML)], s.use(NST, ML) * 16)
                    if first:
                        nc.scalar.activation(made[s.slot(NST, ML)][:, 0:HALF], g.bank[2 + s.slot(2, ML)][:, :], ACT.Copy)
                    nc.scalar.activation(made[s.slot(NST, ML)][:, HALF:], g.bank[4 + s.slot(2, ML)][:, :], ACT.Copy).then_inc(s_right, 1)
                if s.live(HL, NBLK):
                    need(act, s_tr, s.at(HL) + 1)
                    need(act, s_mm, s.at(HL + 1))
                    k = s.slot(2, HL)
                    nc.scalar.activation(h_t[k][:, :], g.bank[k][:, 0:P], ACT.Copy).then_inc(s_trc, 1)

            blocks(act, step)

        @block.tensor
        def _(pe):
            def step(s):
                if s.live(ML, NBLK):
                    k = s.slot(2, ML)
                    need(pe, s_trc, s.at(ML) + 1)
                    if not first:
                        need(pe, s_left, s.at(ML + 1))
                    need(pe, s_right, s.at(ML + 1))
                    need(pe, s_own, s.at(ML + 1))
                    nc.tensor.matmul(g.bank[2 + k][:, :], h_t[k][:, :], wrel[:, 0:HALF], start=True, stop=True)
                    nc.tensor.matmul(g.bank[4 + k][:, :], h_t[k][:, :], wrel[:, HALF:], start=True, stop=True)
                    nc.tensor.matmul(g.bank[6 + k][:, 0:F], h_t[k][:, :], wroot[:, :], start=True, stop=True).then_inc(s_mm, 1)
                if s.live(HL, NBLK):
                    k = s.slot(2, HL)
                    need(pe, s_h, s.at(HL) + 1)
                    need(pe, s_trc, s.at(HL + 1))
                    nc.tensor.transpose(g.bank[k][:, 0:P], h[k][:, :], g.ident[:, :]).then_inc(s_tr, 1)

            blocks(pe, step)

        @block.vector
        def _(dve):
            v = nc.vector
            if first:
                chain = Chain(dve, s_chain)
                v.memset(hacc[:, NBLK:, :], 0.0)
                chain(v.tensor_scalar(seg[:, :], g.srccol[:, :], float(R), None, ALU.mult))
                chain(v.tensor_tensor(seg[:, :], seg[:, :], g.etcol[:, :], ALU.add))
                chain(v.tensor_scalar(g.srccol[:, :], seg[:, :], float(g.NROWS * R - 1), None, ALU.min))

            def step(s):
                k0, k1, km = s.slot(2, 0), s.slot(2, 1), s.slot(2, ML)
                if first and s.live(0, NBLK):
                    for loaded in (s_sums, s_sums2):
                        need(dve, loaded[s.slot(4, 0)], s.use(4, 0) * (8 * TG) + 8 * TG)
                    v.tensor_reduce(added[k0][:, :], sums[s.slot(4, 0)][:, :, :].rearrange("p j f -> p f j"), AX_X, ALU.add).then_inc(s_added, 1)
                if s.live(ML, NBLK):
                    need(dve, s_mm, s.at(ML) + 1)
                    if first:
                        v.tensor_tensor(one(hacc, s.at(ML)), g.bank[6 + km][:, 0:F], biasb[:, :], ALU.add).then_inc(s_own, 1)
                    else:
                        need(dve, s_out[s.slot(NST, ML)], s.use(NST, ML) * 16)
                        v.tensor_copy(made[s.slot(NST, ML)][:, 0:HALF], g.bank[2 + km][:, :]).then_inc(s_left, 1)
                        need(dve, s_sum, s.at(ML + 1))
                        v.tensor_tensor(own[km][:, :], g.bank[6 + km][:, 0:F], biasb[:, :], ALU.add).then_inc(s_own, 1)
                        need(dve, s_own, s.at(ML) + 1)
                        v.tensor_tensor(one(g.xs, s.at(ML)), one(g.xs, s.at(ML)), own[km][:, :], ALU.add).then_inc(s_sum, 1)
                if first and s.live(0, NBLK):
                    need(dve, s_added, s.at(0) + 1)
                    v.tensor_tensor(one(g.xs, s.at(0)), one(g.xs, s.at(0)), added[k0][:, :], ALU.add).then_inc(s_x, 1)
                if first and s.live(1, NBLK):
                    need(dve, s_std, s.at(1) + 1)
                    v.reciprocal(rstd[k1][:, :], rstd[k1][:, :]).then_inc(s_rstd, 1)
                if first and s.live(0, NBLK):
                    need(dve, s_x, s.at(0) + 1)
                    apart(dve, g.gate["dve"])
                    v.bn_stats(bn[k0][:, :], one(g.xs, s.at(0))).then_inc(s_bn, 1)
                if first and s.live(1, NBLK):
                    need(dve, s_h, s.at(2))
                    need(dve, s_rstd, s.at(1) + 1)
                    v.scalar_tensor_tensor(shift[k1][:, :], norm[k1][:, 0:1], -1.0, rstd[k1][:, :], ALU.mult, ALU.mult).then_inc(s_shift, 1)
                if first and s.live(0, NBLK):
                    need(dve, s_shift, s.at(1))
                    need(dve, s_bn, s.at(0) + 1)
                    apart(dve, g.gate["dve"])
                    v.bn_aggr(norm[k0][:, :], bn[k0][:, :]).then_inc(s_var, 1)

            blocks(dve, step)

        if first:
            @block.gpsimd
            def _(pool):
                def step(s):
                    if s.live(0, NBLK):
                        need(pool, s_added, s.at(3))
                        for j in range(TG // 2, TG):
                            pool.dma_start(sums[s.slot(4, 0)][:, j, :], g.acc_dram[j][bass.ds(s.at(0) * P, P), :]).then_inc(s_sums2[s.slot(4, 0)], 16)

                blocks(pool, step)

        @block.sync
        def _(sp):
            SL = ML + 3 if first else ML

            def step(s):
                if first and s.live(0, NBLK):
                    need(sp, s_added, s.at(3))
                    for j in range(TG // 2):
                        sp.dma_start(sums[s.slot(4, 0)][:, j, :], g.acc_dram[j][bass.ds(s.at(0) * P, P), :]).then_inc(s_sums[s.slot(4, 0)], 16)
                if s.live(SL, NBLK):
                    k = s.slot(NST, SL)
                    if not first:
                        need(sp, s_left, s.at(SL) + 1)
                    need(sp, s_right, s.at(SL) + 1)
                    sp.dma_start(table[bass.ds(s.at(SL), 1)].rearrange("a p c -> (a p) c"), made[k][:, :]).then_inc(s_out[k], 16)

            blocks(sp, step, SL)
            for k in range(NST):
                sp.wait_ge(s_out[k], 16 * len(range(k, NBLK, NST)))


def convolve(nc, g, hacc, which):
    NG = g.NG
    sums = hacc if which == 0 else g.xs
    weigh = which == 0
    NGA = 4
    with ExitStack() as ctx:
        def sb(name, shape, dt=F32):
            return ctx.enter_context(nc.sbuf_tensor(f"{name}_{which}", shape, dt))

        def sem(name):
            return nc.alloc_semaphore(f"{name}_{which}")

        idx = [sb(f"cidx{k}", [P, TG], I32) for k in range(NGA)]
        got = [sb(f"got{k}", [P, TG, F]) for k in range(NGA)]
        local = sb("clocal", [P, TG], BF16)
        to_node = [sb(f"cto_node{k}", [P, P, TG], BF16) for k in range(2)]
        share = [sb(f"share{k}", [P, TG, P]) for k in range(2)]
        if weigh:
            rows = [sb(f"crows{k}", [2, GE], BF16) for k in range(4)]
            to_edge = [sb(f"cto_edge{k}", [P, P, TG], BF16) for k in range(2)]
            rest = sb("crest", [P, g.NBX, R])
            lower = [sb(f"lower{k}", [P, 3 * R], BF16) for k in range(2)]
            win = [sb(f"cwin{k}", [P, 3 * R], BF16) for k in range(2)]
            types = sb("ctypes", [P, TG, R])
            by_type = sb("by_type", [P, TG, 3 * R])

        bank_r, bank_w = g.bank[0], g.bank[1]
        window = [g.bank[2 + k][:, 0:F] for k in range(2)]
        rates = bank_w[:, 0:TG * 3 * R]

        s_idx = sem("c_idx")
        s_got = [sem(f"c_got{k}") for k in range(NGA)]
        s_local = sem("c_local")
        s_node = sem("c_node")
        s_share = sem("c_share")
        s_pass = sem("c_pass")
        s_sum = sem("c_sum")
        if weigh:
            s_rows = [sem(f"c_rows{k}") for k in range(4)]
            s_dst = sem("c_dst")
            s_low = sem("c_low")
            s_hot = sem("c_hot")
            s_rate = sem("c_rate")
            s_types = sem("c_types")
            s_by_type = sem("c_by_type")
            s_weight = sem("c_weight")
            s_counts = sem("c_counts")
        block = ctx.enter_context(nc.Block())

        if weigh:
            @block.sync
            def _(sp):
                def step(s):
                    k = s.slot(4, 0)
                    need(sp, s_dst, s.at(3))
                    sp.dma_start(rows[k][:, :], g.rows_dram[bass.ds(s.at(0), 1), :, 0, :].rearrange("a h e -> (a h) e")).then_inc(s_rows[k], 16)

                run_steps(sp, NG, 0, step)

        @block.gpsimd
        def _(pool):
            def step(s):
                k = s.slot(NGA, 0)
                need(pool, s_idx, s.at(0) + 1)
                apart(pool, g.gate["pool"])
                for j in range(TG):
                    pool.indirect_dma_start(got[k][:, j, :], None, g.table_dram[:, :],
                                            bass.IndirectOffsetOnAxis(ap=idx[k][:, j:j + 1], axis=0)).then_inc(s_got[k], 16)

            run_steps(pool, NG, 0, step)

        @block.tensor
        def _(pe):
            def program(windows):
                def step(s):
                    if weigh and s.live(1, NG):
                        k = s.slot(2, 1)
                        need(pe, s_by_type, s.at(1))
                        if not windows.own:
                            nc.tensor.matmul(rates, g.zero16[0:1, 0:P], g.zero16[0:1, 0:TG * 3 * R], start=True, stop=True)
                        with windows.passes(pe) as w:
                            pe.wait_ge(s_hot, windows.number(s.at(1), w) + 1)
                            for j in range(TG):
                                ins = nc.tensor.matmul(rates[:, j * 3 * R:(j + 1) * 3 * R], to_edge[k][:, :, j], win[k][:, :],
                                                       start=windows.own, stop=True, skip_group_check=not windows.own)
                            ins.then_inc(s_rate, 1)
                    if weigh and s.live(0, NG):
                        need(pe, s_rows[s.slot(4, 0)], s.use(4, 0) * 16 + 16)
                        need(pe, s_hot, windows.number(s.at(0)))
                        nc.tensor.matmul(bank_r[:, :], g.coef[0:2, :], rows[s.slot(4, 0)][0:2, :], start=True, stop=True).then_inc(s_dst, 1)
                    if s.live(3, NG):
                        k, ka = s.slot(2, 3), s.slot(NGA, 3)
                        need(pe, s_got[ka], s.use(NGA, 3) * (16 * TG) + 16 * TG)
                        if windows.own:
                            need(pe, s_sum, s.at(4) * 2)
                        apart(pe, g.gate["pe"])
                        with windows.passes(pe) as w:
                            pe.wait_ge(s_share, windows.number(s.at(3), w) + 1)
                            for j in range(TG):
                                ins = nc.tensor.matmul(window[k], share[k][:, j, :], got[ka][:, j, :], start=j == 0, stop=j == TG - 1)
                            ins.then_inc(s_pass, 1)

                run_steps(pe, NG, 3, step)

            for_windows(pe, g, program)

        @block.scalar
        def _(act):
            def program(windows):
                share_lag = 2 if windows.own else 3

                def step(s):
                    if s.live(0, NG):
                        need(act, s_pass, windows.number(s.at(NGA - 1)))
                        nc.scalar.activation(idx[s.slot(NGA, 0)][:, :], g.srccol[:, bass.ds(s.at(0) * TG, TG)], ACT.Copy).then_inc(s_idx, 1)
                    if s.live(share_lag, NG):
                        k = s.slot(2, share_lag)
                        if weigh:
                            need(act, s_weight, s.at(share_lag) + 1)
                        if windows.own:
                            need(act, s_pass, s.at(share_lag + 1))
                        with windows.passes(act) as w:
                            act.wait_ge(s_node, windows.number(s.at(share_lag), w) + 1)
                            for j in range(TG):
                                ins = nc.scalar.activation(share[k][:, j, :], to_node[k][:, :, j], ACT.Copy,
                                                           scale=g.etcol[:, bass.ds(s.at(share_lag) * TG + j, 1)])
                            ins.then_inc(s_share, 1)

                run_steps(act, NG, 3, step)

            for_windows(act, g, program)

        @block.vector
        def _(dve):
            v = nc.vector

            def rate_window(windows, s, w):
                k = s.slot(2, 1)
                entry = windows.entry(s.at(1), w)
                b = dve.value_load(g.blk[0:1, bass.ds(entry, 1)], min_val=0, max_val=g.NBLK - 1)
                v.tensor_scalar(lower[k][:, :], g.rcnt3[:, bass.ds(b + 1, 1), :].rearrange("p a r -> p (a r)"),
                                g.mask_lo[:, bass.ds(entry, 1)], None, ALU.mult).then_inc(s_low, 1)
                v.tensor_scalar(to_edge[k][:, :, :].rearrange("p a b -> p (a b)"), bank_r[:, :],
                                g.nid_res[:, bass.ds(entry, 1)], None, ALU.is_equal)
                dve.wait_ge(s_low, windows.number(s.at(1), w) + 1)
                v.scalar_tensor_tensor(win[k][:, :], g.rcnt3[:, bass.ds(b, 1), :].rearrange("p a r -> p (a r)"),
                                       g.mask_hi[:, bass.ds(entry, 1)], lower[k][:, :], ALU.mult, ALU.add).then_inc(s_hot, 1)

            def program(windows):
                def step(s):
                    if weigh and s.live(2, NG):
                        four = bass.ds(s.at(2) * TG, TG)
                        v.tensor_tensor(types[:, :, :], g.etcol[:, four].unsqueeze(2).to_broadcast([P, TG, R]),
                                        g.iota_r[:, :].unsqueeze(1).to_broadcast([P, TG, R]), ALU.is_equal).then_inc(s_types, 1)
                        dve.wait_ge(s_rate, windows.number(s.at(1)))
                        need(dve, s_types, s.at(2) + 1)
                        for j in range(TG):
                            ins = v.tensor_tensor(by_type[:, j, :].rearrange("p (t r) -> p t r", t=3),
                                                  rates[:, j * 3 * R:(j + 1) * 3 * R].rearrange("p (t r) -> p t r", t=3),
                                                  types[:, j:j + 1, :].to_broadcast([P, 3, R]), ALU.mult)
                        ins.then_inc(s_by_type, 1)
                        need(dve, s_by_type, s.at(2) + 1)
                        apart(dve, g.gate["dve"])
                        v.tensor_reduce(g.etcol[:, four], by_type[:, :, :], AX_X, ALU.add).then_inc(s_weight, 1)
                    if weigh and s.live(1, NG):
                        need(dve, s_dst, s.at(1) + 1)
                        if windows.own:
                            need(dve, s_rate, s.at(2))
                            rate_window(windows, s, 0)
                        else:
                            apart(dve, g.gate["dve"])
                            with windows.passes(dve) as w:
                                rate_window(windows, s, w)
                                dve.wait_ge(s_rate, windows.number(s.at(1), w) + 1)
                    if s.live(2, NG) and windows.own:
                        need(dve, s_share, s.at(3))
                        v.tensor_tensor(to_node[s.slot(2, 2)][:, :, :], g.iota_c[:, :, :],
                                        g.local16[:, bass.ds(s.at(2) * TG, TG)].unsqueeze(1).to_broadcast([P, P, TG]),
                                        ALU.is_equal).then_inc(s_node, 1)
                    if s.live(4, NG) and windows.own:
                        add_window(nc, dve, g, sums, window[s.slot(2, 4)], s_pass, s_sum, s.at(4), s.at(4))
                    if s.live(3, NG) and not windows.own:
                        k = s.slot(2, 3)
                        with windows.passes(dve) as w:
                            q = dve.snap(windows.number(s.at(3), w))
                            v.tensor_scalar(local[:, :], g.dstcol[:, bass.ds(s.at(3) * TG, TG)], g.base_f[:, bass.ds(w, 1)], None,
                                            ALU.subtract).then_inc(s_local, 1)
                            dve.wait_ge(s_local, q + 1)
                            v.tensor_tensor(to_node[k][:, :, :], g.iota_c[:, :, :],
                                            local[:, :].unsqueeze(1).to_broadcast([P, P, TG]), ALU.is_equal).then_inc(s_node, 1)
                            add_window(nc, dve, g, sums, window[k], s_pass, s_sum, w, q, start=1)

                if not windows.own:
                    v.engine_nop().then_inc(s_sum, 1)
                run_steps(dve, NG, 4, step)

            if weigh:
                chain = Chain(dve, s_counts)
                chain(v.tensor_scalar(g.cnt[:, :, :], g.cnt[:, :, :], 1.0, None, ALU.max))
                chain(v.reciprocal(g.cnt[:, :, :], g.cnt[:, :, :]))
                chain(v.tensor_copy(rest[:, :, :], g.cnt[:, :, :]))
                for k in range(3):
                    part = g.rcnt3[:, :, k * R:(k + 1) * R]
                    chain(v.tensor_copy(part, rest[:, :, :]))
                    if k < 2:
                        chain(v.tensor_tensor(rest[:, :, :], rest[:, :, :], part, ALU.subtract))
            for_windows(dve, g, program)


def store_nodes(nc, g, out):
    N, NBLK = g.N, g.NBLK
    with ExitStack() as ctx:
        s_out = nc.alloc_semaphore("s_out")
        block = ctx.enter_context(nc.Block())

        @block.sync
        def _(sp):
            cut = NBLK // 2
            for a, b in ((0, cut), (cut, NBLK - 1)):
                sp.dma_start(out[a * P:b * P, :].rearrange("(b p) f -> p b f", p=P), g.xs[:, a:b, :]).then_inc(s_out, 16)
            sp.dma_start(out[(NBLK - 1) * P:N, :], g.xs[0:N - (NBLK - 1) * P, NBLK - 1, :]).then_inc(s_out, 16)
            sp.wait_ge(s_out, 48)


def gnn_kernel(nc, x, src, dst, edge_attr, edge_type, W1, b1, W2, b2,
               basis1, comp1, root1, bias1, basis2, comp2, root2, bias2, out):
    with ExitStack() as ctx:
        g = Graph(nc, ctx, x.shape[0], edge_attr.shape[0])
        prepare(nc, g, x, src, dst, edge_type, W1, b1, W2, b2,
                (basis1, basis2), (comp1, comp2), (root1, root2), (bias1, bias2))
        filter_layer(nc, g, edge_attr)
        hacc = ctx.enter_context(nc.sbuf_tensor("hacc", [P, g.NBX, F], F32))
        for which in range(2):
            make_table(nc, g, hacc, which)
            convolve(nc, g, hacc, which)
        store_nodes(nc, g, out)


_INS = ['x', 'src', 'dst', 'edge_attr_128', 'edge_type_8', 'L0_gnn_W1', 'L0_gnn_b1', 'L0_gnn_W2', 'L0_gnn_b2',
        'L1_gnn_basis1', 'L1_gnn_comp1', 'L1_gnn_root1', 'L1_gnn_bias1', 'L1_gnn_basis2', 'L1_gnn_comp2',
        'L1_gnn_root2', 'L1_gnn_bias2']


def kernel(**inputs):
    import numpy as _np
    import concourse.bacc as _bacc
    from concourse import mybir as _mybir
    from concourse.bass_utils import run_bass_kernel_spmd as _run

    nc = _bacc.Bacc("TRN2", target_bir_lowering=False, num_devices=1)
    arrays, args = {}, []
    for name in _INS:
        a = _np.ascontiguousarray(inputs[name])
        arrays[f"in_{name}"] = a
        args.append(nc.dram_tensor(f"in_{name}", a.shape, _mybir.dt.from_np(a.dtype), kind="ExternalInput").ap())
    out = nc.dram_tensor("out_x", inputs['x'].shape, _mybir.dt.float32, kind="ExternalOutput").ap()
    gnn_kernel(nc, *args, out)
    r = _run(nc, [arrays], core_ids=[0])
    return r.results[0]["out_x"]
```
